# Optimizing a Trainium2 kernel written in Bass

```python
import numpy as np
import jax
import jax.numpy as jnp

def _softmax(x, axis=-1):
    return jax.nn.softmax(x, axis=axis)
def _gelu(x):
    return jax.nn.gelu(x, approximate=True)
def _silu(x):
    return jax.nn.silu(x)
def _sigmoid(x):
    return jax.nn.sigmoid(x)
def _layernorm(x, axis=-1, eps=1e-5):
    m = jnp.mean(x, axis=axis, keepdims=True)
    v = jnp.var(x, axis=axis, keepdims=True)
    return (x - m) / jnp.sqrt(v + eps)
def _scatter_add(tgt, idx, src, axis=0):
    return tgt.at[idx].add(src)
def _segment_sum(src, seg, n):
    return jax.ops.segment_sum(src, seg, n)

kernel_name = 'mk_conv_preact_d4_conv_nchw384_2e458d'

def setup_inputs(seed: int = 0):
    np.random.seed(seed)
    _w = jnp.asarray
    def _rec_inputs():
        import jax
        import jax.numpy as jnp
        _gk = jax.random.key(seed)
        x = -0.0005058 + 1 * jax.random.normal(jax.random.fold_in(_gk, 1), (4, 384, 48, 48), jnp.float32)
        return x
    x = _rec_inputs()
    def _L0_conv_setup():
        import jax, jax.numpy as jnp
        import numpy as np
        D_MODEL = 384
        D_STATE = 16
        D_CONV = 4
        D_INNER = 2 * D_MODEL
        DT_RANK = -(-D_MODEL // 16)
        B_SZ, H_SZ, W_SZ = (4, 48, 48)
        LN_EPS = 1e-05

        def _mamba_block(x, in_proj_w, conv_w, conv_b, x_proj_w, dt_proj_w, dt_proj_b, A_log, D, out_proj_w, ln_gamma, ln_beta):
            b, c, h, w = x.shape
            L = h * w
            xs = x.transpose(0, 2, 3, 1).reshape(b, L, c)
            xz = xs @ in_proj_w.T
            xin, z = jnp.split(xz, 2, axis=-1)
            xc = jnp.pad(xin.transpose(0, 2, 1), ((0, 0), (0, 0), (D_CONV - 1, 0)))
            xc = jax.lax.conv_general_dilated(xc, conv_w[:, None, :], (1,), 'VALID', dimension_numbers=('NCH', 'OIH', 'NCH'), feature_group_count=D_INNER)
            xin = jax.nn.silu((xc + conv_b[None, :, None]).transpose(0, 2, 1))
            x_dbl = xin @ x_proj_w.T
            dt, Bm, Cm = jnp.split(x_dbl, [DT_RANK, DT_RANK + D_STATE], axis=-1)
            dt = jax.nn.softplus(dt @ dt_proj_w.T + dt_proj_b)
            A = -jnp.exp(A_log)

            def step(h_prev, inp):
                x_t, dt_t, B_t, C_t = inp
                dA = jnp.exp(dt_t[..., None] * A)
                dBx = dt_t[..., None] * B_t[:, None, :] * x_t[..., None]
                h_new = dA * h_prev + dBx
                y_t = jnp.einsum('bds,bs->bd', h_new, C_t)
                return (h_new, y_t)
            h0 = jnp.zeros((b, D_INNER, D_STATE), xin.dtype)
            seq = (xin.transpose(1, 0, 2), dt.transpose(1, 0, 2), Bm.transpose(1, 0, 2), Cm.transpose(1, 0, 2))
            _, ys = jax.lax.scan(step, h0, seq)
            y = ys.transpose(1, 0, 2) + xin * D
            y = y * jax.nn.silu(z)
            out = y @ out_proj_w.T
            mu = out.mean(-1, keepdims=True)
            var = out.var(-1, keepdims=True)
            out = (out - mu) * jax.lax.rsqrt(var + LN_EPS) * ln_gamma + ln_beta
            return out.reshape(b, h, w, c).transpose(0, 3, 1, 2)
        key = jax.random.key(seed)
        ks = jax.random.split(key, 8)
        sc = lambda k, shape, s: jax.random.normal(k, shape, jnp.float32) * s
        x = jax.random.normal(ks[0], (B_SZ, D_MODEL, H_SZ, W_SZ), jnp.float32)
        in_proj_w = sc(ks[1], (2 * D_INNER, D_MODEL), D_MODEL ** (-0.5))
        conv_w = sc(ks[2], (D_INNER, D_CONV), D_CONV ** (-0.5))
        conv_b = jnp.zeros((D_INNER,), jnp.float32)
        x_proj_w = sc(ks[3], (DT_RANK + 2 * D_STATE, D_INNER), D_INNER ** (-0.5))
        dt_proj_w = sc(ks[4], (D_INNER, DT_RANK), DT_RANK ** (-0.5))
        dt_proj_b = jnp.full((D_INNER,), jnp.log(jnp.expm1(0.01)), jnp.float32)
        A_log = jnp.log(jnp.tile(jnp.arange(1, D_STATE + 1, dtype=jnp.float32), (D_INNER, 1)))
        D = jnp.ones((D_INNER,), jnp.float32)
        out_proj_w = sc(ks[5], (D_MODEL, D_INNER), D_INNER ** (-0.5))
        ln_gamma = jnp.ones((D_MODEL,), jnp.float32)
        ln_beta = jnp.zeros((D_MODEL,), jnp.float32)
        return {'x': x, 'in_proj_w': in_proj_w, 'conv_w': conv_w, 'conv_b': conv_b, 'x_proj_w': x_proj_w, 'dt_proj_w': dt_proj_w, 'dt_proj_b': dt_proj_b, 'A_log': A_log, 'D': D, 'out_proj_w': out_proj_w, 'ln_gamma': ln_gamma, 'ln_beta': ln_beta}
    _L0_conv_all = _L0_conv_setup()
    _L0_conv_in = {k: v for k, v in _L0_conv_all.items() if k in ('in_proj_w', 'conv_w', 'conv_b', 'x_proj_w', 'dt_proj_w', 'dt_proj_b', 'A_log', 'D', 'out_proj_w', 'ln_gamma', 'ln_beta', )}
    del _L0_conv_all

    def _L1_conv_setup():
        import jax, jax.numpy as jnp
        import numpy as np
        B, DIM, H, W = (2, 384, 256, 256)
        HID = DIM * 1
        P = 8
        key = jax.random.key(seed)
        k0, k1, k2, k3, k4 = jax.random.split(key, 5)
        x = jax.random.normal(k0, (B, DIM, H, W), jnp.float32)
        fft_filter = jax.random.normal(k1, (HID, P, P // 2 + 1), jnp.float32)
        w_in = jax.random.normal(k2, (HID, DIM), jnp.float32) * (1.0 / np.sqrt(DIM))
        w_dw = jax.random.normal(k3, (HID, 1, 3, 3), jnp.float32) * (1.0 / 3.0)
        w_out = jax.random.normal(k4, (DIM, HID // 2), jnp.float32) * (1.0 / np.sqrt(HID // 2))
        return {'x': x, 'fft_filter': fft_filter, 'w_in': w_in, 'w_dw': w_dw, 'w_out': w_out}
    _L1_conv_all = _L1_conv_setup()
    _L1_conv_in = {k: v for k, v in _L1_conv_all.items() if k in ('fft_filter', 'w_in', 'w_dw', 'w_out', )}
    del _L1_conv_all

    def _L2_conv_setup():
        import jax, jax.numpy as jnp
        import numpy as np
        from jax import lax
        PLANES = 384
        N_POINTS = 4
        KERNEL_SIZE = 11
        INIT_RADIUS = 2.0 * (2.0 / KERNEL_SIZE)

        def _make_kernels(weight_coord, radius, weights):
            K = KERNEL_SIZE
            lin = jnp.linspace(-1.0, 1.0, K)
            gy, gx = jnp.meshgrid(lin, lin, indexing='ij')
            kernel_coord = jnp.stack([gy, gx], axis=0).reshape(2, K * K)
            diff = weight_coord[:, :, None, :] - kernel_coord.T[None, None, :, :]
            diff = jnp.transpose(diff, (0, 1, 3, 2)).reshape(1, N_POINTS, 2, K, K)
            d = jax.nn.relu(1.0 - jnp.abs(diff).sum(axis=2) / radius)
            kernels = jnp.matmul(weights, d.reshape(1, N_POINTS, K * K)).reshape(PLANES, K, K)
            kernels = jnp.flip(jnp.transpose(kernels, (0, 2, 1)), axis=1)
            return kernels
        key = jax.random.key(seed)
        k1, k2, k3 = jax.random.split(key, 3)
        x = jax.random.normal(k1, (16, PLANES, 64, 64), dtype=jnp.float32)
        weight_coord = jnp.clip(0.2 * jax.random.normal(k2, (1, N_POINTS, 2), dtype=jnp.float32), -1.0, 1.0)
        radius = jnp.full((1, N_POINTS, 1, 1), INIT_RADIUS, dtype=jnp.float32)
        weights = 0.02 * jax.random.normal(k3, (1, PLANES, N_POINTS), dtype=jnp.float32)
        return {'x': x, 'weight_coord': weight_coord, 'radius': radius, 'weights': weights}
    _L2_conv_all = _L2_conv_setup()
    _L2_conv_in = {k: v for k, v in _L2_conv_all.items() if k in ('weight_coord', 'radius', 'weights', )}
    del _L2_conv_all

    def _L3_conv_setup():
        import jax, jax.numpy as jnp
        import numpy as np
        B, C, H, W = (32, 384, 28, 28)
        E, HID, K = (4, 384, 2)
        key = jax.random.key(seed)
        ks = jax.random.split(key, 5)
        x = jax.random.normal(ks[0], (B, C, H, W), jnp.float32)
        gate_w = jax.random.normal(ks[1], (C, E), jnp.float32) * 0.02
        gate_b = jnp.zeros((E,), jnp.float32)
        w1 = jax.random.normal(ks[2], (E, HID, C), jnp.float32) * 0.02
        b1 = jnp.zeros((E, HID), jnp.float32)
        w2 = jax.random.normal(ks[3], (E, C, HID), jnp.float32) * 0.02
        b2 = jnp.zeros((E, C), jnp.float32)
        return {'x': x, 'gate_w': gate_w, 'gate_b': gate_b, 'w1': w1, 'b1': b1, 'w2': w2, 'b2': b2}
    _L3_conv_all = _L3_conv_setup()
    _L3_conv_in = {k: v for k, v in _L3_conv_all.items() if k in ('gate_w', 'gate_b', 'w1', 'b1', 'w2', 'b2', )}
    del _L3_conv_all

    return {
        "x": x,
        "L0_conv_in_proj_w": _L0_conv_in["in_proj_w"],
        "L0_conv_conv_w": _L0_conv_in["conv_w"],
        "L0_conv_conv_b": _L0_conv_in["conv_b"],
        "L0_conv_x_proj_w": _L0_conv_in["x_proj_w"],
        "L0_conv_dt_proj_w": _L0_conv_in["dt_proj_w"],
        "L0_conv_dt_proj_b": _L0_conv_in["dt_proj_b"],
        "L0_conv_A_log": _L0_conv_in["A_log"],
        "L0_conv_D": _L0_conv_in["D"],
        "L0_conv_out_proj_w": _L0_conv_in["out_proj_w"],
        "L0_conv_ln_gamma": _L0_conv_in["ln_gamma"],
        "L0_conv_ln_beta": _L0_conv_in["ln_beta"],
        "L1_conv_fft_filter": _L1_conv_in["fft_filter"],
        "L1_conv_w_in": _L1_conv_in["w_in"],
        "L1_conv_w_dw": _L1_conv_in["w_dw"],
        "L1_conv_w_out": _L1_conv_in["w_out"],
        "L2_conv_weight_coord": _L2_conv_in["weight_coord"],
        "L2_conv_radius": _L2_conv_in["radius"],
        "L2_conv_weights": _L2_conv_in["weights"],
        "L3_conv_gate_w": _L3_conv_in["gate_w"],
        "L3_conv_gate_b": _L3_conv_in["gate_b"],
        "L3_conv_w1": _L3_conv_in["w1"],
        "L3_conv_b1": _L3_conv_in["b1"],
        "L3_conv_w2": _L3_conv_in["w2"],
        "L3_conv_b2": _L3_conv_in["b2"],
    }

def reference(x, L0_conv_in_proj_w, L0_conv_conv_w, L0_conv_conv_b, L0_conv_x_proj_w, L0_conv_dt_proj_w, L0_conv_dt_proj_b, L0_conv_A_log, L0_conv_D, L0_conv_out_proj_w, L0_conv_ln_gamma, L0_conv_ln_beta, L1_conv_fft_filter, L1_conv_w_in, L1_conv_w_dw, L1_conv_w_out, L2_conv_weight_coord, L2_conv_radius, L2_conv_weights, L3_conv_gate_w, L3_conv_gate_b, L3_conv_w1, L3_conv_b1, L3_conv_w2, L3_conv_b2):
    import jax
    import jax.numpy as jnp
    def _L0_conv_ref(x, in_proj_w, conv_w, conv_b, x_proj_w, dt_proj_w, dt_proj_b, A_log, D, out_proj_w, ln_gamma, ln_beta):
        import jax, jax.numpy as jnp
        import numpy as np
        D_MODEL = 384
        D_STATE = 16
        D_CONV = 4
        D_INNER = 2 * D_MODEL
        DT_RANK = -(-D_MODEL // 16)
        B_SZ, H_SZ, W_SZ = (4, 48, 48)
        LN_EPS = 1e-05

        def _mamba_block(x, in_proj_w, conv_w, conv_b, x_proj_w, dt_proj_w, dt_proj_b, A_log, D, out_proj_w, ln_gamma, ln_beta):
            b, c, h, w = x.shape
            L = h * w
            xs = x.transpose(0, 2, 3, 1).reshape(b, L, c)
            xz = xs @ in_proj_w.T
            xin, z = jnp.split(xz, 2, axis=-1)
            xc = jnp.pad(xin.transpose(0, 2, 1), ((0, 0), (0, 0), (D_CONV - 1, 0)))
            xc = jax.lax.conv_general_dilated(xc, conv_w[:, None, :], (1,), 'VALID', dimension_numbers=('NCH', 'OIH', 'NCH'), feature_group_count=D_INNER)
            xin = jax.nn.silu((xc + conv_b[None, :, None]).transpose(0, 2, 1))
            x_dbl = xin @ x_proj_w.T
            dt, Bm, Cm = jnp.split(x_dbl, [DT_RANK, DT_RANK + D_STATE], axis=-1)
            dt = jax.nn.softplus(dt @ dt_proj_w.T + dt_proj_b)
            A = -jnp.exp(A_log)

            def step(h_prev, inp):
                x_t, dt_t, B_t, C_t = inp
                dA = jnp.exp(dt_t[..., None] * A)
                dBx = dt_t[..., None] * B_t[:, None, :] * x_t[..., None]
                h_new = dA * h_prev + dBx
                y_t = jnp.einsum('bds,bs->bd', h_new, C_t)
                return (h_new, y_t)
            h0 = jnp.zeros((b, D_INNER, D_STATE), xin.dtype)
            seq = (xin.transpose(1, 0, 2), dt.transpose(1, 0, 2), Bm.transpose(1, 0, 2), Cm.transpose(1, 0, 2))
            _, ys = jax.lax.scan(step, h0, seq)
            y = ys.transpose(1, 0, 2) + xin * D
            y = y * jax.nn.silu(z)
            out = y @ out_proj_w.T
            mu = out.mean(-1, keepdims=True)
            var = out.var(-1, keepdims=True)
            out = (out - mu) * jax.lax.rsqrt(var + LN_EPS) * ln_gamma + ln_beta
            return out.reshape(b, h, w, c).transpose(0, 3, 1, 2)
        return _mamba_block(x, in_proj_w, conv_w, conv_b, x_proj_w, dt_proj_w, dt_proj_b, A_log, D, out_proj_w, ln_gamma, ln_beta)

    def _L1_conv_ref(x, fft_filter, w_in, w_dw, w_out):
        import jax, jax.numpy as jnp
        import numpy as np
        B, DIM, H, W = (2, 384, 256, 256)
        HID = DIM * 1
        P = 8
        b, c, h, w = x.shape
        hid = w_in.shape[0]
        hb, wb = (h // P, w // P)
        t = jnp.einsum('bchw,oc->bohw', x, w_in)
        tp = t.reshape(b, hid, hb, P, wb, P)
        tf = jnp.fft.rfft2(tp, axes=(3, 5))
        tf = tf * fft_filter[None, :, None, :, None, :]
        tp = jnp.fft.irfft2(tf, s=(P, P), axes=(3, 5))
        t = tp.reshape(b, hid, h, w)
        t = jax.lax.conv_general_dilated(t, w_dw, window_strides=(1, 1), padding='SAME', feature_group_count=hid, dimension_numbers=('NCHW', 'OIHW', 'NCHW'))
        x1, x2 = (t[:, :hid // 2], t[:, hid // 2:])
        g = jax.nn.gelu(x1, approximate=False) * x2
        return jnp.einsum('bchw,oc->bohw', g, w_out)

    def _L2_conv_ref(x, weight_coord, radius, weights):
        import jax, jax.numpy as jnp
        import numpy as np
        from jax import lax
        PLANES = 384
        N_POINTS = 4
        KERNEL_SIZE = 11
        INIT_RADIUS = 2.0 * (2.0 / KERNEL_SIZE)

        def _make_kernels(weight_coord, radius, weights):
            K = KERNEL_SIZE
            lin = jnp.linspace(-1.0, 1.0, K)
            gy, gx = jnp.meshgrid(lin, lin, indexing='ij')
            kernel_coord = jnp.stack([gy, gx], axis=0).reshape(2, K * K)
            diff = weight_coord[:, :, None, :] - kernel_coord.T[None, None, :, :]
            diff = jnp.transpose(diff, (0, 1, 3, 2)).reshape(1, N_POINTS, 2, K, K)
            d = jax.nn.relu(1.0 - jnp.abs(diff).sum(axis=2) / radius)
            kernels = jnp.matmul(weights, d.reshape(1, N_POINTS, K * K)).reshape(PLANES, K, K)
            kernels = jnp.flip(jnp.transpose(kernels, (0, 2, 1)), axis=1)
            return kernels
        kernels = _make_kernels(weight_coord, radius, weights)
        pad = KERNEL_SIZE // 2
        out = lax.conv_general_dilated(x, kernels[:, None, :, :], window_strides=(1, 1), padding=[(pad, pad), (pad, pad)], dimension_numbers=('NCHW', 'OIHW', 'NCHW'), feature_group_count=PLANES)
        return out

    def _L3_conv_ref(x, gate_w, gate_b, w1, b1, w2, b2):
        import jax, jax.numpy as jnp
        import numpy as np
        B, C, H, W = (32, 384, 28, 28)
        E, HID, K = (4, 384, 2)
        b, c, h, w = x.shape
        e = gate_b.shape[0]
        x_flat = x.transpose(0, 2, 3, 1).reshape(-1, c)
        scores = jax.nn.softmax(x_flat @ gate_w + gate_b, -1)
        top_v, top_i = jax.lax.top_k(scores, K)
        top_w = jax.nn.softmax(top_v, -1)
        wmap = top_w.T.reshape(K, b, h, w)
        present = (top_i[:, :, None] == jnp.arange(e)[None, None, :]).any(0)
        coef = jnp.einsum('ke,kbhw->ebhw', present.astype(x.dtype), wmap)
        hdn = jax.nn.relu(jnp.einsum('bchw,edc->ebdhw', x, w1) + b1[:, None, :, None, None])
        y = jnp.einsum('ebdhw,eod->ebohw', hdn, w2) + b2[:, None, :, None, None]
        out = jnp.einsum('ebohw,ebhw->bohw', y, coef)
        return out

    def _gn(v, G=32, eps=1e-5):
        B_, C_, H_, W_ = v.shape
        g = v.reshape(B_, G, C_ // G, H_, W_)
        m = jnp.mean(g, axis=(2, 3, 4), keepdims=True)
        s = jnp.var(g, axis=(2, 3, 4), keepdims=True)
        return ((g - m) / jnp.sqrt(s + eps)).reshape(v.shape)

    def _ln_c(v, eps=1e-6):
        m = jnp.mean(v, axis=1, keepdims=True)
        s = jnp.var(v, axis=1, keepdims=True)
        return (v - m) / jnp.sqrt(s + eps)

    def _ln_t(v, eps=1e-5):
        m = jnp.mean(v, axis=-1, keepdims=True)
        s = jnp.var(v, axis=-1, keepdims=True)
        return (v - m) / jnp.sqrt(s + eps)

    def _to_tokens(v):
        B_, C_, H_, W_ = v.shape
        return v.reshape(B_, C_, H_ * W_).transpose(0, 2, 1)
    def _from_tokens(t, like):
        B_, C_, H_, W_ = like.shape
        return t.transpose(0, 2, 1).reshape(B_, C_, H_, W_)

    x = x + _L0_conv_ref(_gn(x), L0_conv_in_proj_w, L0_conv_conv_w, L0_conv_conv_b, L0_conv_x_proj_w, L0_conv_dt_proj_w, L0_conv_dt_proj_b, L0_conv_A_log, L0_conv_D, L0_conv_out_proj_w, L0_conv_ln_gamma, L0_conv_ln_beta)
    x = x + _L1_conv_ref(_gn(x), L1_conv_fft_filter, L1_conv_w_in, L1_conv_w_dw, L1_conv_w_out)
    x = x + _L2_conv_ref(_gn(x), L2_conv_weight_coord, L2_conv_radius, L2_conv_weights)
    x = x + _L3_conv_ref(_gn(x), L3_conv_gate_w, L3_conv_gate_b, L3_conv_w1, L3_conv_b1, L3_conv_w2, L3_conv_b2)
    return x


_drawn_inputs = setup_inputs


def setup_inputs(seed=0):
    import zlib

    import numpy as np

    out = dict(_drawn_inputs(seed))
    spreads = {'L0_conv_conv_b': (0.0, 0.1),
     'L0_conv_dt_proj_b': (-4.600166320800781, 0.553),
     'L0_conv_D': (1.0, 0.2),
     'L0_conv_ln_gamma': (1.0, 0.2),
     'L0_conv_ln_beta': (0.0, 0.1),
     'L2_conv_radius': (0.3636363744735718, 0.6),
     'L3_conv_gate_b': (0.0, 0.8),
     'L3_conv_b1': (0.0, 0.1),
     'L3_conv_b2': (0.0, 0.1)}
    factors = {'L0_conv_A_log': 2.787, 'L3_conv_gate_w': 8.0}
    for name, (base, spread) in spreads.items():
        noise = np.random.default_rng([zlib.crc32(name.encode()), seed]).standard_normal(out[name].shape)
        drawn = base * np.exp(spread * noise) if base else spread * noise
        out[name] = jnp.asarray(drawn.astype(out[name].dtype))
    for name, factor in factors.items():
        out[name] = (out[name] * factor).astype(out[name].dtype)
    return out
```

```python
from contextlib import ExitStack

import numpy as np

import concourse.bass as bass
from concourse import mybir

F32 = mybir.dt.float32
F32R = mybir.dt.float32r
ALU = mybir.AluOpType
ACT = mybir.ActivationFunctionType

NB, C, H, W = 4, 384, 48, 48
L = H * W
CT = 3
DI = 768
DT_ = 6
NS = 16
RK = 24
T = 384
TB = 3
NQ = L // T
NCH = NB * NQ
NT = L // 128
GN_EPS = 1e-5
LN_EPS = 1e-5
K11 = 11
CONV_DVE = ((0, 1), (2, 3), (4, 5))
CONV_POOL = ()
GAP_SILU = 5
GAP_LN = 6
ENGINES = ("pe", "act", "dve", "pool", "sp")


class Done:

    __slots__ = ("eng", "make", "waits", "sem", "value", "used")

    def __init__(self, eng, make, waits, sem, value):
        self.eng, self.make, self.waits = eng, make, waits
        self.sem, self.value, self.used = sem, value, sem is not None


def flat(waits):
    for w in waits:
        if w is None:
            continue
        if isinstance(w, Done):
            yield w
        else:
            yield from flat(w)


class Queues:

    def __init__(self, nc, ctx):
        self.nc, self.ctx = nc, ctx
        self.q = {e: [] for e in ENGINES}
        self.sems = {e: ctx.enter_context(nc.semaphore(f"s_{e}")) for e in ENGINES}
        self.dma_sems, self.dma_count = {}, {}

    def op(self, eng, make, *waits):
        d = Done(eng, make, list(flat(waits)), None, 0)
        for w in d.waits:
            w.used = True
        self.q[eng].append(d)
        return d

    def dma(self, name, out, in_, *waits, eng="sp"):
        if name not in self.dma_sems:
            self.dma_sems[name] = self.ctx.enter_context(self.nc.semaphore(f"d_{name}"))
            self.dma_count[name] = 0
        self.dma_count[name] += 16
        d = Done(eng, lambda e: e.dma_start(out, in_), list(flat(waits)),
                 self.dma_sems[name], self.dma_count[name])
        for w in d.waits:
            w.used = True
        self.q[eng].append(d)
        return d

    def last(self):
        return [self.q[e][-1] for e in ENGINES if self.q[e] and self.q[e][-1].sem is None]

    def emit(self, block):
        for e in ENGINES:
            n = 0
            for d in self.q[e]:
                if d.sem is None and d.used:
                    n += 1
                    d.value = n

        def run(name, eng):
            seen = {}
            for d in self.q[name]:
                need = {}
                for w in d.waits:
                    key = (w.eng, None) if w.sem is None else ("dma", id(w.sem))
                    s = self.sems[w.eng] if w.sem is None else w.sem
                    if w.value > need.get(key, (None, 0))[1]:
                        need[key] = (s, w.value)
                for key, (s, v) in need.items():
                    if seen.get(key, 0) < v:
                        seen[key] = v
                        eng.wait_ge(s, v)
                ins = d.make(eng)
                if d.sem is not None:
                    ins.then_inc(d.sem, 16)
                elif d.used:
                    ins.then_inc(self.sems[name], 1)

        block.tensor(lambda e: run("pe", e))
        block.scalar(lambda e: run("act", e))
        block.vector(lambda e: run("dve", e))
        block.gpsimd(lambda e: run("pool", e))
        block.sync(lambda e: run("sp", e))


class Ring:

    def __init__(self, bufs):
        self.bufs, self.free, self.held, self.n = bufs, [None] * len(bufs), [False] * len(bufs), -1

    def get(self):
        for _ in self.bufs:
            self.n += 1
            i = self.n % len(self.bufs)
            if not self.held[i]:
                self.held[i] = True
                return i, self.bufs[i], self.free[i]
        raise RuntimeError("no buffer of the ring is free")

    def put(self, i, done):
        assert self.held[i]
        self.held[i] = False
        self.free[i] = done


class Arena:

    def __init__(self, nc, base, tag):
        self.nc, self.at, self.tag = nc, (base + 63) // 64 * 64, tag

    def __call__(self, name, shape, dt=F32):
        n = 4
        for s in shape[1:]:
            n *= s
        off = self.at
        self.at = (off + n + 63) // 64 * 64
        return self.nc.alloc_sbuf_tensor_at(f"{self.tag}_{name}", shape, dt, offset=off)


def build(nc, d, layers=(0, 1, 3), images=NB):
    ctx = ExitStack()
    with ctx:
        p = Queues(nc, ctx)
        bank = [ctx.enter_context(nc.psum_tensor(f"ps{i}", [128, 512], F32)) for i in range(4)]
        wide = [ctx.enter_context(nc.psum_tensor(f"pw{i}", [128, 1024], F32)) for i in range(2)]
        base0 = nc.sbuf_base
        keep = Arena(nc, base0, "g")
        ident = keep("ident", [128, 128])
        gm = keep("gm", [128, 9, 128])
        ones = keep("ones", [128, 128])
        mhalf = keep("mhalf", [128, 4])
        base = keep.at
        late = Arena(nc, base, "g2")
        coef = late("coef", [128, NB * NT, 4])
        gst = late("gst", [128, NB, 2, 3])

        t_const = [p.dma("ident", ident[:], d["ident"]), p.dma("gm", gm[:], d["gm"])]
        t_ones = p.op("pool", lambda e: e.memset(ones[:], 1.0))
        t_mh = p.op("pool", lambda e: e.memset(mhalf[:], -0.5))
        t_const += [t_ones, t_mh]

        def mm(out, lhsT, rhs, start, stop, *waits, skip=False):
            return p.op("pe", lambda e: e.matmul(out, lhsT, rhs, start=start, stop=stop, skip_group_check=skip), *waits)

        def tr(out, in_, *waits):
            n = in_.shape[0]
            return p.op("pe", lambda e: e.transpose(out, in_, ident[0:n, 0:n]), *waits)

        def act(out, in_, func, *waits, **kw):
            return p.op("act", lambda e: e.activation(out, in_, func, **kw), *waits)

        def ts(out, in_, s1, s2, op0, op1, *waits, eng="dve"):
            if op1 is None:
                return p.op(eng, lambda e: e.tensor_scalar(out, in_, s1, None, op0), *waits)
            return p.op(eng, lambda e: e.tensor_scalar(out, in_, s1, s2, op0, op1), *waits)

        def tt(out, a, b, op, *waits, eng="dve"):
            return p.op(eng, lambda e: e.tensor_tensor(out, a, b, op), *waits)

        def stt(out, a, s, b, op0, op1, *waits):
            return p.op("dve", lambda e: e.scalar_tensor_tensor(out=out, in0=a, scalar=s, in1=b, op0=op0, op1=op1), *waits)

        def copy(eng, out, in_, *waits):
            if eng == "act":
                return act(out, in_, ACT.Copy, *waits)
            return p.op(eng, lambda e: e.tensor_copy(out, in_), *waits)

        def finish_stats(bn, mv, gs, ps, ps_free, bn_done, out, out_free):
            a = None
            for c in range(CT):
                a = p.op("dve", lambda e, c=c: e.bn_aggr(mv[:, c, :], bn[:, c, :, :].rearrange("p k s -> p (k s)")), bn_done, out_free)
            b = tt(gs[:, 0, :], mv[:, :, 0], mv[:, :, 0], ALU.mult, a)
            b = tt(mv[:, :, 1], mv[:, :, 1], gs[:, 0, :], ALU.add, b)
            last = None
            for co in range(CT):
                cis = [ci for ci in range(CT) if abs(ci - co) <= 1]
                for ci in cis:
                    last = mm(ps[:, 2 * co:2 * co + 2], gm[:, 3 * ci + co, :], mv[:, ci, :],
                              ci == cis[0], ci == cis[-1], b, ps_free, t_const)
            g = ts(gs[:, 1:3, :], ps[:, 0:6].rearrange("p (c k) -> p k c", k=2), 1.0 / 12.0, None, ALU.mult, None, last)
            x = tt(gs[:, 0, :], gs[:, 1, :], gs[:, 1, :], ALU.mult, g)
            x = tt(gs[:, 2, :], gs[:, 2, :], gs[:, 0, :], ALU.subtract, x)
            x = ts(gs[:, 2, :], gs[:, 2, :], GN_EPS, None, ALU.add, None, x)
            r = tt(out[:, 0, :], gs[:, 2, :], mhalf[:, 0:3], ALU.pow, x, eng="pool")
            f = stt(out[:, 1, :], gs[:, 1, :], -1.0, out[:, 0, :], ALU.mult, ALU.mult, r)
            return g, f

        stored = {}

        def layer0(xin_d, xout_d):
            ar = Arena(nc, base, "a")
            WinT = ar("WinT", [128, 3, 1536])
            WxT = ar("WxT", [128, 6, 64])
            WdtT = ar("WdtT", [RK, DI])
            WoT = ar("WoT", [128, 6, C])
            pv = ar("pv", [128, 6, 23])
            pc = ar("pc", [128, 3, 2])
            Aneg = ar("Aneg", [128, 6, NS])
            one1 = ar("one1", [128, 1])
            xs = [ar(f"xs{i}", [128, 3, T]) for i in range(3)]
            xn = ar("xn", [128, 3, T])
            sx = ar("sx", [128, 3, T])
            bn = ar("bn", [128, 3, NQ, 6])
            mv = ar("mv", [128, 3, 2])
            gs = ar("gs", [128, 3, 3])
            sc = [ar(f"sc{i}", [128, 2, 3]) for i in range(2)]
            raw = ar("raw", [128, 6, T + 3])
            V = raw[:, :, 3:T + 3]
            xin = [ar(f"xin{i}", [128, 6, T]) for i in range(2)]
            sz = [ar(f"sz{i}", [128, 6, T]) for i in range(2)]
            dt = [ar(f"dt{i}", [128, 6, T]) for i in range(2)]
            dtxT = [ar(f"dtxT{i}", [128, TB, DI]) for i in range(2)]
            BC = [ar(f"BC{i}", [128, TB, 32]) for i in range(2)]
            dtl = ar("dtl", [64, T])
            dBT = [ar(f"dBT{i}", [128, TB, DI]) for i in range(2)]
            dA = Ring([ar(f"dA{i}", [128, T]) for i in range(8)])
            hb = [ar(f"h{i}", [128, 6, T]) for i in range(2)]
            st = ar("st", [128, 6, NS])
            acc = ar("acc", [128, TB, DI])
            ob = ar("ob", [128, TB, C])
            lbn = ar("lbn", [128, TB, 6])
            lmv = ar("lmv", [128, TB, 2])
            lsc = ar("lsc", [128, TB, 2])
            pp = Ring(bank)
            pb = pp
            ph = Ring(wide)

            w_in = p.dma("WinT", WinT[:], d["WinT"].rearrange("(k p) n -> p k n", p=128))
            w_pv = p.dma("pv", pv[:], d["pv"])
            w_pc = p.dma("pc", pc[:], d["pc"])
            w_x = p.dma("WxT", WxT[:], d["WxT"].rearrange("(k p) n -> p k n", p=128))
            w_dt = p.dma("WdtT", WdtT[:], d["WdtT"])
            w_o = p.dma("WoT", WoT[:], d["WoT"].rearrange("(k p) n -> p k n", p=128))
            one_t = p.op("pool", lambda e: e.memset(one1[:], 1.0))
            p.op("act", lambda e: e.preload_act_table_set("natural_log_exp_and_others"))
            a0 = act(Aneg[:], pv[:, :, 7:23], ACT.Exp, w_pv)
            t_A = ts(Aneg[:], Aneg[:], -1.0, None, ALU.mult, None, a0)
            cw = lambda m, j: pv[:, m, j:j + 1]
            cb = lambda m: pv[:, m, 4:5]
            db = lambda m: pv[:, m, 5:6]
            Dm = lambda m: pv[:, m, 6:7]
            xv = xin_d.rearrange("b (c p) l -> b p c l", p=128)
            xo = xout_d.rearrange("b (c p) l -> b p c l", p=128)

            free = {n: [None, None, None] for n in ("xs", "xin", "sz", "dt", "dtxT", "BC", "dBT", "h", "sc", "tap")}
            free.update({n: None for n in ("sx", "bn", "xn", "raw", "V", "dtl", "ob", "acc")})
            scale_done, beta_done, ready, acc_done = {}, {}, {}, {}
            halo_done = [None]
            st_done = [None] * NS

            def stats(b):
                t = None
                for q in range(NQ):
                    ld = p.dma("sx", sx[:], xv[b, :, :, q * T:(q + 1) * T], free["sx"])
                    yield
                    for c in range(CT):
                        t = p.op("dve", lambda e, c=c, q=q: e.bn_stats(bn[:, c, q, :], sx[:, c, :]), ld, free["bn"])
                        yield
                    free["sx"] = t
                i, ps, fr = pp.get()
                g, f = finish_stats(bn, mv, gs, ps, fr, t, sc[b % 2], free["sc"][b % 2])
                pp.put(i, g)
                free["bn"] = f
                scale_done[b] = f
                yield

            posted = {}

            def project(col, xn_t, evac):
                held = x = None
                for m in range(6):
                    if held:
                        pp.put(held[0], evac(*held[1:]))
                    i, ps, fr = pp.get()
                    for kk in range(CT):
                        x = mm(ps[:, 0:T], WinT[:, kk, col + m * 128:col + (m + 1) * 128], xn[:, kk, :], kk == 0, kk == 2, xn_t, fr, w_in)
                        yield
                    held = (i, m, ps, x)
                yield
                pp.put(held[0], evac(*held[1:]))
                free["xn"] = x

            def pre(k):
                b, q = divmod(k, NQ)
                o = k % 2
                t0 = q * T
                xb = xs[k % 3]
                ld = p.dma(f"xs{k % 3}", xb[:], xv[b, :, :, t0:t0 + T], free["xs"][k % 3])
                yield
                for c in range(CT):
                    n = ts(xn[:, c, :], xb[:, c, :], sc[b % 2][:, 0, c:c + 1], sc[b % 2][:, 1, c:c + 1],
                           ALU.mult, ALU.add, ld, scale_done[b], free["xn"], eng="pool")
                if q == NQ - 1:
                    free["sc"][b % 2] = n
                yield
                for c in range(CT):
                    beta_done[k] = act(xb[:, c, :], xb[:, c, :], ACT.Identity, n, w_pc, bias=pc[:, c, 1:2])
                zs = [None] * 6

                def to_sz(m, ps, x):
                    assert k < 2 or posted.get((k - 2, "sz"))
                    zs[m] = copy("act", sz[o][:, m, :], ps[:, 0:T], x, free["sz"][o])
                    return zs[m]

                while k >= 2 and not posted.get((k - 2, "sz")):
                    yield
                yield from project(DI, n, to_sz)
                zt = act(sz[o][:], sz[o][:], ACT.Silu, zs)
                p.op("act", lambda e: e.preload_act_table_set("natural_log_exp_and_others"))
                if q == 0:
                    hl = p.op("pool", lambda e: e.memset(raw[:, :, 0:3], 0.0), free["raw"])
                else:
                    hl = halo_done[0]
                rw = [None] * 6

                def to_raw(m, ps, x):
                    rw[m] = copy("act", raw[:, m, 3:T + 3], ps[:, 0:T], x, free["raw"], free["V"], hl)
                    return rw[m]

                prev = [None] * 6

                def conv(m):
                    prev[m] = ts(xin[o][:, m, :], raw[:, m, 0:T], cw(m, 0), cb(m), ALU.mult, ALU.add,
                                 rw[m], hl, free["xin"][o], w_pv)
                    for j in range(1, 4):
                        yield
                        prev[m] = stt(xin[o][:, m, :], raw[:, m, j:j + T], cw(m, j), xin[o][:, m, :], ALU.mult, ALU.add, prev[m])

                while k >= 2 and not posted.get((k - 2, "xin")):
                    yield
                going, cm = [], 0
                pj = project(0, n, to_raw)
                alive = True
                while alive or cm < 6 or going:
                    if alive and next(pj, 1) == 1:
                        alive = False
                    while cm < 6 and rw[cm] is not None and len(going) < 2:
                        going.append(conv(cm))
                        cm += 1
                    going = [g for g in going if next(g, 1) != 1]
                    yield
                if q < NQ - 1:
                    halo_done[0] = p.op("pool", lambda e: e.tensor_copy(raw[:, :, 0:3], raw[:, :, T:T + 3]), prev)
                    halo = halo_done[0]
                else:
                    halo = prev
                xt = act(xin[o][:], xin[o][:], ACT.Silu, prev)
                p.op("act", lambda e: e.preload_act_table_set("natural_log_exp_and_others"))
                for _ in range(GAP_SILU):
                    yield
                i, ps, fr = pp.get()
                for m in range(6):
                    x = mm(ps[0:64, 0:T], WxT[:, m, :], xin[o][:, m, :], m == 0, m == 5, xt, fr, w_x)
                    yield
                tl = copy("act", dtl[:], ps[0:64, 0:T], x, free["dtl"])
                pp.put(i, tl)
                yield
                yield
                i, ps, fr = pp.get()
                for tb in range(TB):
                    x = p.op("pe", lambda e, tb=tb, ps=ps: e.transpose(
                        ps[:, tb * 32:tb * 32 + 32], dtl[32:64, tb * 128:(tb + 1) * 128], ident[32:64, 32:64]), tl, fr, t_const)
                tBC = copy("act", BC[o][:], ps[:, 0:96].rearrange("p (a n) -> p a n", n=32), x, free["BC"][o])
                pp.put(i, tBC)
                vs = []
                for m in range(6):
                    i, ps, fr = pp.get()
                    x = mm(ps[:, 0:T], WdtT[:, m * 128:(m + 1) * 128], dtl[0:RK, :], True, True, tl, fr, w_dt)
                    yield
                    vs.append(act(V[:, m, :], ps[:, 0:T], ACT.Identity, x, halo, prev, bias=db(m)))
                    pp.put(i, vs[m])
                free["dtl"] = [x, tBC]
                yield
                c0 = ts(dt[o][:], V, 40.0, -3.0e38, ALU.min, ALU.max, vs, free["dt"][o], eng="pool")
                yield
                yield
                yield
                c1 = act(dt[o][:], dt[o][:], ACT.Exp, c0)
                c2 = act(dt[o][:], dt[o][:], ACT.Ln, c1, one_t, bias=one1[:, 0:1])
                for _ in range(GAP_LN):
                    yield
                tdt, tx, ct = [], [], []
                for m in range(6):
                    tdt.append(tt(dt[o][:, m, :], dt[o][:, m, :], V[:, m, :], ALU.max, c2))
                    tx.append(tt(V[:, m, :], dt[o][:, m, :], xin[o][:, m, :], ALU.mult, tdt[m], xt, eng="pool"))
                    yield
                yield
                for hf in range(2):
                    for tb in range(TB):
                        i, ps, fr = pp.get()
                        for cc in range(3):
                            x = tr(ps[:, cc * 128:(cc + 1) * 128], V[:, hf * 3 + cc, tb * 128:(tb + 1) * 128], tx[hf * 3 + cc], fr, t_const)
                        yield
                        ct.append(copy("act", dtxT[o][:, tb, hf * T:(hf + 1) * T], ps[:, 0:T], x, free["dtxT"][o]))
                        pp.put(i, ct[-1])
                free["V"] = x
                free["raw"] = prev
                ready[k] = dict(xt=xt, zt=zt, BC=tBC, dt=tdt, dtx=ct)

            nk = images * NQ
            exps = {}
            scaled = {}
            LEAD = 7

            def exp_to(n):
                while len(exps) <= min(n, nk * NS * 6 - 1):
                    g = len(exps)
                    k, r = divmod(g, NS * 6)
                    s, c = divmod(r, 6)
                    if k not in ready:
                        return
                    j, da, df = dA.get()
                    e = act(da[:], dt[k % 2][:, c, :], ACT.Exp, ready[k]["dt"][c], df, t_A, scale=Aneg[:, c, s:s + 1])
                    exps[g] = (j, da, e)
                    if r == NS * 6 - 1:
                        free["dt"][k % 2] = e

            def scale_to(n):
                while len(scaled) <= min(n, nk * NS - 1):
                    g = len(scaled)
                    k, s = divmod(g, NS)
                    if k not in ready:
                        return
                    o = k % 2
                    for tb in range(TB):
                        bt = ts(dBT[g % 2][:, tb, :], dtxT[o][:, tb, :], BC[o][:, tb, s:s + 1], 1.0, ALU.mult, ALU.mult,
                                ready[k]["dtx"], ready[k]["BC"], free["dBT"][g % 2], eng="pool")
                    scaled[g] = bt
                    if s == NS - 1:
                        free["dtxT"][o] = bt

            acc_t = [None] * TB

            def contract(k, s, tb, hd):
                o = k % 2
                i, ps, fr = ph.get()
                for c in range(6):
                    x = tr(ps[:, c * 128:(c + 1) * 128], hb[s % 2][:, c, tb * 128:(tb + 1) * 128], hd[c], fr, t_const)
                cs = BC[o][:, tb, 16 + s:17 + s]
                if s == 0:
                    y = ts(acc[:, tb, :], ps[:, 0:DI], cs, None, ALU.mult, None, x, ready[k]["BC"], free["acc"])
                else:
                    y = stt(acc[:, tb, :], ps[:, 0:DI], cs, acc[:, tb, :], ALU.mult, ALU.add, x, acc_t[tb])
                acc_t[tb] = y
                ph.put(i, y)
                if tb == TB - 1:
                    free["h"][s % 2] = [x, st_done[s]]
                return y

            def scan(k):
                b, q = divmod(k, NQ)
                hd = {}
                y = None
                for s in range(NS + 1):
                    if s < NS:
                        scale_to(k * NS + s + 1)
                        hd[s] = []
                    for c in range(6):
                        if s < NS:
                            g = (k * NS + s) * 6 + c
                            exp_to(g + LEAD)
                            j, da, e = exps[g]
                            i, ps, fr = pb.get()
                            src = dBT[(k * NS + s) % 2]
                            for tb in range(TB):
                                x = tr(ps[:, tb * 128:(tb + 1) * 128], src[:, tb, c * 128:(c + 1) * 128], scaled[k * NS + s], fr, t_const)
                            init = 0.0 if q == 0 else st[:, c, s:s + 1]
                            h = p.op("dve", lambda e, c=c, s=s, da=da, ps=ps, init=init: e.tensor_tensor_scan(
                                hb[s % 2][:, c, :], da[:], ps[:, 0:T], init, ALU.mult, ALU.add),
                                x, e, free["h"][s % 2], None if q == 0 else st_done[s])
                            pb.put(i, h)
                            dA.put(j, h)
                            hd[s].append(h)
                            if c == 5:
                                free["dBT"][(k * NS + s) % 2] = x
                                st_done[s] = p.op("pool", lambda e, s=s: e.tensor_copy(st[:, :, s], hb[s % 2][:, :, T - 1]), hd[s])
                        if s > 0 and c % 2 == 1:
                            y = contract(k, s - 1, c // 2, hd[s - 1])
                        if s < NS or c % 2 == 1:
                            yield
                free["BC"][k % 2] = [y, scaled[k * NS + NS - 1]]
                acc_done[k] = y

            def post(k):
                b, q = divmod(k, NQ)
                o = k % 2
                t0 = q * T
                xb = xs[k % 3]
                R = ready[k]
                yt = []
                for c in range(6):
                    i, ps, fr = pp.get()
                    for tb in range(TB):
                        x = tr(ps[:, tb * 128:(tb + 1) * 128], acc[:, tb, c * 128:(c + 1) * 128], acc_done[k], fr)
                    yield
                    y = stt(xin[o][:, c, :], xin[o][:, c, :], Dm(c), ps[:, 0:T], ALU.mult, ALU.add, x, R["xt"])
                    pp.put(i, y)
                    yt.append(tt(xin[o][:, c, :], xin[o][:, c, :], sz[o][:, c, :], ALU.mult, y, R["zt"], eng="pool"))
                free["acc"] = x
                free["sz"][o] = yt
                posted[k, "sz"] = True
                yield
                obs = [None] * TB

                def norm(tb, i, ps, x):
                    s1 = p.op("dve", lambda e: e.bn_stats(lbn[:, tb, :], ps[:, 0:C]), x, free["ob"])
                    s2 = p.op("dve", lambda e: e.bn_aggr(lmv[:, tb, :], lbn[:, tb, :]), s1)
                    s3 = ts(lmv[:, tb, 1:2], lmv[:, tb, 1:2], LN_EPS, None, ALU.add, None, s2)
                    s4 = tt(lsc[:, tb, 0:1], lmv[:, tb, 1:2], mhalf[:, 0:1], ALU.pow, s3, eng="pool")
                    yield
                    yield
                    s5 = stt(lsc[:, tb, 1:2], lmv[:, tb, 0:1], -1.0, lsc[:, tb, 0:1], ALU.mult, ALU.mult, s4)
                    yield
                    obs[tb] = act(ob[:, tb, :], ps[:, 0:C], ACT.Identity, s5, free["ob"], scale=lsc[:, tb, 0:1], bias=lsc[:, tb, 1:2])
                    pp.put(i, obs[tb])

                nr = None
                for tb in range(TB):
                    i, ps, fr = pp.get()
                    for m in range(6):
                        x = mm(ps[:, 0:C], xin[o][:, m, tb * 128:(tb + 1) * 128], WoT[:, m, :], m == 0, m == 5, yt[m], fr, w_o)
                        yield
                        if nr is not None and next(nr, 1) == 1:
                            nr = None
                    nr = norm(tb, i, ps, x)
                free["xin"][o] = x
                posted[k, "xin"] = True
                yield
                for _ in nr:
                    yield
                yield
                for c in range(3):
                    i, ps, fr = pp.get()
                    for tb in range(TB):
                        x = tr(ps[:, tb * 128:(tb + 1) * 128], ob[:, tb, c * 128:(c + 1) * 128], obs, fr)
                    yield
                    y = stt(xb[:, c, :], ps[:, 0:T], pc[:, c, 0:1], xb[:, c, :], ALU.mult, ALU.add, x, beta_done[k])
                    pp.put(i, y)
                free["ob"] = x
                w = p.dma(f"x1o{k % 3}", xo[b, :, :, t0:t0 + T], xb[:], y)
                free["xs"][k % 3] = w
                stored.setdefault(("x1", b), []).append(w)

            for _ in stats(0):
                pass
            for _ in pre(0):
                pass

            for k in range(nk):
                threads = []
                if k > 0:
                    threads.append((post(k - 1), lambda n: n < 7 or n % 4 != 3))
                if k + 1 < nk:
                    threads.append((pre(k + 1), lambda n: True))
                if k % NQ == 2 and k // NQ + 1 < images:
                    threads.append((stats(k // NQ + 1), lambda n: n % 2))
                n = 0

                def step(n):
                    for g in list(threads):
                        if g[1](n) and next(g[0], 1) == 1:
                            threads.remove(g)

                for _ in scan(k):
                    step(n)
                    n += 1
                while threads:
                    step(n)
                    n += 1
            for _ in post(nk - 1):
                pass

        def fence():
            return p.last() + [t for v in stored.values() for t in v]

        def split(hi, lo, src, *waits):
            a = copy("act", hi, src, *waits)
            return a, tt(lo, src, hi.bitcast(F32), ALU.subtract, a, *waits)

        def layer12(x1_d, x3_d):
            fe = fence()
            ar = Arena(nc, late.at, "b")
            Win1 = ar("Win1", [128, 3, C])
            Fwd = ar("Fwd", [128, 128])
            Inv = ar("Inv", [128, 128])
            feff = ar("feff", [128, C])
            WoA = ar("WoA", [128, C])
            WoC = ar("WoC", [128, C])
            dw = ar("dw", [128, 3, 9])
            wn = ar("wn", [128, 3, 4])
            gw = ar("gw", [128, 3, 4])
            gb = ar("gb", [1, 4])
            row = ar("row", [1, 12])
            par = ar("par", [128, 12])
            Th = ar("Th", [128, 4, 1920], F32R)
            Tl = ar("Tl", [128, 4, 1920], F32R)
            x = [ar(f"x{i}", [128, 3, L]) for i in range(2)]
            xn = ar("xn", [128, 3, L])
            tT = Ring([ar(f"tT{i}", [128, C]) for i in range(2)])
            tf = Ring([ar(f"tf{i}", [128, C]) for i in range(2)])
            bn = ar("bn", [128, 3, NQ, 6])
            mv = ar("mv", [128, 3, 2])
            gs = ar("gs", [128, 3, 3])
            sc = ar("sc", [128, 2, 3])
            u0 = ar.at
            timg = [ar(f"ti{i}", [128, 50, 50]) for i in range(3)]
            cv = [ar(f"cv{i}", [128, L]) for i in range(3)]
            ar.at = u0
            xTh = ar("xTh", [128, NT, C], F32R)
            xTl = ar("xTl", [128, NT, C], F32R)
            ar.at = u0
            G0 = ar("G0", [128, 1920])
            G1 = ar("G1", [128, 1920])
            GM = ar("GM", [128, 1920])
            gt = ar("gt", [128, 1920])
            gu = ar("gu", [128, 1920])
            S40 = ar("S40", [40, 128])
            f40 = ar("f40", [40, C])
            banks = Ring(bank + [wide[0][:, 0:512], wide[0][:, 512:1024], wide[1][:, 0:512], wide[1][:, 512:1024]])
            xv = x1_d.rearrange("b (c p) l -> b p c l", p=128)
            xo = x3_d.rearrange("b (c p) l -> b p c l", p=128)

            ld = [p.dma(f"x1i{i}", x[i][:], xv[i], fe, stored.get(("x1", i), [])) for i in range(min(2, images))]
            w = [p.dma(n, t[:], src, fe) for n, t, src in (
                ("Win1", Win1, d["Win1T"].rearrange("(k p) n -> p k n", p=128)), ("Fwd", Fwd, d["Fwd"]), ("Inv", Inv, d["Inv"]),
                ("S40", S40, d["S40"]), ("f40", f40, d["f40"]), ("WoA", WoA, d["Wo1T"][0:128, :]),
                ("dw", dw, d["dw"]), ("wn", wn, d["wn"]), ("gw", gw, d["gw"].rearrange("(k p) n -> p k n", p=128)),
                ("gb", gb, d["gb"]), ("row", row, d["row"]), ("G0", G0, d["G0"]), ("G1", G1, d["G1"]), ("GM", GM, d["GM"]))]
            w.append(p.dma("WoC", WoC[64:128, :], d["Wo1T"][128:192, :], fe))

            i, ps, fr = banks.get()
            a = mm(ps[:, 0:C], S40[:], f40[:], True, True, w, fr, t_const, fe)
            t_feff = copy("act", feff[:], ps[:, 0:C], a)
            banks.put(i, t_feff)
            i, ps, fr = banks.get()
            a = mm(ps[:, 0:12], ones[0:1, :], row[:], True, True, w, fr, t_const)
            b_ = copy("dve", par[:], ps[:, 0:12], a)
            banks.put(i, b_)
            r_ = p.op("dve", lambda e: e.reciprocal(par[:, 8:12], par[:, 8:12]), b_)
            r_ = ts(par[:], par[:], -1.0, None, ALU.mult, None, r_)
            t_T = None
            for n in range(4):
                a0 = act(gt[:], G0[:], ACT.Abs, r_, t_T, bias=par[:, 2 * n:2 * n + 1])
                a1 = act(gu[:], G1[:], ACT.Abs, r_, t_T, bias=par[:, 2 * n + 1:2 * n + 2])
                a2 = tt(gt[:], gt[:], gu[:], ALU.add, a0, a1)
                a3 = ts(gt[:], gt[:], par[:, 8 + n:9 + n], 1.0, ALU.mult, ALU.add, a2)
                a4 = stt(gt[:], gt[:], 0.0, GM[:], ALU.max, ALU.mult, a3)
                t_T = split(Th[:, n, :], Tl[:, n, :], gt[:], a4)
            t_T = list(t_T)
            u_free = [t_T, t_feff]
            xn_free = [fe]
            sc_free = None

            def normalize(xt, ready, out, out_free, patches=False):
                for q in range(NQ):
                    for c in range(CT):
                        t = p.op("dve", lambda e, c=c, q=q: e.bn_stats(bn[:, c, q, :], xt[:, c, q * T:(q + 1) * T]), ready, out_free)
                i, ps, fr = banks.get()
                g, f = finish_stats(bn, mv, gs, ps, fr, t, out, out_free)
                banks.put(i, g)
                n = []
                for r in range(NQ if patches else 1):
                    for c in range(CT):
                        src, dst = xt[:, c, :], xn[:, c, :]
                        if patches:
                            src = xt[:, c, r * T:(r + 1) * T].rearrange("p (h j w) -> p j h w", j=3, w=16)
                            dst = xn[:, c, r * T:(r + 1) * T].rearrange("p (j h w) -> p j h w", j=3, w=16)
                        n.append(ts(dst, src, out[:, 0, c:c + 1], out[:, 1, c:c + 1], ALU.mult, ALU.add, f, xn_free))
                return n

            def mix(b, xt, nrm):
                zero = [p.op("pool", lambda e, i=i: e.memset(timg[i][:], 0.0), u_free) for i in range(3)]
                st1, st2, ob = {}, {}, {}
                img = [[None] * 6 for _ in range(3)]
                last = None
                conv_t = [[None] * 3 for _ in range(3)]

                def conv(g):
                    need = [img[o][r] for o in range(3) for r in range(min(6, 2 * g + 3))]
                    prev = [None] * 3
                    for k in range(9):
                        dy, dx = divmod(k, 3)
                        for o in range(3):
                            src = timg[o][:, 16 * g + dy:16 * g + dy + 16, dx:dx + W]
                            dst = cv[o][:, 768 * g:768 * g + 768].rearrange("p (h w) -> p h w", w=W)
                            if k == 0:
                                prev[o] = ts(dst, src, dw[:, o, 0:1], None, ALU.mult, None, need, u_free)
                            else:
                                prev[o] = stt(dst, src, dw[:, o, k:k + 1], dst, ALU.mult, ALU.add, prev[o])
                    for o in range(3):
                        conv_t[o][g] = prev[o]

                for n in range(NT + 2):
                    if n < NT:
                        r, j = divmod(n, 3)
                        i, ps, fr = banks.get()
                        for kk in range(CT):
                            a = mm(ps[:, 0:C], xn[:, kk, n * 128:(n + 1) * 128], Win1[:, kk, :], kk == 0, kk == 2, nrm, fr, w)
                        last = a
                        ti, tb_, tfr = tT.get()
                        c_ = copy("act", tb_[:], ps[:, 0:C], a, tfr, fe)
                        banks.put(i, c_)
                        st1[n] = (ti, tb_, c_)
                    if 1 <= n <= NT:
                        ti, tb_, c_ = st1[n - 1]
                        i, ps, fr = banks.get()
                        a = mm(ps[:, 0:C], Fwd[:], tb_[:], True, True, c_, fr)
                        tT.put(ti, a)
                        fi, fb, ffr = tf.get()
                        c_ = tt(fb[:], ps[:, 0:C], feff[:], ALU.mult, a, ffr, t_feff, fe)
                        banks.put(i, c_)
                        st2[n - 1] = (fi, fb, c_)
                    if n >= 2:
                        r, j = divmod(n - 2, 3)
                        fi, fb, c_ = st2[n - 2]
                        if j == 0:
                            ob = {o: banks.get() for o in range(3)}
                        for o in range(3):
                            i, ps, fr = ob[o]
                            cols = fb[:, o * 128:(o + 1) * 128]
                            a = mm(ps[:, 0:T].rearrange("p (h w) -> p h w", w=W)[:, :, 16 * j:16 * j + 16], cols,
                                   Inv[:].rearrange("p (h w) -> p h w", w=16), True, True, c_, fr, skip=True)
                            if j == 2:
                                img[o][r] = copy("act", timg[o][:, 8 * r + 1:8 * r + 9, 1:1 + W],
                                                 ps[:, 0:T].rearrange("p (h w) -> p h w", w=W), a, zero)
                                banks.put(i, img[o][r])
                        tf.put(fi, a)
                        if j == 2 and r in (2, 4):
                            conv(r // 2 - 1)
                conv(2)
                xn_free[:] = [last]
                out = None
                for g in range(3):
                    sl = slice(768 * g, 768 * g + 768)
                    a = act(cv[0][:, sl], cv[0][:, sl], ACT.Gelu, conv_t[0][g])
                    a = tt(cv[0][:, sl], cv[0][:, sl], cv[1][:, sl], ALU.mult, a, conv_t[1][g])
                    c_ = act(cv[1][64:128, sl], cv[2][0:64, sl], ACT.Gelu, conv_t[2][g], a)
                    c_ = tt(cv[1][64:128, sl], cv[1][64:128, sl], cv[2][64:128, sl], ALU.mult, c_)
                    for hf in range(2):
                        s2 = slice(768 * g + T * hf, 768 * g + T * hf + T)
                        for o in range(3):
                            i, ps, fr = banks.get()
                            m = mm(ps[:, 0:T], WoA[:, o * 128:(o + 1) * 128], cv[0][:, s2], True, False, a, fr, w)
                            m = mm(ps[:, 0:T], WoC[64:128, o * 128:(o + 1) * 128], cv[1][64:128, s2], False, True, c_)
                            out = tt(xt[:, o, s2], xt[:, o, s2], ps[:, 0:T], ALU.add, m)
                            banks.put(i, out)
                u_free[:] = [m]
                return out

            def sparse(b, xt, nrm):
                hl = []
                for j in range(NT):
                    i, ps, fr = banks.get()
                    for c in range(CT):
                        a = tr(ps[:, c * 128:(c + 1) * 128], xn[:, c, j * 128:(j + 1) * 128], nrm, fr, t_const)
                    h = copy("act", xTh[:, j, :], ps[:, 0:C], a, u_free)
                    l_ = tt(xTl[:, j, :], ps[:, 0:C], xTh[:, j, :].bitcast(F32), ALU.subtract, h)
                    banks.put(i, l_)
                    hl.append([h, l_])
                xn_free[:] = [a]
                off = [0, 128, 384, 768, 1152, 1536, 1792]
                wd = [128, 256, 384, 384, 384, 256, 128]
                os_ = [0, 0, 0, 0, 0, 128, 256]
                out = None
                for r in range(6):
                    js = [jj for jj in (2, 3, 4, 1, 5, 0, 6) if 0 <= 3 * r - 2 + jj < NT]
                    for c in range(CT):
                        sl = slice(T * r, T * r + T)
                        prev = None
                        for n in range(4):
                            i, ps, fr = banks.get()
                            q = [(jj, A, B) for jj in js for A, B in ((xTh, Th), (xTl, Th), (xTh, Tl))]
                            for u, (jj, A, B) in enumerate(q):
                                a = mm(ps[:, os_[jj]:os_[jj] + wd[jj]], A[:, 3 * r - 2 + jj, c * 128:(c + 1) * 128],
                                       B[:, n, off[jj]:off[jj] + wd[jj]], u == 0, u == len(q) - 1, hl[3 * r - 2 + jj], fr, t_T, skip=True)
                            prev = stt(xt[:, c, sl], ps[:, 0:T], wn[:, c, n:n + 1], xt[:, c, sl], ALU.mult, ALU.add, a, prev)
                            banks.put(i, prev)
                        out = prev
                u_free[:] = [a]
                return out

            def gate(b, nrm):
                i, ps, fr = banks.get()
                for j in range(NT):
                    for kk in range(CT):
                        mm(ps[:, 4 * j:4 * j + 4], xn[:, kk, j * 128:(j + 1) * 128], gw[:, kk, :], kk == 0, False, nrm, fr)
                    a = mm(ps[:, 4 * j:4 * j + 4], ones[0:1, :], gb[:], False, True)
                xn_free[:] = [a]
                g = copy("act", coef[:, b * NT:(b + 1) * NT, :], ps[:, 0:4 * NT].rearrange("p (j e) -> p j e", e=4), a, fe)
                banks.put(i, g)
                return g

            gated = []
            for b in range(images):
                xt = x[b % 2]
                nrm = normalize(xt, [ld[b], u_free if b == 0 else None], sc, xn_free, patches=True)
                y = mix(b, xt, nrm)
                nrm = normalize(xt, y, sc, xn_free)
                y = sparse(b, xt, nrm)
                nrm = normalize(xt, y, gst[:, b], None)
                gated.append(gate(b, nrm))
                o = p.dma(f"x3o{b % 2}", xo[b], xt[:], y)
                stored[("x3", b)] = [o]
                if b + 2 < images:
                    ld.append(p.dma(f"x1i{b % 2}", xt[:], xv[b + 2], o, nrm, stored.get(("x1", b + 2), [])))
            return gated

        def layer3(x3_d, out_d, gated):
            fe = fence()
            ar = Arena(nc, late.at, "c")
            W1h = ar("W1h", [128, 3, 4 * C], F32R)
            W1l = ar("W1l", [128, 3, 4 * C], F32R)
            W2h = ar("W2h", [128, 3, 4 * C], F32R)
            W2l = ar("W2l", [128, 3, 4 * C], F32R)
            b1 = ar("b1", [128, 3, 4])
            b2 = ar("b2", [4, C])
            xs = [ar(f"xs{i}", [128, 3, T]) for i in range(3)]
            xn = ar("xn", [128, 3, T])
            xh = [ar(f"xh{i}", [128, 3, T], F32R) for i in range(2)]
            xl = [ar(f"xl{i}", [128, 3, T], F32R) for i in range(2)]
            hf = Ring([ar(f"hf{i}", [128, T]) for i in range(3)])
            hh = Ring([ar(f"hh{i}", [128, 3, T], F32R) for i in range(2)])
            hl = Ring([ar(f"hl{i}", [128, 3, T], F32R) for i in range(2)])
            acc = [ar(f"acc{i}", [128, TB, C]) for i in range(2)]
            cT = [ar(f"cT{i}", [4, T]) for i in range(2)]
            mx = ar("mx", [128, NB * NT])
            v1 = ar("v1", [128, NB * NT])
            cum = ar("cum", [128, NB * NT])
            eq = ar("eq", [128, NB * NT])
            wk = ar("wk", [128, 2, NB * NT])
            fk = ar("fk", [128, 2, 4, NB * NT])
            fl = ar("fl", [128, 8])
            fb = ar("fb", [128, 8])
            banks = Ring(bank + [wide[0][:, 0:512], wide[0][:, 512:1024], wide[1][:, 0:512], wide[1][:, 512:1024]])
            xv = x3_d.rearrange("b (c p) l -> b p c l", p=128)
            ov = out_d.rearrange("b (c p) l -> b p c l", p=128)
            u0 = ar.at
            Wt = [ar(f"Wt{i}", [128, 3, 4 * C]) for i in range(2)]
            l1 = p.dma("W1", Wt[0][:], d["W1T"].rearrange("(k p) n -> p k n", p=128), fe)
            l2 = p.dma("W2", Wt[1][:], d["W2T"].rearrange("(k p) n -> p k n", p=128), fe)
            lb = [p.dma("b1", b1[:], d["b1"], fe), p.dma("b2", b2[:], d["b2"], fe)]
            w1 = list(split(W1h[:], W1l[:], Wt[0][:], l1))
            w2 = list(split(W2h[:], W2l[:], Wt[1][:], l2))

            M = images * NT
            sc = lambda e: coef[:, 0:M, e]
            X = lambda t: t[:, 0:M]
            t = tt(X(mx), sc(0), sc(1), ALU.max, gated, fe)
            t = tt(X(mx), X(mx), sc(2), ALU.max, t)
            t = tt(X(mx), X(mx), sc(3), ALU.max, t)
            a = [tt(sc(e), sc(e), X(mx), ALU.subtract, t) for e in range(4)]
            a = act(coef[:, 0:M, :], coef[:, 0:M, :], ACT.Exp, a)
            t = tt(X(v1), sc(0), sc(1), ALU.add, a)
            t = tt(X(v1), X(v1), sc(2), ALU.add, t)
            t = tt(X(v1), X(v1), sc(3), ALU.add, t)
            t = p.op("dve", lambda e: e.reciprocal(X(v1), X(v1)), t)
            a = [tt(sc(e), sc(e), X(v1), ALU.mult, t) for e in range(4)]
            for k in range(2):
                top = wk[:, k, 0:M]
                t = tt(top, sc(0), sc(1), ALU.max, a)
                t = tt(top, top, sc(2), ALU.max, t)
                t = tt(top, top, sc(3), ALU.max, t)
                z = None
                for e in range(4):
                    f = fk[:, k, e, 0:M]
                    q = tt(X(eq), sc(e), top, ALU.is_equal, t, z)
                    if e == 0:
                        z = copy("dve", f, X(eq), q)
                        z = copy("dve", X(cum), X(eq), z)
                    else:
                        z = tt(f, X(eq), X(cum), ALU.is_gt, q)
                        z = tt(X(cum), X(cum), X(eq), ALU.max, z)
                if k == 0:
                    a = [stt(sc(e), fk[:, k, e, 0:M], -2.0, sc(e), ALU.mult, ALU.add, z) for e in range(4)]
                z = p.op("dve", lambda e, k=k: e.tensor_reduce(fl[:, 4 * k:4 * k + 4], fk[:, k, :, 0:M], mybir.AxisListType.X, ALU.max), z)
            t = tt(X(eq), wk[:, 1, 0:M], wk[:, 0, 0:M], ALU.subtract, z)
            t = act(X(eq), X(eq), ACT.Exp, t)
            t = ts(X(cum), X(eq), 1.0, None, ALU.add, None, t)
            r0 = p.op("dve", lambda e: e.reciprocal(wk[:, 0, 0:M], X(cum)), t)
            r1 = tt(wk[:, 1, 0:M], X(eq), wk[:, 0, 0:M], ALU.mult, r0)
            i, ps, fr = banks.get()
            m = mm(ps[:, 0:8], ones[:], fl[:], True, True, z, fr)
            g = ts(fb[:], ps[:, 0:8], 0.0, None, ALU.is_gt, None, m, fe)
            banks.put(i, g)
            tc_ = []
            for e in range(4):
                q = ts(sc(e), wk[:, 0, 0:M], fb[:, e:e + 1], None, ALU.mult, None, g, r1)
                tc_.append(stt(sc(e), wk[:, 1, 0:M], fb[:, 4 + e:5 + e], sc(e), ALU.mult, ALU.add, q))

            xs_free, xh_free, acc_free, cT_free, xn_free = [fe] * 3, [fe] * 2, [fe] * 2, [fe] * 2, fe
            nk = images * NQ
            pre_t = {}

            def pre(k):
                b, q = divmod(k, NQ)
                o = k % 2
                nonlocal xn_free
                ld = p.dma(f"x3i{k % 3}", xs[k % 3][:], xv[b, :, :, q * T:(q + 1) * T], xs_free[k % 3], stored.get(("x3", b), []))
                for c in range(CT):
                    n = ts(xn[:, c, :], xs[k % 3][:, c, :], gst[:, b, 0, c:c + 1], gst[:, b, 1, c:c + 1], ALU.mult, ALU.add, ld, xn_free)
                s = split(xh[o][:], xl[o][:], xn[:], n, xh_free[o])
                xn_free = list(s)
                i, ps, fr = banks.get()
                for tb in range(TB):
                    a = tr(ps[0:4, tb * 128:(tb + 1) * 128], coef[:, k * TB + tb, :], tc_, fr)
                c_ = copy("act", cT[o][:], ps[0:4, 0:T], a, cT_free[o])
                banks.put(i, c_)
                pre_t[k] = (list(s), ld, c_)

            def hidden(k, e):
                o = k % 2
                s = pre_t[k][0]
                ih, H, fh = hh.get()
                il, Lw, fl_ = hl.get()
                done = []
                for m in range(3):
                    i, ps, fr = banks.get()
                    q = [(kk, A, B) for kk in range(CT) for A, B in ((W1h, xh[o]), (W1l, xh[o]), (W1h, xl[o]))]
                    for u, (kk, A, B) in enumerate(q):
                        a = mm(ps[:, 0:T], A[:, kk, e * C + m * 128:e * C + (m + 1) * 128], B[:, kk, :], u == 0, u == len(q) - 1, s, fr, w1)
                    j, f, ff = hf.get()
                    r = act(f[:], ps[:, 0:T], ACT.Relu, a, ff, lb, fe, bias=b1[:, m, e:e + 1])
                    banks.put(i, r)
                    c1 = copy("act", H[:, m, :], f[:], r, fh, fe)
                    c2 = tt(Lw[:, m, :], f[:], H[:, m, :].bitcast(F32), ALU.subtract, c1, fl_)
                    hf.put(j, c2)
                    done.append([c1, c2])
                xh_free[o] = a
                return ih, H, il, Lw, done

            acc_t = {}

            def combine(k, e, hd):
                o = k % 2
                ih, H, il, Lw, done = hd
                for tb in range(TB):
                    i, ps, fr = banks.get()
                    q = [(m, A, B) for m in range(3) for A, B in ((H, W2h), (Lw, W2h), (H, W2l))]
                    for u, (m, A, B) in enumerate(q):
                        a = mm(ps[:, 0:C], A[:, m, tb * 128:(tb + 1) * 128], B[:, m, e * C:(e + 1) * C], u == 0, u == len(q) - 1, done[m], fr, w2)
                    cf = coef[:, k * TB + tb, e:e + 1]
                    if e == 0:
                        y = ts(acc[o][:, tb, :], ps[:, 0:C], cf, None, ALU.mult, None, a, acc_free[o], tc_)
                    else:
                        y = stt(acc[o][:, tb, :], ps[:, 0:C], cf, acc[o][:, tb, :], ALU.mult, ALU.add, a, acc_t[k, tb])
                    acc_t[k, tb] = y
                    banks.put(i, y)
                hh.put(ih, a)
                hl.put(il, a)

            def finish(k):
                b, q = divmod(k, NQ)
                o = k % 2
                for c in range(CT):
                    i, ps, fr = banks.get()
                    for tb in range(TB):
                        p.op("pe", lambda e, tb=tb, c=c, ps=ps: e.matmul(
                            ps[:, tb * 128:(tb + 1) * 128], acc[o][:, tb, c * 128:(c + 1) * 128], ident[:],
                            start=tb == 0, stop=False, is_transpose=True, skip_group_check=True), acc_t[k, tb], fr)
                    a = mm(ps[:, 0:T], b2[:, c * 128:(c + 1) * 128], cT[o][:], False, True, pre_t[k][2], lb, skip=True)
                    y = tt(xs[k % 3][:, c, :], xs[k % 3][:, c, :], ps[:, 0:T], ALU.add, a)
                    banks.put(i, y)
                acc_free[o] = a
                cT_free[o] = a
                w = p.dma(f"oo{k % 3}", ov[b, :, :, q * T:(q + 1) * T], xs[k % 3][:], y)
                xs_free[k % 3] = w
                stored[("out", k)] = [w]

            pre(0)
            queue = [(k, e) for k in range(nk) for e in range(4)]
            hd = hidden(0, 0)
            for n, (k, e) in enumerate(queue):
                nxt = None
                if n + 1 < len(queue):
                    if e == 2 and k + 1 < nk:
                        pre(k + 1)
                    nxt = hidden(*queue[n + 1])
                combine(k, e, hd)
                if e == 0 and k > 0:
                    finish(k - 1)
                hd = nxt
            finish(nk - 1)

        if 0 in layers:
            layer0(d["x"], d["x1"])
        gated = []
        if 1 in layers:
            gated = layer12(d["x1"], d["x3"])
        if 3 in layers:
            layer3(d["x3"], d["out"], gated)
        p.op("sp", lambda e: e.nop(), *[t for v in stored.values() for t in v])
        block = ctx.enter_context(nc.Block())
        p.emit(block)


def constants():
    a = {}
    dofs = []
    for ky in range(8):
        for kx in range(5):
            if kx in (0, 4):
                if ky in (0, 4):
                    dofs.append((ky, kx, 0, 1.0))
                elif ky < 4:
                    dofs += [(ky, kx, 0, 2.0), (ky, kx, 1, 2.0)]
            else:
                dofs += [(ky, kx, 0, 2.0), (ky, kx, 1, 2.0)]
    assert len(dofs) == 64
    yy, xx = np.meshgrid(np.arange(8), np.arange(8), indexing="ij")
    fwd, inv, sel = np.zeros((128, 128)), np.zeros((128, 128)), np.zeros((40, 128))
    for i, (ky, kx, odd, m) in enumerate(dofs):
        ang = 2 * np.pi * ((ky * yy + kx * xx) % 8) / 8
        v = np.sin(ang) if odd else np.cos(ang)
        for h in range(2):
            tok = (yy * 16 + 8 * h + xx).ravel()
            fwd[tok, 64 * h + i] = v.ravel()
            inv[64 * h + i, tok] = m / 64 * v.ravel()
            if kx in (0, 4):
                sel[ky * 5 + kx, 64 * h + i] += 0.5
                sel[(-ky) % 8 * 5 + kx, 64 * h + i] += 0.5
            else:
                sel[ky * 5 + kx, 64 * h + i] = 1.0
    a["Fwd"], a["Inv"], a["S40"] = (v.astype(np.float32) for v in (fwd, inv, sel))
    lin = np.linspace(-1.0, 1.0, K11, dtype=np.float32)
    G0, G1, GM = (np.zeros((128, 1920), np.float32) for _ in range(3))
    off = 0
    i = np.arange(128)[:, None]
    for jj in range(7):
        o0, n = [(0, 1), (0, 2), (0, 3), (0, 3), (0, 3), (1, 2), (2, 1)][jj]
        c = 128 * o0 + np.arange(128 * n)[None, :]
        fi = 128 * (jj - 2) + i
        dy, dx = fi // W - c // W, fi % W - c % W
        ok = (abs(dy) <= 5) & (abs(dx) <= 5)
        sl = slice(off, off + 128 * n)
        G0[:, sl] = np.where(ok, lin[np.clip(dx + 5, 0, 10)], 0)
        G1[:, sl] = np.where(ok, lin[np.clip(5 - dy, 0, 10)], 0)
        GM[:, sl] = ok
        off += 128 * n
    a["G0"], a["G1"], a["GM"] = G0, G1, GM
    return a


def lay(inputs):
    f = {k: np.asarray(v) for k, v in inputs.items()}
    a = {}
    a["x"] = np.ascontiguousarray(f["x"].reshape(NB, C, L))
    a["WinT"] = np.ascontiguousarray(f["L0_conv_in_proj_w"].T)
    wx = f["L0_conv_x_proj_w"].T
    a["WxT"] = np.concatenate([wx[:, :RK], np.zeros((DI, 32 - RK), np.float32), wx[:, RK:]], axis=1)
    a["WdtT"] = np.ascontiguousarray(f["L0_conv_dt_proj_w"].T)
    a["WoT"] = np.ascontiguousarray(f["L0_conv_out_proj_w"].T)
    pv = np.concatenate([f["L0_conv_conv_w"], f["L0_conv_conv_b"][:, None], f["L0_conv_dt_proj_b"][:, None],
                         f["L0_conv_D"][:, None], f["L0_conv_A_log"]], axis=1)
    a["pv"] = np.ascontiguousarray(pv.reshape(6, 128, 23).transpose(1, 0, 2))
    pc = np.stack([f["L0_conv_ln_gamma"], f["L0_conv_ln_beta"]], axis=1)
    a["pc"] = np.ascontiguousarray(pc.reshape(3, 128, 2).transpose(1, 0, 2))
    ch = np.arange(C) // 12
    g = (ch[:, None] == ch[None, :]).astype(np.float32).reshape(3, 128, 3, 128)
    a["gm"] = np.ascontiguousarray(g.transpose(1, 0, 2, 3).reshape(128, 9, 128))
    a.update(constants())
    order = np.concatenate([np.arange(0, 128), np.arange(192, 320), np.arange(128, 192), np.arange(320, 384)])
    a["Win1T"] = np.ascontiguousarray(f["L1_conv_w_in"][order].T)
    a["f40"] = np.ascontiguousarray(f["L1_conv_fft_filter"].reshape(C, 40)[order].T)
    a["Wo1T"] = np.ascontiguousarray(f["L1_conv_w_out"].T)
    a["dw"] = np.ascontiguousarray(f["L1_conv_w_dw"].reshape(C, 9)[order].reshape(3, 128, 9).transpose(1, 0, 2))
    a["wn"] = np.ascontiguousarray(f["L2_conv_weights"][0].reshape(3, 128, 4).transpose(1, 0, 2))
    a["row"] = np.concatenate([f["L2_conv_weight_coord"].reshape(8), f["L2_conv_radius"].reshape(4)])[None, :]
    a["gw"] = np.ascontiguousarray(f["L3_conv_gate_w"])
    a["gb"] = np.ascontiguousarray(f["L3_conv_gate_b"][None, :])
    a["W1T"] = np.ascontiguousarray(f["L3_conv_w1"].transpose(2, 0, 1).reshape(C, 4 * C))
    a["W2T"] = np.ascontiguousarray(f["L3_conv_w2"].transpose(2, 0, 1).reshape(C, 4 * C))
    a["b1"] = np.ascontiguousarray(f["L3_conv_b1"].reshape(4, 3, 128).transpose(2, 1, 0))
    a["b2"] = np.ascontiguousarray(f["L3_conv_b2"])
    a["ident"] = np.eye(128, dtype=np.float32)
    return a


def kernel(**inputs):
    import concourse.bacc as bacc
    from concourse.bass_utils import run_bass_kernel_spmd

    nc = bacc.Bacc("TRN2", target_bir_lowering=False, num_devices=1, dynamic_dma_scratch_size=1024)
    arrays = lay(inputs)
    d = {n: nc.dram_tensor(f"in_{n}", a.shape, F32, kind="ExternalInput").ap() for n, a in arrays.items()}
    d["out"] = nc.dram_tensor("out", [NB, C, L], F32, kind="ExternalOutput").ap()
    for n in ("x1", "x3"):
        d[n] = nc.dram_tensor(n, [NB, C, L], F32).ap()
    build(nc, d)
    r = run_bass_kernel_spmd(nc, [{f"in_{n}": a for n, a in arrays.items()}], core_ids=[0])
    return r.results[0]["out"].reshape(NB, C, H, W)
```

```python
from contextlib import ExitStack

import numpy as np

import concourse.bass as bass
from concourse import mybir

F32 = mybir.dt.float32
F32R = mybir.dt.float32r
ALU = mybir.AluOpType
ACT = mybir.ActivationFunctionType

NB, C, H, W = 4, 384, 48, 48
L = H * W
CT = 3
DI = 768
DT_ = 6
NS = 16
RK = 24
T = 384
TB = 3
NQ = L // T
NCH = NB * NQ
NT = L // 128
GN_EPS = 1e-5
LN_EPS = 1e-5
K11 = 11
CONV_DVE = ((0, 1), (2, 3), (4, 5))
CONV_POOL = ()
GAP_SILU = 5
MM, RATE = 0.64, 0.62
LOG = False
S_COST, M_COST, M_A, M_B, CONV_RATE, HEAD_FROM, REST = 130.0, 90.0, 0.3, 0.8, 0.7, 0.7, 4.0
BANDS = ((0, 9), (9, 19), (19, 29), (29, 39), (39, 48))
GAP_LN = 6
ENGINES = ("pe", "act", "dve", "pool", "sp")


class Done:

    __slots__ = ("eng", "make", "waits", "sem", "value", "used")

    def __init__(self, eng, make, waits, sem, value):
        self.eng, self.make, self.waits = eng, make, waits
        self.sem, self.value, self.used = sem, value, sem is not None


def flat(waits):
    for w in waits:
        if w is None:
            continue
        if isinstance(w, Done):
            yield w
        else:
            yield from flat(w)


class Queues:

    def __init__(self, nc, ctx):
        self.nc, self.ctx = nc, ctx
        self.q = {e: [] for e in ENGINES}
        self.sems = {e: ctx.enter_context(nc.semaphore(f"s_{e}")) for e in ENGINES}
        self.dma_sems, self.dma_count = {}, {}

    def op(self, eng, make, *waits):
        d = Done(eng, make, list(flat(waits)), None, 0)
        for w in d.waits:
            w.used = True
        self.q[eng].append(d)
        return d

    def dma(self, name, out, in_, *waits, eng="sp"):
        if name not in self.dma_sems:
            self.dma_sems[name] = self.ctx.enter_context(self.nc.semaphore(f"d_{name}"))
            self.dma_count[name] = 0
        self.dma_count[name] += 16
        d = Done(eng, lambda e: e.dma_start(out, in_), list(flat(waits)),
                 self.dma_sems[name], self.dma_count[name])
        for w in d.waits:
            w.used = True
        self.q[eng].append(d)
        return d

    def last(self):
        return [self.q[e][-1] for e in ENGINES if self.q[e] and self.q[e][-1].sem is None]

    def emit(self, block):
        for e in ENGINES:
            n = 0
            for d in self.q[e]:
                if d.sem is None and d.used:
                    n += 1
                    d.value = n

        def run(name, eng):
            seen = {}
            for d in self.q[name]:
                need = {}
                for w in d.waits:
                    key = (w.eng, None) if w.sem is None else ("dma", id(w.sem))
                    s = self.sems[w.eng] if w.sem is None else w.sem
                    if w.value > need.get(key, (None, 0))[1]:
                        need[key] = (s, w.value)
                for key, (s, v) in need.items():
                    if seen.get(key, 0) < v:
                        seen[key] = v
                        eng.wait_ge(s, v)
                ins = d.make(eng)
                if d.sem is not None:
                    ins.then_inc(d.sem, 16)
                elif d.used:
                    ins.then_inc(self.sems[name], 1)

        block.tensor(lambda e: run("pe", e))
        block.scalar(lambda e: run("act", e))
        block.vector(lambda e: run("dve", e))
        block.gpsimd(lambda e: run("pool", e))
        block.sync(lambda e: run("sp", e))


class Ring:

    def __init__(self, bufs):
        self.bufs, self.free, self.held, self.n = bufs, [None] * len(bufs), [False] * len(bufs), -1

    def get(self):
        for _ in self.bufs:
            self.n += 1
            i = self.n % len(self.bufs)
            if not self.held[i]:
                self.held[i] = True
                return i, self.bufs[i], self.free[i]
        raise RuntimeError("no buffer of the ring is free")

    def put(self, i, done):
        assert self.held[i]
        self.held[i] = False
        self.free[i] = done


class Arena:

    def __init__(self, nc, base, tag):
        self.nc, self.at, self.tag = nc, (base + 63) // 64 * 64, tag

    def __call__(self, name, shape, dt=F32):
        n = 4
        for s in shape[1:]:
            n *= s
        off = self.at
        self.at = (off + n + 63) // 64 * 64
        return self.nc.alloc_sbuf_tensor_at(f"{self.tag}_{name}", shape, dt, offset=off)


def build(nc, d, layers=(0, 1, 3), images=NB):
    ctx = ExitStack()
    with ctx:
        p = Queues(nc, ctx)
        bank = [ctx.enter_context(nc.psum_tensor(f"ps{i}", [128, 512], F32)) for i in range(4)]
        wide = [ctx.enter_context(nc.psum_tensor(f"pw{i}", [128, 1024], F32)) for i in range(2)]
        base0 = nc.sbuf_base
        keep = Arena(nc, base0, "g")
        ident = keep("ident", [128, 128])
        gm = keep("gm", [128, 9, 128])
        ones = keep("ones", [128, 128])
        mhalf = keep("mhalf", [128, 4])
        base = keep.at
        late = Arena(nc, base, "g2")
        coef = late("coef", [128, NB * NT, 4])
        gst = late("gst", [128, NB, 2, 3])

        t_const = [p.dma("ident", ident[:], d["ident"]), p.dma("gm", gm[:], d["gm"])]
        t_ones = p.op("pool", lambda e: e.memset(ones[:], 1.0))
        t_mh = p.op("pool", lambda e: e.memset(mhalf[:], -0.5))
        t_const += [t_ones, t_mh]

        def mm(out, lhsT, rhs, start, stop, *waits, skip=False):
            return p.op("pe", lambda e: e.matmul(out, lhsT, rhs, start=start, stop=stop, skip_group_check=skip), *waits)

        def tr(out, in_, *waits):
            n = in_.shape[0]
            return p.op("pe", lambda e: e.transpose(out, in_, ident[0:n, 0:n]), *waits)

        def act(out, in_, func, *waits, **kw):
            return p.op("act", lambda e: e.activation(out, in_, func, **kw), *waits)

        def ts(out, in_, s1, s2, op0, op1, *waits, eng="dve"):
            if op1 is None:
                return p.op(eng, lambda e: e.tensor_scalar(out, in_, s1, None, op0), *waits)
            return p.op(eng, lambda e: e.tensor_scalar(out, in_, s1, s2, op0, op1), *waits)

        def tt(out, a, b, op, *waits, eng="dve"):
            return p.op(eng, lambda e: e.tensor_tensor(out, a, b, op), *waits)

        def stt(out, a, s, b, op0, op1, *waits):
            return p.op("dve", lambda e: e.scalar_tensor_tensor(out=out, in0=a, scalar=s, in1=b, op0=op0, op1=op1), *waits)

        def copy(eng, out, in_, *waits):
            if eng == "act":
                return act(out, in_, ACT.Copy, *waits)
            return p.op(eng, lambda e: e.tensor_copy(out, in_), *waits)

        def finish_stats(bn, mv, gs, ps, ps_free, bn_done, out, out_free):
            a = None
            for c in range(CT):
                a = p.op("dve", lambda e, c=c: e.bn_aggr(mv[:, c, :], bn[:, c, :, :].rearrange("p k s -> p (k s)")), bn_done, out_free)
            b = tt(gs[:, 0, :], mv[:, :, 0], mv[:, :, 0], ALU.mult, a)
            b = tt(mv[:, :, 1], mv[:, :, 1], gs[:, 0, :], ALU.add, b)
            last = None
            for co in range(CT):
                cis = [ci for ci in range(CT) if abs(ci - co) <= 1]
                for ci in cis:
                    last = mm(ps[:, 2 * co:2 * co + 2], gm[:, 3 * ci + co, :], mv[:, ci, :],
                              ci == cis[0], ci == cis[-1], b, ps_free, t_const)
            g = ts(gs[:, 1:3, :], ps[:, 0:6].rearrange("p (c k) -> p k c", k=2), 1.0 / 12.0, None, ALU.mult, None, last)
            x = tt(gs[:, 0, :], gs[:, 1, :], gs[:, 1, :], ALU.mult, g)
            x = tt(gs[:, 2, :], gs[:, 2, :], gs[:, 0, :], ALU.subtract, x)
            x = ts(gs[:, 2, :], gs[:, 2, :], GN_EPS, None, ALU.add, None, x)
            r = tt(out[:, 0, :], gs[:, 2, :], mhalf[:, 0:3], ALU.pow, x, eng="pool")
            f = stt(out[:, 1, :], gs[:, 1, :], -1.0, out[:, 0, :], ALU.mult, ALU.mult, r)
            return g, f

        stored = {}

        def layer0(xin_d, xout_d):
            ar = Arena(nc, base, "a")
            WinT = ar("WinT", [128, 3, 1536])
            WxT = ar("WxT", [128, 6, 64])
            WdtT = ar("WdtT", [RK, DI])
            WoT = ar("WoT", [128, 6, C])
            pv = ar("pv", [128, 6, 23])
            pc = ar("pc", [128, 3, 2])
            Aneg = ar("Aneg", [128, 6, NS])
            one1 = ar("one1", [128, 1])
            xs = [ar(f"xs{i}", [128, 3, T]) for i in range(3)]
            xn = ar("xn", [128, 3, T])
            sx = ar("sx", [128, 3, T])
            bn = ar("bn", [128, 3, NQ, 6])
            mv = ar("mv", [128, 3, 2])
            gs = ar("gs", [128, 3, 3])
            sc = [ar(f"sc{i}", [128, 2, 3]) for i in range(2)]
            raw = ar("raw", [128, 6, T + 3])
            V = raw[:, :, 3:T + 3]
            xin = [ar(f"xin{i}", [128, 6, T]) for i in range(3)]
            sz = [ar(f"sz{i}", [128, 6, T]) for i in range(2)]
            dt = [ar(f"dt{i}", [128, 6, T]) for i in range(2)]
            dtxT = [ar(f"dtxT{i}", [128, TB, DI]) for i in range(2)]
            BC = [ar(f"BC{i}", [128, TB, 32]) for i in range(2)]
            dtl = ar("dtl", [64, T])
            dBT = [ar(f"dBT{i}", [128, TB, DI]) for i in range(2)]
            dA = Ring([ar(f"dA{i}", [128, T]) for i in range(8)])
            hb = [ar(f"h{i}", [128, 6, T]) for i in range(2)]
            st = ar("st", [128, 6, NS])
            acc = ar("acc", [128, TB, DI])
            ob = ar("ob", [128, TB, C])
            lbn = ar("lbn", [128, TB, 6])
            lmv = ar("lmv", [128, TB, 2])
            lsc = ar("lsc", [128, TB, 2])
            pp = Ring(bank)
            pb = pp
            ph = Ring(wide)

            w_in = p.dma("WinT", WinT[:], d["WinT"].rearrange("(k p) n -> p k n", p=128))
            w_pv = p.dma("pv", pv[:], d["pv"])
            w_pc = p.dma("pc", pc[:], d["pc"])
            w_x = p.dma("WxT", WxT[:], d["WxT"].rearrange("(k p) n -> p k n", p=128))
            w_dt = p.dma("WdtT", WdtT[:], d["WdtT"])
            w_o = p.dma("WoT", WoT[:], d["WoT"].rearrange("(k p) n -> p k n", p=128))
            one_t = p.op("pool", lambda e: e.memset(one1[:], 1.0))
            p.op("act", lambda e: e.preload_act_table_set("natural_log_exp_and_others"))
            a0 = act(Aneg[:], pv[:, :, 7:23], ACT.Exp, w_pv)
            t_A = ts(Aneg[:], Aneg[:], -1.0, None, ALU.mult, None, a0)
            cw = lambda m, j: pv[:, m, j:j + 1]
            cb = lambda m: pv[:, m, 4:5]
            db = lambda m: pv[:, m, 5:6]
            Dm = lambda m: pv[:, m, 6:7]
            xv = xin_d.rearrange("b (c p) l -> b p c l", p=128)
            xo = xout_d.rearrange("b (c p) l -> b p c l", p=128)

            free = {n: [None, None, None] for n in ("xs", "xin", "sz", "dt", "dtxT", "BC", "dBT", "h", "sc", "tap")}
            free.update({n: None for n in ("sx", "bn", "xn", "raw", "V", "dtl", "ob", "acc")})
            free["xn"] = []
            scale_done, beta_done, ready, acc_done = {}, {}, {}, {}
            halo_done = [None]
            st_done = [None] * NS

            def stats(b):
                t = None
                for q in range(NQ):
                    ld = p.dma("sx", sx[:], xv[b, :, :, q * T:(q + 1) * T], free["sx"])
                    yield 0
                    for c in range(CT):
                        t = p.op("dve", lambda e, c=c, q=q: e.bn_stats(bn[:, c, q, :], sx[:, c, :]), ld, free["bn"])
                        yield 0
                    free["sx"] = t
                i, ps, fr = pp.get()
                g, f = finish_stats(bn, mv, gs, ps, fr, t, sc[b % 2], free["sc"][b % 2])
                pp.put(i, g)
                free["bn"] = f
                scale_done[b] = f
                yield 0

            posted, normed, gate_raw, gated_z = {}, {}, {}, {}

            def project(col, xn_t, xn_read, evac):
                held = x = None
                for m in range(6):
                    if held:
                        pp.put(held[0], evac(*held[1:]))
                    i, ps, fr = pp.get()
                    for kk in range(CT):
                        x = mm(ps[:, 0:T], WinT[:, kk, col + m * 128:col + (m + 1) * 128], xn[:, kk, :], kk == 0, kk == 2, xn_t, fr, w_in)
                        yield MM
                    held = (i, m, ps, x)
                yield 0
                pp.put(held[0], evac(*held[1:]))
                xn_read.append(x)

            def gate_in(k):
                o = k % 2
                zs = gate_raw[k] = []

                def to_sz(m, ps, x):
                    zs.append(copy("act", sz[o][:, m, :], ps[:, 0:T], x, free["sz"][o]))
                    return zs[m]

                while k not in normed or (k >= 2 and not posted.get((k - 2, "sz"))):
                    yield 0
                yield from project(DI, normed[k], free["xn"], to_sz)
                posted[k, "z"] = True

            def silu_gate(k):
                zt = act(sz[k % 2][:], sz[k % 2][:], ACT.Silu, gate_raw[k])
                gated_z[k] = zt

            def pre(k):
                b, q = divmod(k, NQ)
                o, o3 = k % 2, k % 3
                t0 = q * T
                xb = xs[k % 3]
                ld = p.dma(f"xs{k % 3}", xb[:], xv[b, :, :, t0:t0 + T], free["xs"][k % 3])
                yield 0
                while k > 0 and not posted.get((k - 1, "z")):
                    yield 0
                n = []
                for c in range(CT):
                    n.append(ts(xn[:, c, :], xb[:, c, :], sc[b % 2][:, 0, c:c + 1], sc[b % 2][:, 1, c:c + 1],
                                ALU.mult, ALU.add, ld, scale_done[b], free["xn"], eng="pool"))
                free["xn"] = []
                normed[k] = n
                if q == NQ - 1:
                    free["sc"][b % 2] = n
                for c in range(CT):
                    beta_done[k] = act(xb[:, c, :], xb[:, c, :], ACT.Identity, n, w_pc, bias=pc[:, c, 1:2])
                if q == 0:
                    hl = p.op("pool", lambda e: e.memset(raw[:, :, 0:3], 0.0), free["raw"])
                else:
                    hl = halo_done[0]
                yield 0
                rw = [None] * 6

                def to_raw(m, ps, x):
                    rw[m] = copy("act", raw[:, m, 3:T + 3], ps[:, 0:T], x, free["raw"], free["V"], hl)
                    return rw[m]

                prev = [None] * 6

                def conv(m):
                    prev[m] = ts(xin[o3][:, m, :], raw[:, m, 0:T], cw(m, 0), cb(m), ALU.mult, ALU.add,
                                 rw[m], hl, free["xin"][o3], w_pv)
                    for j in range(1, 4):
                        yield
                        prev[m] = stt(xin[o3][:, m, :], raw[:, m, j:j + T], cw(m, j), xin[o3][:, m, :], ALU.mult, ALU.add, prev[m])

                while k >= 3 and not posted.get((k - 3, "xin")):
                    yield 0
                going, cm = [], 0
                pj = project(0, n, free["xn"], to_raw)
                alive = True
                while alive or cm < 6 or going:
                    cost = 0
                    if alive:
                        cost = next(pj, -1)
                        if cost < 0:
                            alive, cost = False, 0
                    while cm < 6 and rw[cm] is not None and len(going) < 2:
                        going.append(conv(cm))
                        cm += 1
                    going = [g for g in going if next(g, 1) != 1]
                    yield cost
                if q < NQ - 1:
                    halo_done[0] = p.op("pool", lambda e: e.tensor_copy(raw[:, :, 0:3], raw[:, :, T:T + 3]), prev)
                    halo = halo_done[0]
                else:
                    halo = prev
                while k > 0 and not posted.get((k - 1, "z")):
                    yield 0
                xt = act(xin[o3][:], xin[o3][:], ACT.Silu, prev)
                if k > 0:
                    silu_gate(k - 1)
                p.op("act", lambda e: e.preload_act_table_set("natural_log_exp_and_others"))
                for _ in range(GAP_SILU):
                    yield 0
                i, ps, fr = pp.get()
                for m in range(6):
                    x = mm(ps[0:64, 0:T], WxT[:, m, :], xin[o3][:, m, :], m == 0, m == 5, xt, fr, w_x)
                    yield MM
                tl = copy("act", dtl[:], ps[0:64, 0:T], x, free["dtl"])
                pp.put(i, tl)
                yield 0
                yield 0
                i, ps, fr = pp.get()
                for tb in range(TB):
                    x = p.op("pe", lambda e, tb=tb, ps=ps: e.transpose(
                        ps[:, tb * 32:tb * 32 + 32], dtl[32:64, tb * 128:(tb + 1) * 128], ident[32:64, 32:64]), tl, fr, t_const)
                tBC = copy("act", BC[o][:], ps[:, 0:96].rearrange("p (a n) -> p a n", n=32), x, free["BC"][o])
                pp.put(i, tBC)
                vs = []
                for m in range(6):
                    i, ps, fr = pp.get()
                    x = mm(ps[:, 0:T], WdtT[:, m * 128:(m + 1) * 128], dtl[0:RK, :], True, True, tl, fr, w_dt)
                    yield MM
                    vs.append(act(V[:, m, :], ps[:, 0:T], ACT.Identity, x, halo, prev, bias=db(m)))
                    pp.put(i, vs[m])
                free["dtl"] = [x, tBC]
                yield 0
                c0 = act(dt[o][:], V, ACT.Abs, vs, free["dt"][o])
                yield 0
                c1 = act(dt[o][:], dt[o][:], ACT.Exp, c0, scale=-1.0)
                yield 0
                c2 = act(dt[o][:], dt[o][:], ACT.Ln, c1, one_t, bias=one1[:, 0:1])
                for _ in range(GAP_LN):
                    yield 0
                tdt, tx, ct = [], [], []
                for m in range(6):
                    tdt.append(stt(dt[o][:, m, :], V[:, m, :], 0.0, dt[o][:, m, :], ALU.max, ALU.add, c2))
                    tx.append(tt(V[:, m, :], dt[o][:, m, :], xin[o3][:, m, :], ALU.mult, tdt[m], xt, eng="pool"))
                    yield 0
                yield 0
                for hf in range(2):
                    for tb in range(TB):
                        i, ps, fr = pp.get()
                        for cc in range(3):
                            x = tr(ps[:, cc * 128:(cc + 1) * 128], V[:, hf * 3 + cc, tb * 128:(tb + 1) * 128], tx[hf * 3 + cc], fr, t_const)
                        yield MM / 2
                        ct.append(copy("act", dtxT[o][:, tb, hf * T:(hf + 1) * T], ps[:, 0:T], x, free["dtxT"][o]))
                        pp.put(i, ct[-1])
                free["V"] = x
                free["raw"] = prev
                ready[k] = dict(xt=xt, BC=tBC, dt=tdt, dtx=ct)

            nk = images * NQ
            exps = {}
            scaled = {}
            LEAD = 6

            def exp_to(n):
                while len(exps) <= min(n, nk * NS * 6 - 1):
                    g = len(exps)
                    k, r = divmod(g, NS * 6)
                    s, c = divmod(r, 6)
                    if k not in ready:
                        return
                    j, da, df = dA.get()
                    e = act(da[:], dt[k % 2][:, c, :], ACT.Exp, ready[k]["dt"][c], df, t_A, scale=Aneg[:, c, s:s + 1])
                    exps[g] = (j, da, e)
                    if r == NS * 6 - 1:
                        free["dt"][k % 2] = e

            def scale_to(n):
                while len(scaled) <= min(n, nk * NS - 1):
                    g = len(scaled)
                    k, s = divmod(g, NS)
                    if k not in ready:
                        return
                    o = k % 2
                    for tb in range(TB):
                        bt = ts(dBT[g % 2][:, tb, :], dtxT[o][:, tb, :], BC[o][:, tb, s:s + 1], 1.0, ALU.mult, ALU.mult,
                                ready[k]["dtx"], ready[k]["BC"], free["dBT"][g % 2], eng="pool")
                    scaled[g] = bt
                    if s == NS - 1:
                        free["dtxT"][o] = bt

            acc_t = [None] * TB

            def contract(k, s, tb, hd):
                o = k % 2
                i, ps, fr = ph.get()
                for c in range(6):
                    x = tr(ps[:, c * 128:(c + 1) * 128], hb[s % 2][:, c, tb * 128:(tb + 1) * 128], hd[c], fr, t_const)
                cs = BC[o][:, tb, 16 + s:17 + s]
                if s == 0:
                    y = ts(acc[:, tb, :], ps[:, 0:DI], cs, None, ALU.mult, None, x, ready[k]["BC"], free["acc"])
                else:
                    y = stt(acc[:, tb, :], ps[:, 0:DI], cs, acc[:, tb, :], ALU.mult, ALU.add, x, acc_t[tb])
                acc_t[tb] = y
                ph.put(i, y)
                if tb == TB - 1:
                    free["h"][s % 2] = [x, st_done[s]]
                return y

            def scan(k):
                b, q = divmod(k, NQ)
                hd = {}
                y = None
                for s in range(NS + 1):
                    if s < NS:
                        scale_to(k * NS + s + 1)
                        hd[s] = []
                    for c in range(6):
                        if s < NS:
                            g = (k * NS + s) * 6 + c
                            exp_to(g + LEAD)
                            j, da, e = exps[g]
                            i, ps, fr = pb.get()
                            src = dBT[(k * NS + s) % 2]
                            for tb in range(TB):
                                x = tr(ps[:, tb * 128:(tb + 1) * 128], src[:, tb, c * 128:(c + 1) * 128], scaled[k * NS + s], fr, t_const)
                            init = 0.0 if q == 0 else st[:, c, s:s + 1]
                            h = p.op("dve", lambda e, c=c, s=s, da=da, ps=ps, init=init: e.tensor_tensor_scan(
                                hb[s % 2][:, c, :], da[:], ps[:, 0:T], init, ALU.mult, ALU.add),
                                x, e, free["h"][s % 2], None if q == 0 else st_done[s])
                            pb.put(i, h)
                            dA.put(j, h)
                            hd[s].append(h)
                            if c == 5:
                                free["dBT"][(k * NS + s) % 2] = x
                        if s > 0 and c == 0:
                            st_done[s - 1] = p.op("pool", lambda e, s=s: e.tensor_copy(st[:, :, s - 1], hb[(s - 1) % 2][:, :, T - 1]), hd[s - 1])
                        if s > 0 and c % 2 == 1:
                            y = contract(k, s - 1, c // 2, hd[s - 1])
                        if s < NS or c % 2 == 1:
                            yield
                free["BC"][k % 2] = [y, scaled[k * NS + NS - 1]]
                acc_done[k] = y

            def post(k):
                b, q = divmod(k, NQ)
                o, o3 = k % 2, k % 3
                t0 = q * T
                xb = xs[k % 3]
                R = ready[k]
                yt = []
                for c in range(6):
                    i, ps, fr = pp.get()
                    for tb in range(TB):
                        x = tr(ps[:, tb * 128:(tb + 1) * 128], acc[:, tb, c * 128:(c + 1) * 128], acc_done[k], fr)
                    yield MM / 2
                    y = stt(xin[o3][:, c, :], xin[o3][:, c, :], Dm(c), ps[:, 0:T], ALU.mult, ALU.add, x, R["xt"])
                    pp.put(i, y)
                    yt.append(tt(xin[o3][:, c, :], xin[o3][:, c, :], sz[o][:, c, :], ALU.mult, y, gated_z[k], eng="pool"))
                free["acc"] = x
                free["sz"][o] = yt
                posted[k, "sz"] = True
                yield 0
                obs = [None] * TB

                def norm(tb, i, ps, x):
                    s0 = copy("act", ob[:, tb, :], ps[:, 0:C], x, free["ob"])
                    pp.put(i, s0)
                    yield
                    s1 = p.op("dve", lambda e: e.bn_stats(lbn[:, tb, :], ob[:, tb, :]), s0)
                    s2 = p.op("dve", lambda e: e.bn_aggr(lmv[:, tb, :], lbn[:, tb, :]), s1)
                    s3 = ts(lmv[:, tb, 1:2], lmv[:, tb, 1:2], LN_EPS, None, ALU.add, None, s2)
                    s4 = tt(lsc[:, tb, 0:1], lmv[:, tb, 1:2], mhalf[:, 0:1], ALU.pow, s3, eng="pool")
                    yield
                    yield
                    s5 = stt(lsc[:, tb, 1:2], lmv[:, tb, 0:1], -1.0, lsc[:, tb, 0:1], ALU.mult, ALU.mult, s4)
                    yield
                    obs[tb] = act(ob[:, tb, :], ob[:, tb, :], ACT.Identity, s5, scale=lsc[:, tb, 0:1], bias=lsc[:, tb, 1:2])

                nr = None
                for tb in range(TB):
                    i, ps, fr = pp.get()
                    for m in range(6):
                        x = mm(ps[:, 0:C], xin[o3][:, m, tb * 128:(tb + 1) * 128], WoT[:, m, :], m == 0, m == 5, yt[m], fr, w_o)
                        yield MM
                        if nr is not None and next(nr, 1) == 1:
                            nr = None
                    nr = norm(tb, i, ps, x)
                free["xin"][o3] = x
                posted[k, "xin"] = True
                yield 0
                for _ in nr:
                    yield 0
                yield 0
                for c in range(3):
                    i, ps, fr = pp.get()
                    for tb in range(TB):
                        x = tr(ps[:, tb * 128:(tb + 1) * 128], ob[:, tb, c * 128:(c + 1) * 128], obs, fr)
                    yield MM / 2
                    y = stt(xb[:, c, :], ps[:, 0:T], pc[:, c, 0:1], xb[:, c, :], ALU.mult, ALU.add, x, beta_done[k])
                    pp.put(i, y)
                free["ob"] = x
                w = p.dma(f"x1o{k % 3}", xo[b, :, :, t0:t0 + T], xb[:], y)
                free["xs"][k % 3] = w
                stored.setdefault(("x1", b), []).append(w)

            for _ in stats(0):
                pass
            for _ in pre(0):
                pass

            def run_all(threads):
                while threads:
                    threads = [t for t in threads if next(t, None) is not None]

            for k in range(nk):
                first = post(k - 1) if k > 0 else None
                main = pre(k + 1) if k + 1 < nk else None
                rest = [gate_in(0)] if k == 0 else []
                if k > 0:
                    rest.append(first)
                if k + 1 < nk:
                    rest.append(gate_in(k + 1))
                st_ = stats(k // NQ + 1) if k % NQ == 2 and k // NQ + 1 < images else None
                credit, n = 0.0, 0
                for _ in scan(k):
                    credit = min(credit + RATE, MM)
                    if n < 7 and first is not None:
                        credit -= next(first)
                    if main is not None and credit > 0:
                        c = next(main, None)
                        if c is None:
                            main = None
                        else:
                            credit -= c
                    if n >= 7:
                        while rest and credit > 0:
                            c = next(rest[0], None)
                            if c is None:
                                rest.pop(0)
                            else:
                                credit -= c
                                if c == 0:
                                    break
                    if st_ is not None and n % 2:
                        next(st_, None)
                    n += 1
                if LOG:
                    print("chunk", k, "steps", n, "left", main is not None, len(rest))
                run_all([t for t in [main, st_] + rest if t is not None])
            silu_gate(nk - 1)
            for _ in post(nk - 1):
                pass

        def fence():
            return p.last() + [t for v in stored.values() for t in v]

        def split(hi, lo, src, *waits):
            a = copy("act", hi, src, *waits)
            return a, tt(lo, src, hi.bitcast(F32), ALU.subtract, a, *waits)

        def layer12(x1_d, x3_d):
            fe = fence()
            ar = Arena(nc, late.at, "b")
            x = [ar(f"x{i}", [128, 3, L]) for i in range(2)]
            timg = [ar(f"ti{i}", [128, 50, 50]) for i in range(3)]
            cv = [ar(f"cv{i}", [128, 3, 2 * T]) for i in range(2)]
            tT = Ring([ar(f"tT{i}", [128, C]) for i in range(2)])
            tf = Ring([ar(f"tf{i}", [128, C]) for i in range(2)])
            Win1 = ar("Win1", [128, 3, C])
            Fwd = ar("Fwd", [128, 128])
            Inv = ar("Inv", [128, 128])
            feff = ar("feff", [128, C])
            WoA = ar("WoA", [128, C])
            WoC = ar("WoC", [128, C])
            dw = ar("dw", [128, 3, 9])
            wn = ar("wn", [128, 3, 4])
            gw = ar("gw", [128, 3, 4])
            gws = ar("gws", [128, 3, 4])
            gb = ar("gb", [1, 4])
            gbs = ar("gbs", [1, 4])
            row = ar("row", [1, 12])
            par = ar("par", [128, 12])
            Th = ar("Th", [128, 4, 18, 28], F32R)
            Tl = ar("Tl", [128, 4, 18, 28], F32R)
            xn = Ring([ar(f"xn{i}", [128, 3, T]) for i in range(3)])
            sm = [dict(bn=ar(f"bn{i}", [128, 3, NQ, 6]), mv=ar(f"mv{i}", [128, 3, 2]), gs=ar(f"gs{i}", [128, 3, 3]),
                       sc=ar(f"sc{i}", [128, 2, 3])) for i in range(2)]
            bn3 = ar("bn3", [128, 3, len(BANDS), 6])
            mv3 = ar("mv3", [128, 3, 2])
            gs3 = ar("gs3", [128, 3, 3])
            u0 = ar.at
            xTh = ar("xTh", [128, NT, C], F32R)
            xTl = ar("xTl", [128, NT, C], F32R)
            ar.at = u0
            G0 = ar("G0", [128, 504])
            G1 = ar("G1", [128, 504])
            GM = ar("GM", [128, 504])
            gt = ar("gt", [128, 504])
            gu = ar("gu", [128, 504])
            S40 = ar("S40", [40, 128])
            f40 = ar("f40", [40, C])
            banks = Ring(bank + [wide[0][:, 0:512], wide[0][:, 512:1024], wide[1][:, 0:512], wide[1][:, 512:1024]])
            xv = x1_d.rearrange("b (c p) l -> b p c l", p=128)
            xo = x3_d.rearrange("b (c p) l -> b p c l", p=128)
            rows = lambda r: slice(T * r, T * r + T)

            def load(b, *waits):
                return [p.dma(f"x1i{b % 2}{r}", x[b % 2][:, :, rows(r)], xv[b, :, :, rows(r)], waits, stored.get(("x1", b), []))
                        for r in range(NQ)]

            ld = {0: load(0, fe)}
            w = [p.dma(n, t[:], src, fe) for n, t, src in (
                ("Win1", Win1, d["Win1T"].rearrange("(k p) n -> p k n", p=128)), ("Fwd", Fwd, d["Fwd"]), ("Inv", Inv, d["Inv"]),
                ("S40", S40, d["S40"]), ("f40", f40, d["f40"]), ("WoA", WoA, d["Wo1T"][0:128, :]),
                ("dw", dw, d["dw"]), ("wn", wn, d["wn"]), ("gw", gw, d["gw"].rearrange("(k p) n -> p k n", p=128)),
                ("gb", gb, d["gb"]), ("row", row, d["row"]), ("G0", G0, d["G0"]), ("G1", G1, d["G1"]), ("GM", GM, d["GM"]))]
            w.append(p.dma("WoC", WoC[64:128, :], d["Wo1T"][128:192, :], fe))
            if images > 1:
                ld[1] = load(1, fe)
            zero = [p.op("pool", lambda e, i=i: e.memset(timg[i][:], 0.0), fe) for i in range(3)]

            i, ps, fr = banks.get()
            a = mm(ps[:, 0:C], S40[:], f40[:], True, True, w, fr, t_const, fe)
            t_feff = copy("act", feff[:], ps[:, 0:C], a)
            banks.put(i, t_feff)
            i, ps, fr = banks.get()
            a = mm(ps[:, 0:12], ones[0:1, :], row[:], True, True, w, fr, t_const)
            b_ = copy("dve", par[:], ps[:, 0:12], a)
            banks.put(i, b_)
            r_ = p.op("dve", lambda e: e.reciprocal(par[:, 8:12], par[:, 8:12]), b_)
            r_ = ts(par[:], par[:], -1.0, None, ALU.mult, None, r_)
            t_T = None
            flat_ = lambda t, n: t[:, n].rearrange("p h w -> p (h w)")
            for n in range(4):
                a0 = act(gt[:], G0[:], ACT.Abs, r_, t_T, bias=par[:, 2 * n:2 * n + 1])
                a1 = act(gu[:], G1[:], ACT.Abs, r_, t_T, bias=par[:, 2 * n + 1:2 * n + 2])
                a2 = tt(gt[:], gt[:], gu[:], ALU.add, a0, a1)
                a3 = ts(gt[:], gt[:], par[:, 8 + n:9 + n], 1.0, ALU.mult, ALU.add, a2)
                a4 = stt(gt[:], gt[:], 0.0, GM[:], ALU.max, ALU.mult, a3)
                t_T = split(flat_(Th, n), flat_(Tl, n), gt[:], a4)
            t_T = list(t_T)

            def patches(t, r):
                return t[:, rows(r)].rearrange("p (h j w) -> p j h w", j=3, w=16)

            def normalize(xt, r, sc, ready):
                i, n, fr = xn.get()
                t = []
                for c in range(CT):
                    t.append(ts(n[:, c, :].rearrange("p (j h w) -> p j h w", j=3, w=16), patches(xt[:, c, :], r),
                                sc[:, 0, c:c + 1], sc[:, 1, c:c + 1], ALU.mult, ALU.add, ready, fr, fe, eng="pool"))
                return i, n, t

            conv_q = []
            mixed, sc_free = {}, [None, None]

            def mix(b):
                xt, S = x[b % 2], sm[0]
                for r in range(NQ):
                    for c in range(CT):
                        t = p.op("dve", lambda e, c=c, r=r: e.bn_stats(S["bn"][:, c, r, :], xt[:, c, rows(r)]), ld[b][r], fe)
                    yield 0
                i, ps, fr = banks.get()
                g, f = finish_stats(S["bn"], S["mv"], S["gs"], ps, fr, t, S["sc"], sc_free[0])
                banks.put(i, g)
                yield 0
                img = [[None] * 6 for _ in range(3)]
                conv_t, out_t = {}, {}

                def conv(g):
                    while g == 2 and 0 not in out_t:
                        yield
                    need = [img[o][r] for o in range(3) for r in range(min(6, 2 * g + 3))]
                    prev = [None] * 3
                    for k in range(9):
                        dy, dx = divmod(k, 3)
                        for o in range(3):
                            src = timg[o][:, 16 * g + dy:16 * g + dy + 16, dx:dx + W]
                            dst = cv[g % 2][:, o, :].rearrange("p (h w) -> p h w", w=W)
                            if k == 0:
                                prev[o] = ts(dst, src, dw[:, o, 0:1], None, ALU.mult, None, need, cv_free[g % 2])
                            else:
                                prev[o] = stt(dst, src, dw[:, o, k:k + 1], dst, ALU.mult, ALU.add, prev[o])
                            yield
                    conv_t[g] = prev
                    if g == 2:
                        timg_free[:] = prev

                st1, st2, ob, nx = {}, {}, {}, None
                for n in range(NT + 2):
                    if n < NT:
                        r, j = divmod(n, 3)
                        if j == 0:
                            nx = normalize(xt, r, S["sc"], f)
                        i, ps, fr = banks.get()
                        for kk in range(CT):
                            a = mm(ps[:, 0:C], nx[1][:, kk, j * 128:(j + 1) * 128], Win1[:, kk, :], kk == 0, kk == 2, nx[2], fr, w)
                        if j == 2:
                            xn.put(nx[0], a)
                            sc_free[0] = nx[2]
                        ti, tb_, tfr = tT.get()
                        c_ = copy("act", tb_[:], ps[:, 0:C], a, tfr, fe)
                        banks.put(i, c_)
                        st1[n] = (ti, tb_, c_)
                        yield 3 * MM
                    if 1 <= n <= NT:
                        ti, tb_, c_ = st1[n - 1]
                        i, ps, fr = banks.get()
                        a = mm(ps[:, 0:C], Fwd[:], tb_[:], True, True, c_, fr)
                        tT.put(ti, a)
                        fi, fb, ffr = tf.get()
                        c_ = tt(fb[:], ps[:, 0:C], feff[:], ALU.mult, a, ffr, t_feff, fe)
                        banks.put(i, c_)
                        st2[n - 1] = (fi, fb, c_)
                        yield MM
                    if n >= 2:
                        r, j = divmod(n - 2, 3)
                        fi, fb, c_ = st2[n - 2]
                        if j == 0:
                            ob = {o: banks.get() for o in range(3)}
                        for o in range(3):
                            i, ps, fr = ob[o]
                            a = mm(ps[:, 0:T].rearrange("p (h w) -> p h w", w=W)[:, :, 16 * j:16 * j + 16], fb[:, o * 128:(o + 1) * 128],
                                   Inv[:].rearrange("p (h w) -> p h w", w=16), True, True, c_, fr, skip=True)
                            if j == 2:
                                img[o][r] = copy("act", timg[o][:, 8 * r + 1:8 * r + 9, 1:1 + W],
                                                 ps[:, 0:T].rearrange("p (h w) -> p h w", w=W), a, zero, timg_free)
                                banks.put(i, img[o][r])
                        tf.put(fi, a)
                        if j == 2 and r in (2, 4, 5):
                            conv_q.append(conv(max(0, r // 2 - 1) if r < 5 else 2))
                        yield MM
                res = []
                for g in range(3):
                    while g not in conv_t:
                        yield 0
                    v = cv[g % 2]
                    a = act(v[:, 0, :], v[:, 0, :], ACT.Gelu, conv_t[g])
                    a = tt(v[:, 0, :], v[:, 0, :], v[:, 1, :], ALU.mult, a, eng="pool")
                    c_ = act(v[64:128, 1, :], v[0:64, 2, :], ACT.Gelu, conv_t[g], a)
                    c_ = tt(v[64:128, 1, :], v[64:128, 1, :], v[64:128, 2, :], ALU.mult, c_)
                    yield REST
                    for hf in range(2):
                        r = 2 * g + hf
                        s2 = slice(T * hf, T * hf + T)
                        for o in range(3):
                            i, ps, fr = banks.get()
                            m = mm(ps[:, 0:T], WoA[:, o * 128:(o + 1) * 128], v[:, 0, s2], True, False, a, fr, w)
                            m = mm(ps[:, 0:T], WoC[64:128, o * 128:(o + 1) * 128], v[64:128, 1, s2], False, True, c_)
                            y = tt(xt[:, o, rows(r)], xt[:, o, rows(r)], ps[:, 0:T], ALU.add, m)
                            banks.put(i, y)
                            res.append(y)
                            yield 2 * MM
                            bt = p.op("dve", lambda e, o=o, r=r: e.bn_stats(sm[1]["bn"][:, o, r, :], xt[:, o, rows(r)]), y)
                    cv_free[g % 2] = m
                    out_t[g] = m
                    mixed_t[b] = bt

            cv_free, timg_free, mixed_t = [fe, fe], [None], {}
            xT_free, gated = [[t_T, t_feff] for _ in range(NQ)], []

            heads = {}

            def sparse_head(b):
                xt, S = x[b % 2], sm[1]
                i, ps, fr = banks.get()
                g, f = finish_stats(S["bn"], S["mv"], S["gs"], ps, fr, mixed_t[b], S["sc"], sc_free[1])
                banks.put(i, g)
                yield 0
                hl = {}

                def pixels(r):
                    ni, n, t = normalize(xt, r, S["sc"], f)
                    for j in range(3):
                        i, ps, fr = banks.get()
                        for c in range(CT):
                            a = tr(ps[:, c * 128:(c + 1) * 128], n[:, c, j * 128:(j + 1) * 128], t, fr, t_const)
                        h = copy("act", xTh[:, 3 * r + j, :], ps[:, 0:C], a, xT_free[r])
                        l_ = tt(xTl[:, 3 * r + j, :], ps[:, 0:C], xTh[:, 3 * r + j, :].bitcast(F32), ALU.subtract, h)
                        banks.put(i, l_)
                        hl[r, j] = [h, l_]
                        yield MM / 2
                    xn.put(ni, a)
                    sc_free[1] = t

                yield from pixels(0)
                yield from pixels(1)
                heads[b] = (hl, pixels)

            def sparse(b):
                xt, S = x[b % 2], sm[1]
                hl, pixels = heads[b]
                st_w, up = [], 2
                for r, (b0, b1) in enumerate(BANDS):
                    px, h = slice(W * b0, W * b1), b1 - b0
                    near = [(q, max(b0, 8 * q - 5), min(b1, 8 * q + 13)) for q in range(NQ)]
                    near = [v for v in near if v[1] < v[2]]
                    while up <= near[-1][0]:
                        yield from pixels(up)
                        up += 1
                    for c in range(CT):
                        for e0 in (0, 24):
                            use = []
                            for q, y0, y1 in near:
                                for j in range(3):
                                    x0, x1 = max(e0, 16 * j - 6), min(e0 + 24, 16 * j + 22)
                                    if x0 < x1:
                                        use.append((q, j, y0, y1, x0, x1, y0 - 8 * q + 5, x0 - 16 * j + 6))
                            xb = xt[:, c, px].rearrange("p (h w) -> p h w", w=W)[:, :, e0:e0 + 24]
                            prev = None
                            for n in (0, 2):
                                i, ps, fr = banks.get()
                                po = ps[:, 0:48 * h].rearrange("p (n h w) -> p n h w", n=2, w=24)
                                k = 0
                                for q, j, y0, y1, x0, x1, u, v in use:
                                    for A, B in ((xTh, Th), (xTl, Th), (xTh, Tl)):
                                        a = mm(po[:, :, y0 - b0:y1 - b0, x0 - e0:x1 - e0], A[:, 3 * q + j, c * 128:(c + 1) * 128],
                                               B[:, n:n + 2, u:u + y1 - y0, v:v + x1 - x0], k == 0, k == 3 * len(use) - 1, hl[q, j], fr, t_T, skip=True)
                                        k += 1
                                    yield 3 * max(256, 2 * (y1 - y0) * (x1 - x0)) / 2400
                                for m in range(2):
                                    prev = stt(xb, po[:, m], wn[:, c, n + m:n + m + 1], xb, ALU.mult, ALU.add, a, prev)
                                banks.put(i, prev)
                        bt = p.op("dve", lambda e, c=c, r=r, px=px: e.bn_stats(bn3[:, c, r, :], xt[:, c, px]), prev)
                    for q, _, _ in near:
                        xT_free[q] = a
                    st_w.append(p.dma(f"x3o{b % 2}{r}", xo[b, :, :, px], xt[:, :, px], prev))
                stored[("x3", b)] = st_w
                i, ps, fr = banks.get()
                g, f = finish_stats(bn3, mv3, gs3, ps, fr, bt, gst[:, b], fe)
                banks.put(i, g)
                yield 0
                i, ps, fr = banks.get()
                gt_ = []
                for kk in range(CT):
                    gt_.append(ts(gws[:, kk, :], gw[:, kk, :], gst[:, b, 0, kk:kk + 1], None, ALU.mult, None, f, gated, w))
                    a = mm(ps[0:1, 0:4], gst[:, b, 1, kk:kk + 1], gw[:, kk, :], kk == 0, kk == 2, f, fr)
                gs_ = tt(gbs[:], ps[0:1, 0:4], gb[:], ALU.add, a, gated, w)
                banks.put(i, gs_)
                yield 0
                i, ps, fr = banks.get()
                for j in range(NT):
                    for kk in range(CT):
                        mm(ps[:, 4 * j:4 * j + 4], xt[:, kk, j * 128:(j + 1) * 128], gws[:, kk, :], kk == 0, False, gt_, fr)
                    a = mm(ps[:, 4 * j:4 * j + 4], ones[0:1, :], gbs[:], False, True, gs_)
                    if j % 6 == 5:
                        yield MM
                g = copy("act", coef[:, b * NT:(b + 1) * NT, :], ps[:, 0:4 * NT].rearrange("p (j e) -> p j e", e=4), a, fe)
                banks.put(i, g)
                gated.append(g)
                if b + 2 < images:
                    ld[b + 2] = load(b + 2, st_w, a)

            def step_conv(k):
                for _ in range(k):
                    while conv_q and next(conv_q[0], 1) == 1:
                        conv_q.pop(0)

            def drain_mix(m):
                for _ in m:
                    step_conv(2)

            drain_mix(mix(0))
            for _ in sparse_head(0):
                pass
            for b in range(images):
                m = mix(b + 1) if b + 1 < images else None
                head = None
                sp, mp, cc = 0.0, 0.0, 0.0
                for c in sparse(b):
                    sp += c / S_COST
                    while m is not None and (b == 0 or (b + 1) in ld) and mp < (sp / M_A * 0.62 if sp < M_A else 0.62 + (sp - M_A) / (M_B - M_A) * 0.38):
                        c = next(m, None)
                        if c is None:
                            m, head = None, sparse_head(b + 1)
                        else:
                            mp += max(c, 0.05) / M_COST
                    if head is not None and sp > HEAD_FROM:
                        next(head, None)
                    cc += CONV_RATE
                    while cc >= 1:
                        step_conv(1)
                        cc -= 1
                if LOG:
                    print("image", b, "sparse", sp, "mix", mp, m is None)
                if m is not None:
                    drain_mix(m)
                    head = sparse_head(b + 1)
                if head is not None:
                    for _ in head:
                        pass
            return gated

        def layer3(x3_d, out_d, gated):
            fe = fence()
            ar = Arena(nc, late.at, "c")
            W1h = ar("W1h", [128, 3, 4 * C], F32R)
            W1l = ar("W1l", [128, 3, 4 * C], F32R)
            W2h = ar("W2h", [128, 3, 4 * C], F32R)
            W2l = ar("W2l", [128, 3, 4 * C], F32R)
            b1 = ar("b1", [128, 3, 4])
            b2 = ar("b2", [4, C])
            xs = [ar(f"xs{i}", [128, 3, T]) for i in range(3)]
            xn = ar("xn", [128, 3, T])
            xh = [ar(f"xh{i}", [128, 3, T], F32R) for i in range(2)]
            xl = [ar(f"xl{i}", [128, 3, T], F32R) for i in range(2)]
            hf = Ring([ar(f"hf{i}", [128, T]) for i in range(3)])
            hh = Ring([ar(f"hh{i}", [128, 3, T], F32R) for i in range(2)])
            hl = Ring([ar(f"hl{i}", [128, 3, T], F32R) for i in range(2)])
            acc = [ar(f"acc{i}", [128, TB, C]) for i in range(2)]
            cT = [ar(f"cT{i}", [4, T]) for i in range(2)]
            mx = ar("mx", [128, NB * NT])
            v1 = ar("v1", [128, NB * NT])
            cum = ar("cum", [128, NB * NT])
            eq = ar("eq", [128, NB * NT])
            wk = ar("wk", [128, 2, NB * NT])
            fk = ar("fk", [128, 2, 4, NB * NT])
            fl = ar("fl", [128, 8])
            fb = ar("fb", [128, 8])
            banks = Ring(bank + [wide[0][:, 0:512], wide[0][:, 512:1024], wide[1][:, 0:512], wide[1][:, 512:1024]])
            xv = x3_d.rearrange("b (c p) l -> b p c l", p=128)
            ov = out_d.rearrange("b (c p) l -> b p c l", p=128)
            u0 = ar.at
            Wt = [ar(f"Wt{i}", [128, 3, 4 * C]) for i in range(2)]
            l1 = p.dma("W1", Wt[0][:], d["W1T"].rearrange("(k p) n -> p k n", p=128), fe)
            l2 = p.dma("W2", Wt[1][:], d["W2T"].rearrange("(k p) n -> p k n", p=128), fe)
            lb = [p.dma("b1", b1[:], d["b1"], fe), p.dma("b2", b2[:], d["b2"], fe)]
            w1 = list(split(W1h[:], W1l[:], Wt[0][:], l1))
            w2 = list(split(W2h[:], W2l[:], Wt[1][:], l2))

            M = images * NT
            sc = lambda e: coef[:, 0:M, e]
            X = lambda t: t[:, 0:M]
            t = tt(X(mx), sc(0), sc(1), ALU.max, gated, fe)
            t = tt(X(mx), X(mx), sc(2), ALU.max, t)
            t = tt(X(mx), X(mx), sc(3), ALU.max, t)
            a = [tt(sc(e), sc(e), X(mx), ALU.subtract, t) for e in range(4)]
            a = act(coef[:, 0:M, :], coef[:, 0:M, :], ACT.Exp, a)
            t = tt(X(v1), sc(0), sc(1), ALU.add, a)
            t = tt(X(v1), X(v1), sc(2), ALU.add, t)
            t = tt(X(v1), X(v1), sc(3), ALU.add, t)
            t = p.op("dve", lambda e: e.reciprocal(X(v1), X(v1)), t)
            a = [tt(sc(e), sc(e), X(v1), ALU.mult, t) for e in range(4)]
            for k in range(2):
                top = wk[:, k, 0:M]
                t = tt(top, sc(0), sc(1), ALU.max, a)
                t = tt(top, top, sc(2), ALU.max, t)
                t = tt(top, top, sc(3), ALU.max, t)
                z = None
                for e in range(4):
                    f = fk[:, k, e, 0:M]
                    q = tt(X(eq), sc(e), top, ALU.is_equal, t, z)
                    if e == 0:
                        z = copy("dve", f, X(eq), q)
                        z = copy("dve", X(cum), X(eq), z)
                    else:
                        z = tt(f, X(eq), X(cum), ALU.is_gt, q)
                        z = tt(X(cum), X(cum), X(eq), ALU.max, z)
                if k == 0:
                    a = [stt(sc(e), fk[:, k, e, 0:M], -2.0, sc(e), ALU.mult, ALU.add, z) for e in range(4)]
                z = p.op("dve", lambda e, k=k: e.tensor_reduce(fl[:, 4 * k:4 * k + 4], fk[:, k, :, 0:M], mybir.AxisListType.X, ALU.max), z)
            t = tt(X(eq), wk[:, 1, 0:M], wk[:, 0, 0:M], ALU.subtract, z)
            t = act(X(eq), X(eq), ACT.Exp, t)
            t = ts(X(cum), X(eq), 1.0, None, ALU.add, None, t)
            r0 = p.op("dve", lambda e: e.reciprocal(wk[:, 0, 0:M], X(cum)), t)
            r1 = tt(wk[:, 1, 0:M], X(eq), wk[:, 0, 0:M], ALU.mult, r0)
            i, ps, fr = banks.get()
            m = mm(ps[:, 0:8], ones[:], fl[:], True, True, z, fr)
            g = ts(fb[:], ps[:, 0:8], 0.0, None, ALU.is_gt, None, m, fe)
            banks.put(i, g)
            tc_ = []
            for e in range(4):
                q = ts(sc(e), wk[:, 0, 0:M], fb[:, e:e + 1], None, ALU.mult, None, g, r1)
                tc_.append(stt(sc(e), wk[:, 1, 0:M], fb[:, 4 + e:5 + e], sc(e), ALU.mult, ALU.add, q))

            xs_free, xh_free, acc_free, cT_free, xn_free = [fe] * 3, [fe] * 2, [fe] * 2, [fe] * 2, fe
            nk = images * NQ
            pre_t = {}

            def pre(k):
                b, q = divmod(k, NQ)
                o = k % 2
                nonlocal xn_free
                ld = p.dma(f"x3i{k % 3}", xs[k % 3][:], xv[b, :, :, q * T:(q + 1) * T], xs_free[k % 3], stored.get(("x3", b), []))
                for c in range(CT):
                    n = ts(xn[:, c, :], xs[k % 3][:, c, :], gst[:, b, 0, c:c + 1], gst[:, b, 1, c:c + 1], ALU.mult, ALU.add, ld, xn_free)
                s = split(xh[o][:], xl[o][:], xn[:], n, xh_free[o])
                xn_free = list(s)
                i, ps, fr = banks.get()
                for tb in range(TB):
                    a = tr(ps[0:4, tb * 128:(tb + 1) * 128], coef[:, k * TB + tb, :], tc_, fr)
                c_ = copy("act", cT[o][:], ps[0:4, 0:T], a, cT_free[o])
                banks.put(i, c_)
                pre_t[k] = (list(s), ld, c_)

            def hidden(k, e):
                o = k % 2
                s = pre_t[k][0]
                ih, H, fh = hh.get()
                il, Lw, fl_ = hl.get()
                done = []
                for m in range(3):
                    i, ps, fr = banks.get()
                    q = [(kk, A, B) for kk in range(CT) for A, B in ((W1h, xh[o]), (W1l, xh[o]), (W1h, xl[o]))]
                    for u, (kk, A, B) in enumerate(q):
                        a = mm(ps[:, 0:T], A[:, kk, e * C + m * 128:e * C + (m + 1) * 128], B[:, kk, :], u == 0, u == len(q) - 1, s, fr, w1)
                    j, f, ff = hf.get()
                    r = act(f[:], ps[:, 0:T], ACT.Relu, a, ff, lb, fe, bias=b1[:, m, e:e + 1])
                    banks.put(i, r)
                    c1 = copy("act", H[:, m, :], f[:], r, fh, fe)
                    c2 = tt(Lw[:, m, :], f[:], H[:, m, :].bitcast(F32), ALU.subtract, c1, fl_)
                    hf.put(j, c2)
                    done.append([c1, c2])
                xh_free[o] = a
                return ih, H, il, Lw, done

            acc_t = {}

            def combine(k, e, hd):
                o = k % 2
                ih, H, il, Lw, done = hd
                for tb in range(TB):
                    i, ps, fr = banks.get()
                    q = [(m, A, B) for m in range(3) for A, B in ((H, W2h), (Lw, W2h), (H, W2l))]
                    for u, (m, A, B) in enumerate(q):
                        a = mm(ps[:, 0:C], A[:, m, tb * 128:(tb + 1) * 128], B[:, m, e * C:(e + 1) * C], u == 0, u == len(q) - 1, done[m], fr, w2)
                    cf = coef[:, k * TB + tb, e:e + 1]
                    if e == 0:
                        y = ts(acc[o][:, tb, :], ps[:, 0:C], cf, None, ALU.mult, None, a, acc_free[o], tc_)
                    else:
                        y = stt(acc[o][:, tb, :], ps[:, 0:C], cf, acc[o][:, tb, :], ALU.mult, ALU.add, a, acc_t[k, tb])
                    acc_t[k, tb] = y
                    banks.put(i, y)
                hh.put(ih, a)
                hl.put(il, a)

            def finish(k):
                b, q = divmod(k, NQ)
                o = k % 2
                for c in range(CT):
                    i, ps, fr = banks.get()
                    for tb in range(TB):
                        p.op("pe", lambda e, tb=tb, c=c, ps=ps: e.matmul(
                            ps[:, tb * 128:(tb + 1) * 128], acc[o][:, tb, c * 128:(c + 1) * 128], ident[:],
                            start=tb == 0, stop=False, is_transpose=True, skip_group_check=True), acc_t[k, tb], fr)
                    a = mm(ps[:, 0:T], b2[:, c * 128:(c + 1) * 128], cT[o][:], False, True, pre_t[k][2], lb, skip=True)
                    y = tt(xs[k % 3][:, c, :], xs[k % 3][:, c, :], ps[:, 0:T], ALU.add, a)
                    banks.put(i, y)
                acc_free[o] = a
                cT_free[o] = a
                w = p.dma(f"oo{k % 3}", ov[b, :, :, q * T:(q + 1) * T], xs[k % 3][:], y)
                xs_free[k % 3] = w
                stored[("out", k)] = [w]

            pre(0)
            queue = [(k, e) for k in range(nk) for e in range(4)]
            hd = hidden(0, 0)
            for n, (k, e) in enumerate(queue):
                nxt = None
                if n + 1 < len(queue):
                    if e == 2 and k + 1 < nk:
                        pre(k + 1)
                    nxt = hidden(*queue[n + 1])
                combine(k, e, hd)
                if e == 0 and k > 0:
                    finish(k - 1)
                hd = nxt
            finish(nk - 1)

        if 0 in layers:
            layer0(d["x"], d["x1"])
        gated = []
        if 1 in layers:
            gated = layer12(d["x1"], d["x3"])
        if 3 in layers:
            layer3(d["x3"], d["out"], gated)
        p.op("sp", lambda e: e.nop(), *[t for v in stored.values() for t in v])
        block = ctx.enter_context(nc.Block())
        p.emit(block)


def constants():
    a = {}
    dofs = []
    for ky in range(8):
        for kx in range(5):
            if kx in (0, 4):
                if ky in (0, 4):
                    dofs.append((ky, kx, 0, 1.0))
                elif ky < 4:
                    dofs += [(ky, kx, 0, 2.0), (ky, kx, 1, 2.0)]
            else:
                dofs += [(ky, kx, 0, 2.0), (ky, kx, 1, 2.0)]
    assert len(dofs) == 64
    yy, xx = np.meshgrid(np.arange(8), np.arange(8), indexing="ij")
    fwd, inv, sel = np.zeros((128, 128)), np.zeros((128, 128)), np.zeros((40, 128))
    for i, (ky, kx, odd, m) in enumerate(dofs):
        ang = 2 * np.pi * ((ky * yy + kx * xx) % 8) / 8
        v = np.sin(ang) if odd else np.cos(ang)
        for h in range(2):
            tok = (yy * 16 + 8 * h + xx).ravel()
            fwd[tok, 64 * h + i] = v.ravel()
            inv[64 * h + i, tok] = m / 64 * v.ravel()
            if kx in (0, 4):
                sel[ky * 5 + kx, 64 * h + i] += 0.5
                sel[(-ky) % 8 * 5 + kx, 64 * h + i] += 0.5
            else:
                sel[ky * 5 + kx, 64 * h + i] = 1.0
    a["Fwd"], a["Inv"], a["S40"] = (v.astype(np.float32) for v in (fwd, inv, sel))
    lin = np.linspace(-1.0, 1.0, K11, dtype=np.float32)
    i = np.arange(128)[:, None, None]
    dy = np.arange(18)[None, :, None] - 5 - i // 16
    dx = np.arange(28)[None, None, :] - 6 - i % 16
    ok = (abs(dy) <= 5) & (abs(dx) <= 5)
    G0 = np.where(ok, lin[np.clip(5 - dx, 0, 10)], 0)
    G1 = np.where(ok, lin[np.clip(5 + dy, 0, 10)], 0)
    for n, v in (("G0", G0), ("G1", G1), ("GM", ok)):
        a[n] = np.ascontiguousarray(v.astype(np.float32).reshape(128, 504))
    return a


def lay(inputs):
    f = {k: np.asarray(v) for k, v in inputs.items()}
    a = {}
    a["x"] = np.ascontiguousarray(f["x"].reshape(NB, C, L))
    a["WinT"] = np.ascontiguousarray(f["L0_conv_in_proj_w"].T)
    wx = f["L0_conv_x_proj_w"].T
    a["WxT"] = np.concatenate([wx[:, :RK], np.zeros((DI, 32 - RK), np.float32), wx[:, RK:]], axis=1)
    a["WdtT"] = np.ascontiguousarray(f["L0_conv_dt_proj_w"].T)
    a["WoT"] = np.ascontiguousarray(f["L0_conv_out_proj_w"].T)
    pv = np.concatenate([f["L0_conv_conv_w"], f["L0_conv_conv_b"][:, None], f["L0_conv_dt_proj_b"][:, None],
                         f["L0_conv_D"][:, None], f["L0_conv_A_log"]], axis=1)
    a["pv"] = np.ascontiguousarray(pv.reshape(6, 128, 23).transpose(1, 0, 2))
    pc = np.stack([f["L0_conv_ln_gamma"], f["L0_conv_ln_beta"]], axis=1)
    a["pc"] = np.ascontiguousarray(pc.reshape(3, 128, 2).transpose(1, 0, 2))
    ch = np.arange(C) // 12
    g = (ch[:, None] == ch[None, :]).astype(np.float32).reshape(3, 128, 3, 128)
    a["gm"] = np.ascontiguousarray(g.transpose(1, 0, 2, 3).reshape(128, 9, 128))
    a.update(constants())
    order = np.concatenate([np.arange(0, 128), np.arange(192, 320), np.arange(128, 192), np.arange(320, 384)])
    a["Win1T"] = np.ascontiguousarray(f["L1_conv_w_in"][order].T)
    a["f40"] = np.ascontiguousarray(f["L1_conv_fft_filter"].reshape(C, 40)[order].T)
    a["Wo1T"] = np.ascontiguousarray(f["L1_conv_w_out"].T)
    a["dw"] = np.ascontiguousarray(f["L1_conv_w_dw"].reshape(C, 9)[order].reshape(3, 128, 9).transpose(1, 0, 2))
    a["wn"] = np.ascontiguousarray(f["L2_conv_weights"][0].reshape(3, 128, 4).transpose(1, 0, 2))
    a["row"] = np.concatenate([f["L2_conv_weight_coord"].reshape(8), f["L2_conv_radius"].reshape(4)])[None, :]
    a["gw"] = np.ascontiguousarray(f["L3_conv_gate_w"])
    a["gb"] = np.ascontiguousarray(f["L3_conv_gate_b"][None, :])
    a["W1T"] = np.ascontiguousarray(f["L3_conv_w1"].transpose(2, 0, 1).reshape(C, 4 * C))
    a["W2T"] = np.ascontiguousarray(f["L3_conv_w2"].transpose(2, 0, 1).reshape(C, 4 * C))
    a["b1"] = np.ascontiguousarray(f["L3_conv_b1"].reshape(4, 3, 128).transpose(2, 1, 0))
    a["b2"] = np.ascontiguousarray(f["L3_conv_b2"])
    a["ident"] = np.eye(128, dtype=np.float32)
    return a


def kernel(**inputs):
    import concourse.bacc as bacc
    from concourse.bass_utils import run_bass_kernel_spmd

    nc = bacc.Bacc("TRN2", target_bir_lowering=False, num_devices=1, dynamic_dma_scratch_size=1024)
    arrays = lay(inputs)
    d = {n: nc.dram_tensor(f"in_{n}", a.shape, F32, kind="ExternalInput").ap() for n, a in arrays.items()}
    d["out"] = nc.dram_tensor("out", [NB, C, L], F32, kind="ExternalOutput").ap()
    for n in ("x1", "x3"):
        d[n] = nc.dram_tensor(n, [NB, C, L], F32).ap()
    build(nc, d)
    r = run_bass_kernel_spmd(nc, [{f"in_{n}": a for n, a in arrays.items()}], core_ids=[0])
    return r.results[0]["out"].reshape(NB, C, H, W)
```

```python
from contextlib import ExitStack

import numpy as np

import concourse.bass as bass
from concourse import mybir

F32 = mybir.dt.float32
F32R = mybir.dt.float32r
ALU = mybir.AluOpType
ACT = mybir.ActivationFunctionType

NB, C, H, W = 4, 384, 48, 48
L = H * W
CT = 3
DI = 768
DT_ = 6
NS = 16
RK = 24
T = 384
TB = 3
NQ = L // T
NCH = NB * NQ
NT = L // 128
GN_EPS = 1e-5
LN_EPS = 1e-5
K11 = 11
CONV_DVE = (1, 4)
GAP_SILU = 11
MM, RATE = 0.64, 0.5
M_0 = 0.1
S_COST, M_COST, M_A, M_B, CONV_RATE, HEAD_FROM, REST = 130.0, 90.0, 0.3, 0.8, 0.7, 0.7, 4.0
BANDS = ((0, 9), (9, 19), (19, 29), (29, 39), (39, 48))
GAP_LN = 4
EARLY = 3
GAP_OB = 6
HEAD_GAP = 4
ENGINES = ("pe", "act", "dve", "pool", "sp")


class Done:

    __slots__ = ("eng", "make", "waits", "sem", "value", "used")

    def __init__(self, eng, make, waits, sem, value):
        self.eng, self.make, self.waits = eng, make, waits
        self.sem, self.value, self.used = sem, value, sem is not None


def flat(waits):
    for w in waits:
        if w is None:
            continue
        if isinstance(w, Done):
            yield w
        else:
            yield from flat(w)


class Queues:

    def __init__(self, nc, ctx):
        self.nc, self.ctx = nc, ctx
        self.q = {e: [] for e in ENGINES}
        self.sems = {e: ctx.enter_context(nc.semaphore(f"s_{e}")) for e in ENGINES}
        self.dma_sems, self.dma_count = {}, {}

    def op(self, eng, make, *waits):
        d = Done(eng, make, list(flat(waits)), None, 0)
        for w in d.waits:
            w.used = True
        self.q[eng].append(d)
        return d

    def dma(self, name, out, in_, *waits, eng="sp"):
        if name not in self.dma_sems:
            self.dma_sems[name] = self.ctx.enter_context(self.nc.semaphore(f"d_{name}"))
            self.dma_count[name] = 0
        self.dma_count[name] += 16
        d = Done(eng, lambda e: e.dma_start(out, in_), list(flat(waits)),
                 self.dma_sems[name], self.dma_count[name])
        for w in d.waits:
            w.used = True
        self.q[eng].append(d)
        return d

    def last(self):
        return [self.q[e][-1] for e in ENGINES if self.q[e] and self.q[e][-1].sem is None]

    def emit(self, block):
        for e in ENGINES:
            n = 0
            for d in self.q[e]:
                if d.sem is None and d.used:
                    n += 1
                    d.value = n

        def run(name, eng):
            seen = {}
            for d in self.q[name]:
                need = {}
                for w in d.waits:
                    key = (w.eng, None) if w.sem is None else ("dma", id(w.sem))
                    s = self.sems[w.eng] if w.sem is None else w.sem
                    if w.value > need.get(key, (None, 0))[1]:
                        need[key] = (s, w.value)
                for key, (s, v) in need.items():
                    if seen.get(key, 0) < v:
                        seen[key] = v
                        eng.wait_ge(s, v)
                ins = d.make(eng)
                if d.sem is not None:
                    ins.then_inc(d.sem, 16)
                elif d.used:
                    ins.then_inc(self.sems[name], 1)

        block.tensor(lambda e: run("pe", e))
        block.scalar(lambda e: run("act", e))
        block.vector(lambda e: run("dve", e))
        block.gpsimd(lambda e: run("pool", e))
        block.sync(lambda e: run("sp", e))


class Ring:

    def __init__(self, bufs):
        self.bufs, self.free, self.held, self.n = bufs, [None] * len(bufs), [False] * len(bufs), -1

    def get(self):
        for _ in self.bufs:
            self.n += 1
            i = self.n % len(self.bufs)
            if not self.held[i]:
                self.held[i] = True
                return i, self.bufs[i], self.free[i]
        raise RuntimeError("no buffer of the ring is free")

    def put(self, i, done):
        assert self.held[i]
        self.held[i] = False
        self.free[i] = done


class Arena:

    def __init__(self, nc, base, tag):
        self.nc, self.at, self.tag = nc, (base + 63) // 64 * 64, tag

    def __call__(self, name, shape, dt=F32):
        n = 4
        for s in shape[1:]:
            n *= s
        off = self.at
        self.at = (off + n + 63) // 64 * 64
        return self.nc.alloc_sbuf_tensor_at(f"{self.tag}_{name}", shape, dt, offset=off)


def build(nc, d, layers=(0, 1, 3), images=NB):
    ctx = ExitStack()
    with ctx:
        p = Queues(nc, ctx)
        bank = [ctx.enter_context(nc.psum_tensor(f"ps{i}", [128, 512], F32)) for i in range(4)]
        wide = [ctx.enter_context(nc.psum_tensor(f"pw{i}", [128, 1024], F32)) for i in range(2)]
        base0 = nc.sbuf_base
        keep = Arena(nc, base0, "g")
        ident = keep("ident", [128, 128])
        gm = keep("gm", [128, 9, 128])
        ones = keep("ones", [128, 128])
        mhalf = keep("mhalf", [128, 4])
        base = keep.at
        late = Arena(nc, base, "g2")
        coef = late("coef", [128, NB * NT, 4])
        gst = late("gst", [128, NB, 2, 3])

        t_const = [p.dma("ident", ident[:], d["ident"]), p.dma("gm", gm[:], d["gm"])]
        t_ones = p.op("pool", lambda e: e.memset(ones[:], 1.0))
        t_mh = p.op("pool", lambda e: e.memset(mhalf[:], -0.5))
        t_const += [t_ones, t_mh]

        def mm(out, lhsT, rhs, start, stop, *waits, skip=False):
            return p.op("pe", lambda e: e.matmul(out, lhsT, rhs, start=start, stop=stop, skip_group_check=skip), *waits)

        def tr(out, in_, *waits):
            n = in_.shape[0]
            return p.op("pe", lambda e: e.transpose(out, in_, ident[0:n, 0:n]), *waits)

        def act(out, in_, func, *waits, **kw):
            return p.op("act", lambda e: e.activation(out, in_, func, **kw), *waits)

        def ts(out, in_, s1, s2, op0, op1, *waits, eng="dve"):
            if op1 is None:
                return p.op(eng, lambda e: e.tensor_scalar(out, in_, s1, None, op0), *waits)
            return p.op(eng, lambda e: e.tensor_scalar(out, in_, s1, s2, op0, op1), *waits)

        def tt(out, a, b, op, *waits, eng="dve"):
            return p.op(eng, lambda e: e.tensor_tensor(out, a, b, op), *waits)

        def stt(out, a, s, b, op0, op1, *waits):
            return p.op("dve", lambda e: e.scalar_tensor_tensor(out=out, in0=a, scalar=s, in1=b, op0=op0, op1=op1), *waits)

        def copy(eng, out, in_, *waits):
            if eng == "act":
                return act(out, in_, ACT.Copy, *waits)
            return p.op(eng, lambda e: e.tensor_copy(out, in_), *waits)

        def finish_stats(bn, mv, gs, ps, ps_free, bn_done, out, out_free):
            b = channel_stats(bn, mv, gs, bn_done, out_free)
            return group_stats(mv, gs, ps, ps_free, b, out)

        def channel_stats(bn, mv, gs, bn_done, out_free):
            a = None
            for c in range(CT):
                a = p.op("dve", lambda e, c=c: e.bn_aggr(mv[:, c, :], bn[:, c, :, :].rearrange("p k s -> p (k s)")), bn_done, out_free)
            b = tt(gs[:, 0, :], mv[:, :, 0], mv[:, :, 0], ALU.mult, a)
            return tt(mv[:, :, 1], mv[:, :, 1], gs[:, 0, :], ALU.add, b)

        def group_stats(mv, gs, ps, ps_free, b, out):
            last = None
            for co in range(CT):
                cis = [ci for ci in range(CT) if abs(ci - co) <= 1]
                for ci in cis:
                    last = mm(ps[:, 2 * co:2 * co + 2], gm[:, 3 * ci + co, :], mv[:, ci, :],
                              ci == cis[0], ci == cis[-1], b, ps_free, t_const)
            g = ts(gs[:, 1:3, :], ps[:, 0:6].rearrange("p (c k) -> p k c", k=2), 1.0 / 12.0, None, ALU.mult, None, last)
            x = tt(gs[:, 0, :], gs[:, 1, :], gs[:, 1, :], ALU.mult, g)
            x = tt(gs[:, 2, :], gs[:, 2, :], gs[:, 0, :], ALU.subtract, x)
            x = ts(gs[:, 2, :], gs[:, 2, :], GN_EPS, None, ALU.add, None, x)
            r = tt(out[:, 0, :], gs[:, 2, :], mhalf[:, 0:3], ALU.pow, x, eng="pool")
            f = stt(out[:, 1, :], gs[:, 1, :], -1.0, out[:, 0, :], ALU.mult, ALU.mult, r)
            return g, f

        stored = {}

        def layer0(xin_d, xout_d):
            ar = Arena(nc, base, "a")
            WinT = ar("WinT", [128, 3, 1536])
            WxT = ar("WxT", [128, 6, 128])
            Wdt3 = ar("Wdt3", [128, DI], F32R)
            raw = ar("raw", [128, 6, T + 3])
            V = raw[:, :, 3:T + 3]
            xn = ar("xn", [128, 3, T])
            sx = ar("sx", [128, 3, T])
            dt = [ar("dt0", [128, 6, T])]
            dtxT = [ar("dtxT0", [128, TB, DI])]
            xs = [ar("xs0", [128, 3, T])]
            dtl = ar("dtl", [64, T])
            dt3 = ar("dt3", [128, T], F32R)
            early_end = ar.at
            Aneg = ar("Aneg", [128, 6, NS])
            one1 = ar("one1", [128, 1])
            xs.append(ar("xs1", [128, 3, T]))
            bn = ar("bn", [128, 3, NQ, 6])
            mv = ar("mv", [128, 3, 2])
            gs = ar("gs", [128, 3, 3])
            sc = [ar(f"sc{i}", [128, 2, 3]) for i in range(2)]
            xin = [ar("xin0", [128, 6, T])]
            sz = [ar("sz0", [128, 6, T])]
            dt.append(ar("dt1", [128, 6, T]))
            dtxT.append(ar("dtxT1", [128, TB, DI]))
            BC = [ar(f"BC{i}", [128, TB, 32]) for i in range(2)]
            dBT = [ar(f"dBT{i}", [128, TB, DI]) for i in range(2)]
            dA = Ring([ar(f"dA{i}", [128, T]) for i in range(12)])
            hb = [ar(f"h{i}", [128, 6, T]) for i in range(2)]
            st = ar("st", [128, 6, NS])
            xs.append(ar("xs2", [128, 3, T]))
            xin.append(ar("xin1", [128, 6, T]))
            sz.append(ar("sz1", [128, 6, T]))
            WoT = ar("WoT", [128, 6, C])
            pv = ar("pv", [128, 6, 23])
            pc = ar("pc", [128, 3, 2])
            acc = ar("acc", [128, TB, DI])
            ob = ar("ob", [128, TB, C])
            lbn = ar("lbn", [128, TB, 6])
            lmv = ar("lmv", [128, TB, 2])
            lsc = ar("lsc", [128, TB, 2])
            pp = Ring(bank)
            pb = pp
            ph = Ring(wide)

            xv = xin_d.rearrange("b (c p) l -> b p c l", p=128)
            xo = xout_d.rearrange("b (c p) l -> b p c l", p=128)
            first = [sx[:], sz[0][:, 0:3, :], sz[0][:, 3:6, :], sz[1][:, 0:3, :], sz[1][:, 3:6, :], xin[1][:, 0:3, :]]
            first_ld = [p.dma(f"fx{q}", t, xv[0, :, :, q * T:(q + 1) * T]) for q, t in enumerate(first)]
            w_in = p.dma("WinT", WinT[:], d["WinT"].rearrange("(k p) n -> p k n", p=128))
            w_pv = p.dma("pv", pv[:], d["pv"])
            w_pc = p.dma("pc", pc[:], d["pc"])
            w_x = p.dma("WxT", WxT[:], d["WxT"].rearrange("(k p) n -> p k n", p=128))
            w_dt = p.dma("Wdt3", acc[:, 0, :], d["Wdt3"])
            w_o = p.dma("WoT", WoT[:], d["WoT"].rearrange("(k p) n -> p k n", p=128))
            one_t = p.op("pool", lambda e: e.memset(one1[:], 1.0))
            p.op("act", lambda e: e.preload_act_table_set("natural_log_exp_and_others"))
            a0 = act(Aneg[:], pv[:, :, 7:23], ACT.Exp, w_pv)
            t_A = ts(Aneg[:], Aneg[:], -1.0, None, ALU.mult, None, a0)
            cw = lambda m, j: pv[:, m, j:j + 1]
            cb = lambda m: pv[:, m, 4:5]
            db = lambda m: pv[:, m, 5:6]
            Dm = lambda m: pv[:, m, 6:7]

            free = {n: [None, None, None] for n in ("xs", "xin", "sz", "dt", "dtxT", "BC", "dBT", "h", "sc", "tap")}
            free.update({n: None for n in ("sx", "bn", "xn", "raw", "V", "dtl", "ob", "acc")})
            free["xn"] = []
            scale_done, beta_done, ready, acc_done = {}, {}, {}, {}
            halo_done = [None]
            st_done = [None] * NS

            def stats(b):
                t = None
                for q in range(NQ):
                    if b == 0:
                        ld, src = first_ld[q], first[q]
                    else:
                        ld, src = p.dma("sx", sx[:], xv[b, :, :, q * T:(q + 1) * T], free["sx"]), sx
                    yield 0
                    for c in range(CT):
                        t = p.op("dve", lambda e, c=c, q=q, src=src: e.bn_stats(bn[:, c, q, :], src[:, c, :]), ld, free["bn"])
                        yield 0
                    free["sx"] = t
                if b == 0:
                    free["sz"], free["xin"][1] = [t, t], t
                i, ps, fr = pp.get()
                g, f = finish_stats(bn, mv, gs, ps, fr, t, sc[b % 2], free["sc"][b % 2])
                pp.put(i, g)
                free["bn"] = f
                scale_done[b] = f
                yield 0

            posted, normed, gate_raw, gated_z = {}, {}, {}, {}

            def project(col, xn_t, xn_read, evac):
                held = x = None
                for m in range(6):
                    if held:
                        pp.put(held[0], evac(*held[1:]))
                    i, ps, fr = pp.get()
                    for kk in range(CT):
                        x = mm(ps[:, 0:T], WinT[:, kk, col + m * 128:col + (m + 1) * 128], xn[:, kk, :], kk == 0, kk == 2, xn_t, fr, w_in)
                        yield MM
                    held = (i, m, ps, x)
                yield 0
                pp.put(held[0], evac(*held[1:]))
                xn_read.append(x)

            def gate_in(k):
                o = k % 2
                zs = gate_raw[k] = []

                def to_sz(m, ps, x):
                    zs.append(copy("act", sz[o][:, m, :], ps[:, 0:T], x, free["sz"][o]))
                    return zs[m]

                while k not in normed or (k >= 2 and not posted.get((k - 2, "sz"))):
                    yield 0
                yield from project(DI, normed[k], free["xn"], to_sz)
                posted[k, "z"] = True

            def silu_gate(k):
                zt = act(sz[k % 2][:], sz[k % 2][:], ACT.Silu, gate_raw[k])
                gated_z[k] = zt

            def pre(k):
                b, q = divmod(k, NQ)
                o = k % 2
                t0 = q * T
                xb = xs[k % 3]
                ld = p.dma(f"xs{k % 3}", xb[:], xv[b, :, :, t0:t0 + T], free["xs"][k % 3])
                yield 0
                while k > 0 and not posted.get((k - 1, "z")):
                    yield 0
                n = []
                for c in range(CT):
                    n.append(ts(xn[:, c, :], xb[:, c, :], sc[b % 2][:, 0, c:c + 1], sc[b % 2][:, 1, c:c + 1],
                                ALU.mult, ALU.add, ld, scale_done[b], free["xn"], eng="pool"))
                free["xn"] = []
                normed[k] = n
                if q == NQ - 1:
                    free["sc"][b % 2] = n
                for c in range(CT):
                    beta_done[k] = act(xb[:, c, :], xb[:, c, :], ACT.Identity, n, w_pc, bias=pc[:, c, 1:2])
                if q == 0:
                    hl = p.op("pool", lambda e: e.memset(raw[:, :, 0:3], 0.0), free["raw"])
                else:
                    hl = halo_done[0]
                yield 0
                rw = [None] * 6

                def to_raw(m, ps, x):
                    rw[m] = copy("act", raw[:, m, 3:T + 3], ps[:, 0:T], x, free["raw"], free["V"], hl)
                    return rw[m]

                prev = [None] * 6

                def conv(m):
                    if m in CONV_DVE:
                        prev[m] = ts(xin[o][:, m, :], raw[:, m, 0:T], cw(m, 0), cb(m), ALU.mult, ALU.add,
                                     rw[m], hl, free["xin"][o], w_pv)
                        for j in range(1, 4):
                            yield
                            prev[m] = stt(xin[o][:, m, :], raw[:, m, j:j + T], cw(m, j), xin[o][:, m, :], ALU.mult, ALU.add, prev[m])
                        return
                    prev[m] = ts(xin[o][:, m, :], raw[:, m, 0:T], cw(m, 0), cb(m), ALU.mult, ALU.add,
                                 rw[m], hl, free["xin"][o], w_pv, eng="pool")
                    for j in range(1, 4):
                        yield
                        i, tm, fr = dA.get()
                        pr = act(tm[:], raw[:, m, j:j + T], ACT.Copy, rw[m], hl, fr, w_pv, scale=cw(m, j))
                        prev[m] = tt(xin[o][:, m, :], xin[o][:, m, :], tm[:], ALU.add, pr, prev[m], eng="pool")
                        dA.put(i, prev[m])
                        yield

                while k >= 2 and not posted.get((k - 2, "xin")):
                    yield 0
                going, cm = [], 0
                pj = project(0, n, free["xn"], to_raw)
                alive = True
                while alive or cm < 6 or going:
                    cost = 0
                    if alive:
                        cost = next(pj, -1)
                        if cost < 0:
                            alive, cost = False, 0
                    while cm < 6 and rw[cm] is not None and len(going) < 2:
                        going.append(conv(cm))
                        cm += 1
                    going = [g for g in going if next(g, 1) != 1]
                    yield cost
                if q < NQ - 1:
                    halo_done[0] = p.op("pool", lambda e: e.tensor_copy(raw[:, :, 0:3], raw[:, :, T:T + 3]), prev)
                    halo = halo_done[0]
                else:
                    halo = prev
                while k > 0 and not posted.get((k - 1, "z")):
                    yield 0
                xt = act(xin[o][:], xin[o][:], ACT.Silu, prev)
                if k > 0:
                    silu_gate(k - 1)
                p.op("act", lambda e: e.preload_act_table_set("natural_log_exp_and_others"))
                for _ in range(GAP_SILU):
                    yield 0
                i, ps, fr = pp.get()
                for m in range(6):
                    x = mm(ps[:, 0:T], WxT[:, m, :], xin[o][:, m, :], m == 0, m == 5, xt, fr, w_x)
                    yield MM
                t3 = copy("act", dt3[:], ps[:, 0:T], x, free["dtl"])
                tl = copy("act", dtl[32:64, :], ps[32:64, 0:T], x, free["dtl"])
                t3 = tt(dt3[64:96, :], ps[64:96, 0:T], dt3[64:96, :].bitcast(F32), ALU.subtract, t3, tl)
                pp.put(i, t3)
                yield 0
                yield 0
                i, ps, fr = pp.get()
                for tb in range(TB):
                    x = p.op("pe", lambda e, tb=tb, ps=ps: e.transpose(
                        ps[:, tb * 32:tb * 32 + 32], dtl[32:64, tb * 128:(tb + 1) * 128], ident[32:64, 32:64]), tl, fr, t_const)
                tBC = copy("act", BC[o][:], ps[:, 0:96].rearrange("p (a n) -> p a n", n=32), x, free["BC"][o])
                pp.put(i, tBC)
                vs = []
                for m in range(6):
                    i, ps, fr = pp.get()
                    x = mm(ps[:, 0:T], Wdt3[:, m * 128:(m + 1) * 128], dt3[:], True, True, t3, fr, w_dt)
                    yield MM / 4
                    vs.append(act(V[:, m, :], ps[:, 0:T], ACT.Identity, x, halo, prev, bias=db(m)))
                    pp.put(i, vs[m])
                free["dtl"] = [x, tBC]
                yield 0
                c0 = act(dt[o][:], V, ACT.Abs, vs, free["dt"][o])
                yield 0
                c1 = act(dt[o][:], dt[o][:], ACT.Exp, c0, scale=-1.0)
                yield 0
                c2 = act(dt[o][:], dt[o][:], ACT.Ln, c1, one_t, bias=one1[:, 0:1])
                for _ in range(GAP_LN):
                    yield 0
                tdt, tx, ct = [], [], []
                for m in range(6):
                    tdt.append(stt(dt[o][:, m, :], V[:, m, :], 0.0, dt[o][:, m, :], ALU.max, ALU.add, c2))
                    tx.append(tt(V[:, m, :], dt[o][:, m, :], xin[o][:, m, :], ALU.mult, tdt[m], xt, eng="pool"))
                    yield 0
                yield 0
                for hf in range(2):
                    for tb in range(TB):
                        i, ps, fr = pp.get()
                        for cc in range(3):
                            x = tr(ps[:, cc * 128:(cc + 1) * 128], V[:, hf * 3 + cc, tb * 128:(tb + 1) * 128], tx[hf * 3 + cc], fr, t_const)
                        yield MM / 2
                        ct.append(copy("act", dtxT[o][:, tb, hf * T:(hf + 1) * T], ps[:, 0:T], x, free["dtxT"][o]))
                        pp.put(i, ct[-1])
                free["V"] = x
                free["raw"] = prev
                ready[k] = dict(xt=xt, BC=tBC, dt=tdt, dtx=ct)

            nk = images * NQ
            exps = {}
            scaled = {}
            LEAD = 5

            def exp_to(n):
                while len(exps) <= min(n, nk * NS * 6 - 1):
                    g = len(exps)
                    k, r = divmod(g, NS * 6)
                    s, c = divmod(r, 6)
                    if k not in ready:
                        return
                    j, da, df = dA.get()
                    e = act(da[:], dt[k % 2][:, c, :], ACT.Exp, ready[k]["dt"][c], df, t_A, scale=Aneg[:, c, s:s + 1])
                    exps[g] = (j, da, e)
                    if r == NS * 6 - 1:
                        free["dt"][k % 2] = e

            def scale_to(n):
                while len(scaled) <= min(n, nk * NS - 1):
                    g = len(scaled)
                    k, s = divmod(g, NS)
                    if k not in ready:
                        return
                    o = k % 2
                    for tb in range(TB):
                        bt = ts(dBT[g % 2][:, tb, :], dtxT[o][:, tb, :], BC[o][:, tb, s:s + 1], 1.0, ALU.mult, ALU.mult,
                                ready[k]["dtx"], ready[k]["BC"], free["dBT"][g % 2], eng="pool")
                    scaled[g] = bt
                    if s == NS - 1:
                        free["dtxT"][o] = bt

            acc_t = [None] * TB

            def contract(k, s, tb, hd):
                o = k % 2
                i, ps, fr = ph.get()
                for c in range(6):
                    x = tr(ps[:, c * 128:(c + 1) * 128], hb[s % 2][:, c, tb * 128:(tb + 1) * 128], hd[c], fr, t_const)
                cs = BC[o][:, tb, 16 + s:17 + s]
                if s == 0:
                    y = ts(acc[:, tb, :], ps[:, 0:DI], cs, None, ALU.mult, None, x, ready[k]["BC"], free["acc"])
                else:
                    y = stt(acc[:, tb, :], ps[:, 0:DI], cs, acc[:, tb, :], ALU.mult, ALU.add, x, acc_t[tb])
                acc_t[tb] = y
                ph.put(i, y)
                if tb == TB - 1:
                    free["h"][s % 2] = [x, st_done[s]]
                return y

            def scan(k):
                b, q = divmod(k, NQ)
                hd = {}
                y = None
                for s in range(NS + 1):
                    if s < NS:
                        scale_to(k * NS + s + 1)
                        hd[s] = []
                    for c in range(6):
                        if s < NS:
                            g = (k * NS + s) * 6 + c
                            exp_to(g + LEAD)
                            j, da, e = exps[g]
                            i, ps, fr = pb.get()
                            src = dBT[(k * NS + s) % 2]
                            for tb in range(TB):
                                x = tr(ps[:, tb * 128:(tb + 1) * 128], src[:, tb, c * 128:(c + 1) * 128], scaled[k * NS + s], fr, t_const)
                            init = 0.0 if q == 0 else st[:, c, s:s + 1]
                            h = p.op("dve", lambda e, c=c, s=s, da=da, ps=ps, init=init: e.tensor_tensor_scan(
                                hb[s % 2][:, c, :], da[:], ps[:, 0:T], init, ALU.mult, ALU.add),
                                x, e, free["h"][s % 2], None if q == 0 else st_done[s])
                            pb.put(i, h)
                            dA.put(j, h)
                            hd[s].append(h)
                            if c == 5:
                                free["dBT"][(k * NS + s) % 2] = x
                        if s > 0 and c == 0:
                            st_done[s - 1] = p.op("pool", lambda e, s=s: e.tensor_copy(st[:, :, s - 1], hb[(s - 1) % 2][:, :, T - 1]), hd[s - 1])
                        if s > 0 and c % 2 == 1:
                            y = contract(k, s - 1, c // 2, hd[s - 1])
                        if s < NS or c % 2 == 1:
                            yield
                free["BC"][k % 2] = [y, scaled[k * NS + NS - 1]]
                acc_done[k] = y

            def post(k):
                b, q = divmod(k, NQ)
                o = k % 2
                t0 = q * T
                xb = xs[k % 3]
                R = ready[k]
                yt = []
                for c in range(6):
                    i, ps, fr = pp.get()
                    for tb in range(TB):
                        x = tr(ps[:, tb * 128:(tb + 1) * 128], acc[:, tb, c * 128:(c + 1) * 128], acc_done[k], fr)
                    yield MM / 2
                    y = stt(xin[o][:, c, :], xin[o][:, c, :], Dm(c), ps[:, 0:T], ALU.mult, ALU.add, x, R["xt"])
                    pp.put(i, y)
                    yt.append(tt(sz[o][:, c, :], xin[o][:, c, :], sz[o][:, c, :], ALU.mult, y, gated_z[k], eng="pool"))
                free["acc"] = x
                free["xin"][o] = yt
                posted[k, "xin"] = True
                yield 0
                obs = [None] * TB

                def norm(tb, i, ps, x):
                    s0 = copy("act", ob[:, tb, :], ps[:, 0:C], x, free["ob"])
                    pp.put(i, s0)
                    yield
                    yield
                    s1 = p.op("dve", lambda e: e.bn_stats(lbn[:, tb, :], ob[:, tb, :]), s0)
                    s2 = p.op("dve", lambda e: e.bn_aggr(lmv[:, tb, :], lbn[:, tb, :]), s1)
                    s3 = ts(lmv[:, tb, 1:2], lmv[:, tb, 1:2], LN_EPS, None, ALU.add, None, s2)
                    s4 = tt(lsc[:, tb, 0:1], lmv[:, tb, 1:2], mhalf[:, 0:1], ALU.pow, s3, eng="pool")
                    yield
                    yield
                    s5 = stt(lsc[:, tb, 1:2], lmv[:, tb, 0:1], -1.0, lsc[:, tb, 0:1], ALU.mult, ALU.mult, s4)
                    yield
                    obs[tb] = act(ob[:, tb, :], ob[:, tb, :], ACT.Identity, s5, scale=lsc[:, tb, 0:1], bias=lsc[:, tb, 1:2])

                nr = None
                for tb in range(TB):
                    i, ps, fr = pp.get()
                    for m in range(6):
                        x = mm(ps[:, 0:C], sz[o][:, m, tb * 128:(tb + 1) * 128], WoT[:, m, :], m == 0, m == 5, yt[m], fr, w_o)
                        yield MM
                        if nr is not None and next(nr, 1) == 1:
                            nr = None
                    nr = norm(tb, i, ps, x)
                free["sz"][o] = x
                posted[k, "sz"] = True
                yield 0
                for _ in nr:
                    yield 0
                for _ in range(GAP_OB):
                    yield 0
                for c in range(3):
                    i, ps, fr = pp.get()
                    for tb in range(TB):
                        x = tr(ps[:, tb * 128:(tb + 1) * 128], ob[:, tb, c * 128:(c + 1) * 128], obs, fr)
                    yield MM / 2
                    y = stt(xb[:, c, :], ps[:, 0:T], pc[:, c, 0:1], xb[:, c, :], ALU.mult, ALU.add, x, beta_done[k])
                    pp.put(i, y)
                free["ob"] = x
                w = p.dma(f"x1o{k % 3}", xo[b, :, :, t0:t0 + T], xb[:], y)
                free["xs"][k % 3] = w
                stored.setdefault(("x1", b), []).append(w)

            for _ in stats(0):
                pass
            w_dt = copy("dve", Wdt3[:], acc[:, 0, :], w_dt)
            w_dt = tt(Wdt3[96:128, :], acc[96:128, 0, :], Wdt3[96:128, :].bitcast(F32), ALU.subtract, w_dt)
            free["acc"] = w_dt
            for _ in pre(0):
                pass

            def run_all(threads):
                while threads:
                    threads = [t for t in threads if next(t, None) is not None]

            for k in range(nk):
                first = post(k - 1) if k > 0 else None
                main = pre(k + 1) if k + 1 < nk else None
                rest = [gate_in(0)] if k == 0 else []
                if k > 0:
                    rest.append(first)
                if k + 1 < nk:
                    rest.append(gate_in(k + 1))
                st_ = stats(k // NQ + 1) if k % NQ == 2 and k // NQ + 1 < images else None
                credit, n = 0.0, 0
                if k == nk - 1 and images > 2 and 1 in layers:
                    prepare1(d["x1"])
                    assert l1["end"] <= early_end
                for _ in scan(k):
                    credit = min(credit + RATE, MM)
                    if n < 7 and first is not None:
                        credit -= next(first)
                    if main is not None and credit > 0:
                        c = next(main, None)
                        if c is None:
                            main = None
                        else:
                            credit -= c
                    if n >= 7:
                        while rest and credit > 0:
                            c = next(rest[0], None)
                            if c is None:
                                rest.pop(0)
                            else:
                                credit -= c
                                if c == 0:
                                    break
                    if st_ is not None and n % 2:
                        next(st_, None)
                    n += 1
                run_all([t for t in [main, st_] + rest if t is not None])
            silu_gate(nk - 1)
            end = post(nk - 1)
            if images <= 2 or 1 not in layers:
                for _ in end:
                    pass
                return None
            pp.bufs, pp.held = pp.bufs[0:2], pp.held[0:2]
            return end, pp

        def fence():
            return p.last() + [t for v in stored.values() for t in v]

        def split(hi, lo, src, *waits):
            a = copy("act", hi, src, *waits)
            return a, tt(lo, src, hi.bitcast(F32), ALU.subtract, a, *waits)

        third, l1 = {}, {}

        def prepare1(x1_d):
            fe = fence()
            ar = Arena(nc, late.at, "b")
            l1["Th"] = ar("Th", [128, 4, 18, 28], F32R)
            l1["Tl"] = ar("Tl", [128, 4, 18, 28], F32R)
            l1["at"] = ar.at
            l1["x0"] = ar("x0", [128, 3, L])
            for n, shape in (("Win1", [128, 3, C]), ("Fwd", [128, 128]), ("Inv", [128, 128]), ("feff", [128, C]),
                             ("WoA", [128, C]), ("WoC", [128, C]), ("dw", [128, 3, 9])):
                l1[n] = ar(n, shape)
            at = ar.at
            l1["tT"] = Ring([ar(f"tT{i}", [128, C]) for i in range(2)])
            l1["tf"] = Ring([ar(f"tf{i}", [128, C]) for i in range(2)])
            l1["end"] = ar.at
            sl = Arena(nc, at, "bf")
            l1["S40"], l1["f40"] = sl("S40", [40, 128]), sl("f40", [40, C])
            xv = x1_d.rearrange("b (c p) l -> b p c l", p=128)
            i = (0 - images) % 2
            assert i == 0 or images < 2 or images % 2
            l1["ld"] = [p.dma(f"x1i{i}{r}", l1["x0"][:, :, r * T:(r + 1) * T], xv[0, :, :, r * T:(r + 1) * T], fe, stored.get(("x1", 0), []))
                        for r in range(NQ)] if i == 0 else None
            l1["w"] = [p.dma(n, l1[n][:], src, fe) for n, src in (
                ("Win1", d["Win1T"].rearrange("(k p) n -> p k n", p=128)), ("Fwd", d["Fwd"]), ("Inv", d["Inv"]), ("S40", d["S40"]),
                ("f40", d["f40"]), ("WoA", d["Wo1T"][0:128, :]), ("dw", d["dw"]))]
            l1["w"].append(p.dma("WoC", l1["WoC"][64:128, :], d["Wo1T"][128:192, :], fe))

        def weights3():
            fe = fence()
            ar = Arena(nc, l1["at"], "c")
            for i in (1, 2):
                third[f"W{i}h"] = ar(f"W{i}h", [128, 3, 4 * C], F32R)
                third[f"W{i}l"] = ar(f"W{i}l", [128, 3, 4 * C], F32R)
            third["at"] = ar.at
            Wt = ar("Wt", [128, 3, 4 * C])
            t = None
            for i in (1, 2):
                ld = p.dma(f"W{i}", Wt[:], d[f"W{i}T"].rearrange("(k p) n -> p k n", p=128), fe, t)
                for _ in range(40):
                    yield
                t = []
                for kk in range(CT):
                    t += split(third[f"W{i}h"][:, kk, :], third[f"W{i}l"][:, kk, :], Wt[:, kk, :], ld)
                    for _ in range(4):
                        yield
                third[f"w{i}"] = t

        def layer12(x1_d, x3_d, under_way):
            if not l1:
                prepare1(x1_d)
            fe = fence()
            Th, Tl, Win1, Fwd, Inv, feff, WoA, WoC, dw, tT, tf, S40, f40 = (l1[n] for n in (
                "Th", "Tl", "Win1", "Fwd", "Inv", "feff", "WoA", "WoC", "dw", "tT", "tf", "S40", "f40"))
            x, w = [l1["x0"]], l1["w"]
            ar = Arena(nc, l1["end"], "b2")
            timg = [ar(f"ti{i}", [128, 50, 50]) for i in range(3)]
            cv = [ar(f"cv{i}", [128, 3, 2 * T]) for i in range(2)]
            tm = Ring([ar(f"tm{i}", [128, 2 * T]) for i in range(2)])
            at1 = ar.at
            x.append(ar("x1", [128, 3, L]))
            wn = ar("wn", [128, 3, 4])
            gw = ar("gw", [128, 3, 4])
            gws = ar("gws", [128, 3, 4])
            gb = ar("gb", [4, 1])
            gbs = ar("gbs", [4, 1])
            lg = Ring([ar("lg", [4, T])])
            row = ar("row", [1, 12])
            par = ar("par", [128, 12])
            xn = Ring([ar(f"xn{i}", [128, 3, T]) for i in range(4)])
            sm = [dict(bn=ar(f"bn{i}", [128, 3, NQ, 6]), mv=ar(f"mv{i}", [128, 3, 2]), gs=ar(f"gs{i}", [128, 3, 3]),
                       sc=ar(f"sc{i}", [128, 2, 3])) for i in range(2)]
            bn3 = ar("bn3", [128, 3, len(BANDS), 6])
            mv3 = ar("mv3", [128, 3, 2])
            gs3 = ar("gs3", [128, 3, 3])
            u0 = ar.at
            xTh = ar("xTh", [128, NT, C], F32R)
            xTl = ar("xTl", [128, NT, C], F32R)
            ar = Arena(nc, at1, "bs")
            G0 = ar("G0", [128, 504])
            G1 = ar("G1", [128, 504])
            GM = ar("GM", [128, 504])
            gt = ar("gt", [128, 504])
            gu = ar("gu", [128, 504])
            banks = Ring((bank if under_way is None else bank[2:4])
                         + [wide[0][:, 0:512], wide[0][:, 512:1024], wide[1][:, 0:512], wide[1][:, 512:1024]])
            xv = x1_d.rearrange("b (c p) l -> b p c l", p=128)
            xo = x3_d.rearrange("b (c p) l -> b p c l", p=128)
            rows = lambda r: slice(T * r, T * r + T)

            def load(b, r, *waits):
                return p.dma(f"x1i{(b - images) % 2}{r}", x[(b - images) % 2][:, :, rows(r)], xv[b, :, :, rows(r)], waits, stored.get(("x1", b), []))

            ld = {0: l1["ld"] or [load(0, r, fe) for r in range(NQ)]}
            w2 = [p.dma(n, t[:], src, fe) for n, t, src in (
                ("wn", wn, d["wn"]), ("gw", gw, d["gw"].rearrange("(k p) n -> p k n", p=128)),
                ("gb", gb, d["gb"]), ("row", row, d["row"]), ("G0", G0, d["G0"]), ("G1", G1, d["G1"]), ("GM", GM, d["GM"]))]
            zero = [p.op("pool", lambda e, i=i: e.memset(timg[i][:], 0.0), fe) for i in range(3)]

            i, ps, fr = banks.get()
            a = mm(ps[:, 0:C], S40[:], f40[:], True, True, w, fr, t_const, fe)
            t_feff = copy("act", feff[:], ps[:, 0:C], a)
            banks.put(i, t_feff)
            t_T = []

            def matrices():
                i, ps, fr = banks.get()
                a = mm(ps[:, 0:12], ones[0:1, :], row[:], True, True, w2, fr, t_const)
                b_ = copy("dve", par[:], ps[:, 0:12], a)
                banks.put(i, b_)
                r_ = p.op("dve", lambda e: e.reciprocal(par[:, 8:12], par[:, 8:12]), b_)
                r_ = ts(par[:], par[:], -1.0, None, ALU.mult, None, r_)
                yield
                t = None
                for n in range(4):
                    a0 = act(gt[:], G0[:], ACT.Abs, r_, t, bias=par[:, 2 * n:2 * n + 1])
                    a1 = act(gu[:], G1[:], ACT.Abs, r_, t, bias=par[:, 2 * n + 1:2 * n + 2])
                    yield
                    a2 = tt(gt[:], gt[:], gu[:], ALU.add, a0, a1)
                    a3 = ts(gt[:], gt[:], par[:, 8 + n:9 + n], 1.0, ALU.mult, ALU.add, a2)
                    a4 = stt(gt[:], gt[:], 0.0, GM[:], ALU.max, ALU.mult, a3)
                    yield
                    t = split(Th[:, n].rearrange("p h w -> p (h w)"), Tl[:, n].rearrange("p h w -> p (h w)"), gt[:], a4)
                    yield
                t_T[:] = list(t)
                if images > 1:
                    ld[1] = [load(1, r, fe, t_T) for r in range(NQ)]

            def patches(t, r):
                return t[:, rows(r)].rearrange("p (h j w) -> p j h w", j=3, w=16)

            def normalize(xt, r, sc, ready):
                i, n, fr = xn.get()
                t = []
                for c in range(CT):
                    t.append(ts(n[:, c, :].rearrange("p (j h w) -> p j h w", j=3, w=16), patches(xt[:, c, :], r),
                                sc[:, 0, c:c + 1], sc[:, 1, c:c + 1], ALU.mult, ALU.add, ready, fr, fe, eng="pool"))
                return i, n, t

            conv_q = []
            mixed, sc_free = {}, [None, None]

            def mix(b):
                xt, S = x[(b - images) % 2], sm[0]
                for r in range(NQ):
                    for c in range(CT):
                        t = p.op("dve", lambda e, c=c, r=r: e.bn_stats(S["bn"][:, c, r, :], xt[:, c, rows(r)]), ld[b][r], fe)
                    yield 0.5
                cs = channel_stats(S["bn"], S["mv"], S["gs"], t, sc_free[0])
                yield REST
                i, ps, fr = banks.get()
                g, f = group_stats(S["mv"], S["gs"], ps, fr, cs, S["sc"])
                banks.put(i, g)
                yield REST / 2
                nx = [normalize(xt, 0, S["sc"], f)]
                yield REST
                img = [[None] * 6 for _ in range(3)]
                conv_t, out_t = {}, {}

                def conv(g):
                    while g == 2 and 0 not in out_t:
                        yield
                    need = [img[o][r] for o in range(3) for r in range(min(6, 2 * g + 3))]
                    prev = [None] * 3
                    for k in range(9):
                        dy, dx = divmod(k, 3)
                        for o in (2, 0, 1):
                            src = timg[o][:, 16 * g + dy:16 * g + dy + 16, dx:dx + W]
                            dst = cv[g % 2][:, o, :].rearrange("p (h w) -> p h w", w=W)
                            if o == 2 and k == 0:
                                prev[o] = act(dst, src, ACT.Copy, need, cv_free[g % 2], scale=dw[:, o, 0:1])
                                continue
                            if o == 2:
                                i, tb_, tfr = tm.get()
                                tv = tb_[:].rearrange("p (h w) -> p h w", w=W)
                                pr = act(tv, src, ACT.Copy, need, tfr, fe, scale=dw[:, o, k:k + 1])
                                prev[o] = tt(dst, dst, tv, ALU.add, pr, prev[o], eng="pool")
                                tm.put(i, prev[o])
                                continue
                            if k == 0:
                                prev[o] = ts(dst, src, dw[:, o, 0:1], None, ALU.mult, None, need, cv_free[g % 2])
                            else:
                                prev[o] = stt(dst, src, dw[:, o, k:k + 1], dst, ALU.mult, ALU.add, prev[o])
                            yield
                    conv_t[g] = prev
                    if g == 2:
                        timg_free[:] = prev

                st1, st2, ob = {}, {}, {}
                for n in range(NT + 2):
                    if n < NT:
                        r, j = divmod(n, 3)
                        if j == 1 and r < NQ - 1:
                            nx.append(normalize(xt, r + 1, S["sc"], f))
                        i, ps, fr = banks.get()
                        for kk in range(CT):
                            a = mm(ps[:, 0:C], nx[0][1][:, kk, j * 128:(j + 1) * 128], Win1[:, kk, :], kk == 0, kk == 2, nx[0][2], fr, w)
                        if j == 2:
                            xn.put(nx[0][0], a)
                            sc_free[0] = nx[0][2]
                            nx.pop(0)
                        ti, tb_, tfr = tT.get()
                        c_ = copy("act", tb_[:], ps[:, 0:C], a, tfr, fe)
                        banks.put(i, c_)
                        st1[n] = (ti, tb_, c_)
                        yield 3 * MM
                    if 1 <= n <= NT:
                        ti, tb_, c_ = st1[n - 1]
                        i, ps, fr = banks.get()
                        a = mm(ps[:, 0:C], Fwd[:], tb_[:], True, True, c_, fr)
                        tT.put(ti, a)
                        fi, fb, ffr = tf.get()
                        c_ = tt(fb[:], ps[:, 0:C], feff[:], ALU.mult, a, ffr, t_feff, fe)
                        banks.put(i, c_)
                        st2[n - 1] = (fi, fb, c_)
                        yield MM
                    if n >= 2:
                        r, j = divmod(n - 2, 3)
                        fi, fb, c_ = st2[n - 2]
                        if j == 0:
                            ob = {o: banks.get() for o in range(3)}
                        for o in range(3):
                            i, ps, fr = ob[o]
                            a = mm(ps[:, 0:T].rearrange("p (h w) -> p h w", w=W)[:, :, 16 * j:16 * j + 16], fb[:, o * 128:(o + 1) * 128],
                                   Inv[:].rearrange("p (h w) -> p h w", w=16), True, True, c_, fr, skip=True)
                            if j == 2:
                                img[o][r] = copy("act", timg[o][:, 8 * r + 1:8 * r + 9, 1:1 + W],
                                                 ps[:, 0:T].rearrange("p (h w) -> p h w", w=W), a, zero, timg_free)
                                banks.put(i, img[o][r])
                        tf.put(fi, a)
                        if j == 2 and r in (2, 4, 5):
                            conv_q.append(conv(max(0, r // 2 - 1) if r < 5 else 2))
                        yield MM
                res = []
                for g in range(3):
                    while g not in conv_t:
                        yield 0
                    v = cv[g % 2]
                    a = act(v[:, 0, :], v[:, 0, :], ACT.Gelu, conv_t[g])
                    a = tt(v[:, 0, :], v[:, 0, :], v[:, 1, :], ALU.mult, a, eng="pool")
                    c_ = act(v[64:128, 1, :], v[0:64, 2, :], ACT.Gelu, conv_t[g], a)
                    c_ = tt(v[64:128, 1, :], v[64:128, 1, :], v[64:128, 2, :], ALU.mult, c_)
                    yield REST
                    for hf in range(2):
                        r = 2 * g + hf
                        s2 = slice(T * hf, T * hf + T)
                        for o in range(3):
                            i, ps, fr = banks.get()
                            m = mm(ps[:, 0:T], WoA[:, o * 128:(o + 1) * 128], v[:, 0, s2], True, False, a, fr, w)
                            m = mm(ps[:, 0:T], WoC[64:128, o * 128:(o + 1) * 128], v[64:128, 1, s2], False, True, c_)
                            y = tt(xt[:, o, rows(r)], xt[:, o, rows(r)], ps[:, 0:T], ALU.add, m)
                            banks.put(i, y)
                            res.append(y)
                            yield 2 * MM
                            bt = p.op("dve", lambda e, o=o, r=r: e.bn_stats(sm[1]["bn"][:, o, r, :], xt[:, o, rows(r)]), y)
                    cv_free[g % 2] = m
                    out_t[g] = m
                    mixed_t[b] = bt

            cv_free, timg_free, mixed_t, bn3_free = [fe, fe], [None], {}, [fe]
            xT_free, gated = [fe] * NQ, []

            heads = {}

            def sparse_head(b):
                xt, S = x[(b - images) % 2], sm[1]
                cs = channel_stats(S["bn"], S["mv"], S["gs"], mixed_t[b], sc_free[1])
                for _ in range(HEAD_GAP):
                    yield 0
                i, ps, fr = banks.get()
                g, f = group_stats(S["mv"], S["gs"], ps, fr, cs, S["sc"])
                banks.put(i, g)
                for _ in range(HEAD_GAP):
                    yield 0
                ahead = {0: normalize(xt, 0, S["sc"], f)}
                for _ in range(HEAD_GAP):
                    yield 0
                hl = {}

                def pixels(r):
                    ni, n, t = ahead.pop(r) if r in ahead else normalize(xt, r, S["sc"], f)
                    for j in range(3):
                        i, ps, fr = banks.get()
                        for c in range(CT):
                            a = tr(ps[:, c * 128:(c + 1) * 128], n[:, c, j * 128:(j + 1) * 128], t, fr, t_const)
                        h = copy("act", xTh[:, 3 * r + j, :], ps[:, 0:C], a, xT_free[r])
                        l_ = tt(xTl[:, 3 * r + j, :], ps[:, 0:C], xTh[:, 3 * r + j, :].bitcast(F32), ALU.subtract, h)
                        banks.put(i, l_)
                        hl[r, j] = [h, l_]
                        yield MM / 2
                    xn.put(ni, a)
                    sc_free[1] = t

                yield from pixels(0)
                yield from pixels(1)
                heads[b] = (hl, pixels, ahead, lambda r: normalize(xt, r, S["sc"], f))

            def sparse(b):
                xt, S = x[(b - images) % 2], sm[1]
                hl, pixels, ahead, norm = heads[b]
                st_w, up = [], 2
                for r, (b0, b1) in enumerate(BANDS):
                    px, h = slice(W * b0, W * b1), b1 - b0
                    near = [(q, max(b0, 8 * q - 5), min(b1, 8 * q + 13)) for q in range(NQ)]
                    near = [v for v in near if v[1] < v[2]]
                    while up <= near[-1][0]:
                        yield from pixels(up)
                        up += 1
                    for c in range(CT):
                        if c == 1 and up < NQ:
                            ahead[up] = norm(up)
                        for e0 in (0, 24):
                            use = []
                            for q, y0, y1 in near:
                                for j in range(3):
                                    x0, x1 = max(e0, 16 * j - 6), min(e0 + 24, 16 * j + 22)
                                    if x0 < x1:
                                        use.append((q, j, y0, y1, x0, x1, y0 - 8 * q + 5, x0 - 16 * j + 6))
                            xb = xt[:, c, px].rearrange("p (h w) -> p h w", w=W)[:, :, e0:e0 + 24]
                            prev = None
                            for n in (0, 2):
                                i, ps, fr = banks.get()
                                po = ps[:, 0:48 * h].rearrange("p (n h w) -> p n h w", n=2, w=24)
                                k = 0
                                for q, j, y0, y1, x0, x1, u, v in use:
                                    for A, B in ((xTh, Th), (xTl, Th), (xTh, Tl)):
                                        a = mm(po[:, :, y0 - b0:y1 - b0, x0 - e0:x1 - e0], A[:, 3 * q + j, c * 128:(c + 1) * 128],
                                               B[:, n:n + 2, u:u + y1 - y0, v:v + x1 - x0], k == 0, k == 3 * len(use) - 1, hl[q, j], fr, t_T, w2, skip=True)
                                        k += 1
                                    yield 3 * max(256, 2 * (y1 - y0) * (x1 - x0)) / 2400
                                for m in range(2):
                                    prev = stt(xb, po[:, m], wn[:, c, n + m:n + m + 1], xb, ALU.mult, ALU.add, a, prev)
                                banks.put(i, prev)
                        bt = p.op("dve", lambda e, c=c, r=r, px=px: e.bn_stats(bn3[:, c, r, :], xt[:, c, px]), prev, bn3_free)
                    for q, _, _ in near:
                        xT_free[q] = a
                    st_w.append(p.dma(f"x3o{(b - images) % 2}{r}", xo[b, :, :, px], xt[:, :, px], prev))
                stored[("x3", b)] = st_w
                tails[b] = tail(b, bt, st_w)

            tails = {}

            def tail(b, bt, st_w):
                xt = x[(b - images) % 2]
                cs = channel_stats(bn3, mv3, gs3, bt, fe)
                for _ in range(HEAD_GAP):
                    yield 0
                i, ps, fr = banks.get()
                g, f = group_stats(mv3, gs3, ps, fr, cs, gst[:, b])
                banks.put(i, g)
                bn3_free[:] = [g]
                for _ in range(HEAD_GAP):
                    yield 0
                i, ps, fr = banks.get()
                gt_ = []
                for kk in range(CT):
                    gt_.append(ts(gws[:, kk, :], gw[:, kk, :], gst[:, b, 0, kk:kk + 1], None, ALU.mult, None, f, gated, w2))
                    a = mm(ps[0:4, 0:1], gw[:, kk, :], gst[:, b, 1, kk:kk + 1], kk == 0, kk == 2, f, fr)
                gs_ = tt(gbs[:], ps[0:4, 0:1], gb[:], ALU.add, a, gated, w2)
                banks.put(i, gs_)
                yield 0
                io, out, fo = banks.get()
                next_ld = []
                for r in range(NQ):
                    i, ps, fr = banks.get()
                    for kk in range(CT):
                        a = mm(ps[0:4, 0:T], gws[:, kk, :], xt[:, kk, rows(r)], kk == 0, kk == 2, gt_, fr)
                        yield MM
                    if b + 2 < images:
                        next_ld.append(load(b + 2, r, st_w, a))
                    j, lt, lf = lg.get()
                    c_ = act(lt[:], ps[0:4, 0:T], ACT.Identity, a, lf, gs_, fe, bias=gbs[:, 0:1])
                    banks.put(i, c_)
                    yield 0
                    yield 0
                    for tb in range(TB):
                        n = 4 * (TB * r + tb)
                        a = tr(out[:, n:n + 4], lt[:, tb * 128:(tb + 1) * 128], c_, fo)
                    lg.put(j, a)
                gd = copy("dve", coef[:, b * NT:(b + 1) * NT, :], out[:, 0:4 * NT].rearrange("p (j e) -> p j e", e=4), a, fe)
                banks.put(io, gd)
                gated.append(gd)
                if next_ld:
                    ld[b + 2] = next_ld

            def step_conv(k):
                for _ in range(k):
                    while conv_q and next(conv_q[0], 1) == 1:
                        conv_q.pop(0)

            def drain_mix(m):
                for _ in m:
                    step_conv(2)

            done_tail = set()
            m = mix(0)
            if under_way is not None:
                end, pp = under_way
                while next(end, None) is not None:
                    next(m)
                    step_conv(2)
                banks.bufs += pp.bufs
                banks.free += pp.free[0:2]
                banks.held += pp.held
                xT_free[:] = [fence()] * NQ
            mt = matrices()
            for n, _ in enumerate(m):
                step_conv(2)
                if n > 12:
                    next(mt, None)
            for _ in mt:
                pass
            for _ in sparse_head(0):
                pass
            for b in range(images):
                m = mix(b + 1) if b + 1 < images else None
                head = None
                sp, mp, cc = 0.0, 0.0, 0.0
                w3 = None
                for c in sparse(b):
                    if w3 is None and b == images - 1 and (b == 0 or (b - 1) in done_tail):
                        w3 = weights3()
                    sp += c / S_COST
                    if w3 is not None:
                        next(w3, None)
                    if b > 0 and next(tails[b - 1], None) is None:
                        done_tail.add(b - 1)
                    while m is not None and (b == 0 or (b + 1) in ld) and sp > (M_0 if b else 0) and mp < (sp / M_A * 0.62 if sp < M_A else 0.62 + (sp - M_A) / (M_B - M_A) * 0.38):
                        c = next(m, None)
                        if c is None:
                            m, head = None, sparse_head(b + 1)
                        else:
                            mp += max(c, 0.05) / M_COST
                    if head is not None and sp > HEAD_FROM:
                        next(head, None)
                    cc += CONV_RATE
                    while cc >= 1:
                        step_conv(1)
                        cc -= 1
                if m is not None:
                    drain_mix(m)
                    head = sparse_head(b + 1)
                if head is not None:
                    for _ in head:
                        pass
                if w3 is not None:
                    for _ in w3:
                        pass
            return gated, tails[images - 1], u0, banks

        def layer3(x3_d, out_d, gated, last_gate, at, banks):
            fe = fence()
            if not third:
                for _ in weights3():
                    pass
            W1h, W1l, W2h, W2l = (third[n] for n in ("W1h", "W1l", "W2h", "W2l"))
            w1, w2 = third["w1"], third["w2"]
            ar = Arena(nc, at, "d")
            b1 = ar("b1", [128, 3, 4])
            b2 = ar("b2", [12, C])
            b2r = ar("b2r", [12, C], F32R)
            pick = ar("pick", [12, 514])
            pickr = ar("pickr", [12, 4, 128], F32R)
            er = Arena(nc, third["at"], "e")
            xs = [er("xs0", [128, 3, T]), ar("xs1", [128, 3, T])]
            xn = er("xn", [128, 3, T])
            xh = [er("xh0", [128, 3, T], F32R), ar("xh1", [128, 3, T], F32R)]
            xl = [er("xl0", [128, 3, T], F32R), ar("xl1", [128, 3, T], F32R)]
            hf = Ring([ar(f"hf{i}", [128, T]) for i in range(3 * EARLY)])
            ar = er
            hh = Ring([ar(f"hh{i}", [128, 3, T], F32R) for i in range(2)])
            hl = Ring([ar(f"hl{i}", [128, 3, T], F32R) for i in range(2)])
            xs.append(ar("xs2", [128, 3, T]))
            cT = [ar(f"cT{i}", [12, T], F32R) for i in range(2)]
            cs = ar("cs", [128, NB * NT, 12], F32R)
            mx = ar("mx", [128, NB * NT])
            v1 = ar("v1", [128, NB * NT])
            cum = ar("cum", [128, NB * NT])
            eq = ar("eq", [128, NB * NT])
            wk = ar("wk", [128, 2, NB * NT])
            fk = ar("fk", [128, 2, 4, NB * NT])
            fl = ar("fl", [128, 8])
            fb = ar("fb", [128, 8])
            xv = x3_d.rearrange("b (c p) l -> b p c l", p=128)
            ov = out_d.rearrange("b (c p) l -> b p c l", p=128)
            lb = [p.dma("b1", b1[:], d["b1"], fe), p.dma("b2", b2[:], d["b2"], fe), p.dma("pick", pick[:], d["pick"], fe)]
            xs_free, xh_free, cT_free, xn_free = [w2, fe, fe], [w2, fe], [fe] * 2, w2
            nk = images * NQ
            pre_t = {}

            def pre(k):
                b, q = divmod(k, NQ)
                o = k % 2
                nonlocal xn_free
                ld = p.dma(f"x3i{k % 3}", xs[k % 3][:], xv[b, :, :, q * T:(q + 1) * T], xs_free[k % 3], stored.get(("x3", b), []), eng="act" if k == 0 else "sp")
                for c in range(CT):
                    n = ts(xn[:, c, :], xs[k % 3][:, c, :], gst[:, b, 0, c:c + 1], gst[:, b, 1, c:c + 1], ALU.mult, ALU.add, ld, xn_free)
                s = split(xh[o][:], xl[o][:], xn[:], n, xh_free[o])
                xn_free = list(s)
                pre_t[k] = (list(s), ld)

            cT_t = {}

            def by_expert(k):
                o = k % 2
                i, ps, fr = banks.get()
                for tb in range(TB):
                    a = tr(ps[0:12, tb * 128:(tb + 1) * 128], cs[:, k * TB + tb, :].bitcast(F32), tc_, fr)
                cT_t[k] = copy("act", cT[o][:], ps[0:12, 0:T], a, cT_free[o])
                banks.put(i, cT_t[k])

            def hidden(k, e, beside=None):
                o = k % 2
                s = pre_t[k][0]
                out = []
                for m in range(3):
                    i, ps, fr = banks.get()
                    q = [(kk, A, B) for kk in range(CT) for A, B in ((W1h, xh[o]), (W1l, xh[o]), (W1h, xl[o]))]
                    for u, (kk, A, B) in enumerate(q):
                        a = mm(ps[:, 0:T], A[:, kk, e * C + m * 128:e * C + (m + 1) * 128], B[:, kk, :], u == 0, u == len(q) - 1, s, fr, w1)
                        if beside is not None and u % 3 == 2:
                            next(beside, None)
                    j, f, ff = hf.get()
                    r = act(f[:], ps[:, 0:T], ACT.Relu, a, ff, lb, fe, bias=b1[:, m, e:e + 1])
                    banks.put(i, r)
                    out.append((j, f, r))
                xh_free[o] = a
                return out

            def weigh(k, e):
                i, ps, fr = banks.get()
                return i, ps, mm(ps[:, 0:T], pickr[:, e, :], cT[k % 2][:], True, True, cT_t[k], t_b2, fr)

            def scale(hid, wt):
                ih, H, fh = hh.get()
                il, Lw, fl_ = hl.get()
                bi, ps, w = wt
                done = []
                gs_ = [tt(f[:], f[:], ps[:, 0:T], ALU.mult, r, w) for j, f, r in hid]
                for m, ((j, f, r), g) in enumerate(zip(hid, gs_)):
                    c1 = copy("act", H[:, m, :], f[:], g, fh, fe)
                    c2 = tt(Lw[:, m, :], f[:], H[:, m, :].bitcast(F32), ALU.subtract, c1, fl_, fe)
                    hf.put(j, c2)
                    done.append([c1, c2])
                banks.put(bi, g)
                return ih, H, il, Lw, done

            outs = {}

            def combine(k, e, hd):
                o = k % 2
                ih, H, il, Lw, done = hd
                for c in range(CT):
                    if e == 0:
                        outs[c] = banks.get()
                        mm(outs[c][1][:, 0:T], b2r[:, c * 128:(c + 1) * 128], cT[o][:], True, False, cT_t[k], t_b2, outs[c][2], skip=True)
                    ps = outs[c][1]
                    q = [(m, A, B) for m in range(3) for A, B in ((W2h, H), (W2l, H), (W2h, Lw))]
                    for u, (m, A, B) in enumerate(q):
                        a = mm(ps[:, 0:T], A[:, m, e * C + c * 128:e * C + (c + 1) * 128], B[:, m, :], False,
                               e == 3 and u == len(q) - 1, done[m], w2, skip=True)
                    if e == 3:
                        y = tt(xs[k % 3][:, c, :], xs[k % 3][:, c, :], ps[:, 0:T], ALU.add, a)
                        banks.put(outs[c][0], y)
                hh.put(ih, a)
                hl.put(il, a)
                if e == 3:
                    b, q = divmod(k, NQ)
                    cT_free[o] = a
                    w = p.dma(f"oo{k % 3}", ov[b, :, :, q * T:(q + 1) * T], xs[k % 3][:], y)
                    xs_free[k % 3] = w
                    stored[("out", k)] = [w]

            next(last_gate)
            pre(0)
            queue = [(k, e) for k in range(nk) for e in range(4)]
            early = [hidden(0, e, last_gate) for e in range(EARLY)]
            c1 = copy("act", pickr[:].rearrange("p e n -> p (e n)"), pick[:, 0:512], lb)
            c2 = copy("act", b2r[:], b2[:], lb)
            z = tt(b2[:], b2[:], b2r[:].bitcast(F32), ALU.subtract, c2)
            z = ts(b2[:], b2[:], pick[:, 513:514], None, ALU.mult, None, z)
            z = stt(b2r[:], b2r[:].bitcast(F32), pick[:, 512:513], b2[:], ALU.mult, ALU.add, z)
            t_b2 = [c1, z]
            for _ in last_gate:
                pass
            fe = fence()
            xs_free[2], cT_free = fe, [fe] * 2
            M = images * NT
            sc = lambda e: coef[:, 0:M, e]
            X = lambda t: t[:, 0:M]
            t = tt(X(mx), sc(0), sc(1), ALU.max, gated, fe)
            t = tt(X(mx), X(mx), sc(2), ALU.max, t)
            t = tt(X(mx), X(mx), sc(3), ALU.max, t)
            a = [tt(sc(e), sc(e), X(mx), ALU.subtract, t) for e in range(4)]
            a = act(coef[:, 0:M, :], coef[:, 0:M, :], ACT.Exp, a)
            t = tt(X(v1), sc(0), sc(1), ALU.add, a)
            t = tt(X(v1), X(v1), sc(2), ALU.add, t)
            t = tt(X(v1), X(v1), sc(3), ALU.add, t)
            t = p.op("dve", lambda e: e.reciprocal(X(v1), X(v1)), t)
            a = [tt(sc(e), sc(e), X(v1), ALU.mult, t) for e in range(4)]
            for k in range(2):
                top = wk[:, k, 0:M]
                t = tt(top, sc(0), sc(1), ALU.max, a)
                t = tt(top, top, sc(2), ALU.max, t)
                t = tt(top, top, sc(3), ALU.max, t)
                z = None
                for e in range(4):
                    f = fk[:, k, e, 0:M]
                    q = tt(X(eq), sc(e), top, ALU.is_equal, t, z)
                    if e == 0:
                        z = copy("dve", f, X(eq), q)
                        z = copy("dve", X(cum), X(eq), z)
                    else:
                        z = tt(f, X(eq), X(cum), ALU.is_gt, q)
                        z = tt(X(cum), X(cum), X(eq), ALU.max, z)
                if k == 0:
                    a = [stt(sc(e), fk[:, k, e, 0:M], -2.0, sc(e), ALU.mult, ALU.add, z) for e in range(4)]
                z = p.op("dve", lambda e, k=k: e.tensor_reduce(fl[:, 4 * k:4 * k + 4], fk[:, k, :, 0:M], mybir.AxisListType.X, ALU.max), z)
            t = tt(X(eq), wk[:, 1, 0:M], wk[:, 0, 0:M], ALU.subtract, z)
            t = act(X(eq), X(eq), ACT.Exp, t)
            t = ts(X(cum), X(eq), 1.0, None, ALU.add, None, t)
            r0 = p.op("dve", lambda e: e.reciprocal(wk[:, 0, 0:M], X(cum)), t)
            r1 = tt(wk[:, 1, 0:M], X(eq), wk[:, 0, 0:M], ALU.mult, r0)
            i, ps, fr = banks.get()
            m = mm(ps[:, 0:8], ones[:], fl[:], True, True, z, fr)
            g = ts(fb[:], ps[:, 0:8], 0.0, None, ALU.is_gt, None, m, fe)
            banks.put(i, g)
            tc_ = []
            for e in range(4):
                q = ts(sc(e), wk[:, 0, 0:M], fb[:, e:e + 1], None, ALU.mult, None, g, r1)
                tc_.append(stt(sc(e), wk[:, 1, 0:M], fb[:, 4 + e:5 + e], sc(e), ALU.mult, ALU.add, q))
            z = copy("act", cs[:, 0:M, 0:4], coef[:, 0:M, :], tc_)
            z1 = tt(cs[:, 0:M, 4:8], coef[:, 0:M, :], cs[:, 0:M, 0:4].bitcast(F32), ALU.subtract, z)
            z2 = copy("act", cs[:, 0:M, 8:12], coef[:, 0:M, :], tc_)
            tc_ = [z, z1, z2]

            by_expert(0)
            hd = scale(early[0], weigh(0, 0))
            for n, (k, e) in enumerate(queue):
                nxt = None
                if n + 1 < len(queue):
                    if e == 2 and k + 1 < nk:
                        pre(k + 1)
                        by_expert(k + 1)
                    wt = weigh(*queue[n + 1])
                    nxt = scale(early[n + 1] if n < EARLY - 1 else hidden(*queue[n + 1]), wt)
                combine(k, e, hd)
                hd = nxt

        under_way = None
        if 0 in layers:
            under_way = layer0(d["x"], d["x1"])
        gated = []
        if 1 in layers:
            gated, last_gate, at, banks = layer12(d["x1"], d["x3"], under_way)
        if 3 in layers:
            layer3(d["x3"], d["out"], gated, last_gate, at, banks)
        p.op("sp", lambda e: e.nop(), *[t for v in stored.values() for t in v])
        block = ctx.enter_context(nc.Block())
        p.emit(block)


def constants():
    a = {}
    dofs = []
    for ky in range(8):
        for kx in range(5):
            if kx in (0, 4):
                if ky in (0, 4):
                    dofs.append((ky, kx, 0, 1.0))
                elif ky < 4:
                    dofs += [(ky, kx, 0, 2.0), (ky, kx, 1, 2.0)]
            else:
                dofs += [(ky, kx, 0, 2.0), (ky, kx, 1, 2.0)]
    assert len(dofs) == 64
    yy, xx = np.meshgrid(np.arange(8), np.arange(8), indexing="ij")
    fwd, inv, sel = np.zeros((128, 128)), np.zeros((128, 128)), np.zeros((40, 128))
    for i, (ky, kx, odd, m) in enumerate(dofs):
        ang = 2 * np.pi * ((ky * yy + kx * xx) % 8) / 8
        v = np.sin(ang) if odd else np.cos(ang)
        for h in range(2):
            tok = (yy * 16 + 8 * h + xx).ravel()
            fwd[tok, 64 * h + i] = v.ravel()
            inv[64 * h + i, tok] = m / 64 * v.ravel()
            if kx in (0, 4):
                sel[ky * 5 + kx, 64 * h + i] += 0.5
                sel[(-ky) % 8 * 5 + kx, 64 * h + i] += 0.5
            else:
                sel[ky * 5 + kx, 64 * h + i] = 1.0
    a["Fwd"], a["Inv"], a["S40"] = (v.astype(np.float32) for v in (fwd, inv, sel))
    lin = np.linspace(-1.0, 1.0, K11, dtype=np.float32)
    i = np.arange(128)[:, None, None]
    dy = np.arange(18)[None, :, None] - 5 - i // 16
    dx = np.arange(28)[None, None, :] - 6 - i % 16
    ok = (abs(dy) <= 5) & (abs(dx) <= 5)
    G0 = np.where(ok, lin[np.clip(5 - dx, 0, 10)], 0)
    G1 = np.where(ok, lin[np.clip(5 + dy, 0, 10)], 0)
    for n, v in (("G0", G0), ("G1", G1), ("GM", ok)):
        a[n] = np.ascontiguousarray(v.astype(np.float32).reshape(128, 504))
    return a


def lay(inputs):
    f = {k: np.asarray(v) for k, v in inputs.items()}
    a = {}
    a["x"] = np.ascontiguousarray(f["x"].reshape(NB, C, L))
    a["WinT"] = np.ascontiguousarray(f["L0_conv_in_proj_w"].T)
    wx = f["L0_conv_x_proj_w"].T
    pad = np.zeros((DI, 32 - RK), np.float32)
    a["WxT"] = np.concatenate([wx[:, :RK], pad, wx[:, RK:], wx[:, :RK], pad, wx[:, :RK], pad], axis=1)
    wd = np.concatenate([f["L0_conv_dt_proj_w"], pad], axis=1).T
    a["Wdt3"] = np.concatenate([wd, np.zeros_like(wd), wd, wd], axis=0)
    a["WoT"] = np.ascontiguousarray(f["L0_conv_out_proj_w"].T)
    pv = np.concatenate([f["L0_conv_conv_w"], f["L0_conv_conv_b"][:, None], f["L0_conv_dt_proj_b"][:, None],
                         f["L0_conv_D"][:, None], f["L0_conv_A_log"]], axis=1)
    a["pv"] = np.ascontiguousarray(pv.reshape(6, 128, 23).transpose(1, 0, 2))
    pc = np.stack([f["L0_conv_ln_gamma"], f["L0_conv_ln_beta"]], axis=1)
    a["pc"] = np.ascontiguousarray(pc.reshape(3, 128, 2).transpose(1, 0, 2))
    ch = np.arange(C) // 12
    g = (ch[:, None] == ch[None, :]).astype(np.float32).reshape(3, 128, 3, 128)
    a["gm"] = np.ascontiguousarray(g.transpose(1, 0, 2, 3).reshape(128, 9, 128))
    a.update(constants())
    order = np.concatenate([np.arange(0, 128), np.arange(192, 320), np.arange(128, 192), np.arange(320, 384)])
    a["Win1T"] = np.ascontiguousarray(f["L1_conv_w_in"][order].T)
    a["f40"] = np.ascontiguousarray(f["L1_conv_fft_filter"].reshape(C, 40)[order].T)
    a["Wo1T"] = np.ascontiguousarray(f["L1_conv_w_out"].T)
    a["dw"] = np.ascontiguousarray(f["L1_conv_w_dw"].reshape(C, 9)[order].reshape(3, 128, 9).transpose(1, 0, 2))
    a["wn"] = np.ascontiguousarray(f["L2_conv_weights"][0].reshape(3, 128, 4).transpose(1, 0, 2))
    a["row"] = np.concatenate([f["L2_conv_weight_coord"].reshape(8), f["L2_conv_radius"].reshape(4)])[None, :]
    a["gw"] = np.ascontiguousarray(f["L3_conv_gate_w"])
    a["gb"] = np.ascontiguousarray(f["L3_conv_gate_b"][:, None])
    a["W1T"] = np.ascontiguousarray(f["L3_conv_w1"].transpose(2, 0, 1).reshape(C, 4 * C))
    a["W2T"] = np.ascontiguousarray(f["L3_conv_w2"].transpose(2, 0, 1).reshape(C, 4 * C))
    a["b1"] = np.ascontiguousarray(f["L3_conv_b1"].reshape(4, 3, 128).transpose(2, 1, 0))
    a["b2"] = np.concatenate([f["L3_conv_b2"]] * 3)
    pick = np.zeros((12, 514), np.float32)
    for e in range(4):
        pick[[e, 4 + e], e * 128:(e + 1) * 128] = 1
    pick[0:8, 512] = 1
    pick[8:12, 513] = 1
    a["pick"] = pick
    a["ident"] = np.eye(128, dtype=np.float32)
    return a


def kernel(**inputs):
    import concourse.bacc as bacc
    from concourse.bass_utils import run_bass_kernel_spmd

    nc = bacc.Bacc("TRN2", target_bir_lowering=False, num_devices=1, dynamic_dma_scratch_size=1024)
    arrays = lay(inputs)
    d = {n: nc.dram_tensor(f"in_{n}", a.shape, F32, kind="ExternalInput").ap() for n, a in arrays.items()}
    d["out"] = nc.dram_tensor("out", [NB, C, L], F32, kind="ExternalOutput").ap()
    for n in ("x1", "x3"):
        d[n] = nc.dram_tensor(n, [NB, C, L], F32).ap()
    build(nc, d)
    r = run_bass_kernel_spmd(nc, [{f"in_{n}": a for n, a in arrays.items()}], core_ids=[0])
    return r.results[0]["out"].reshape(NB, C, H, W)
```
